# Optimizing a Trainium2 kernel written in Bass

```python
import numpy as np
import jax
import jax.numpy as jnp

def _softmax(x, axis=-1):
    return jax.nn.softmax(x, axis=axis)

def _gelu(x):
    return jax.nn.gelu(x, approximate=True)

def _silu(x):
    return jax.nn.silu(x)

def _sigmoid(x):
    return jax.nn.sigmoid(x)

def _layernorm(x, axis=-1, eps=1e-05):
    m = jnp.mean(x, axis=axis, keepdims=True)
    v = jnp.var(x, axis=axis, keepdims=True)
    return (x - m) / jnp.sqrt(v + eps)

def _scatter_add(tgt, idx, src, axis=0):
    return tgt.at[idx].add(src)

def _segment_sum(src, seg, n):
    return jax.ops.segment_sum(src, seg, n)
kernel_name = 'mk_xattn_ffn_d2_seqx_r4_c7b9ee'

def setup_inputs(seed: int=0):
    np.random.seed(seed)
    _w = jnp.asarray

    def _rec_inputs():
        import jax
        import jax.numpy as jnp
        _rk = jax.random.key(seed)
        x = 0.0003765 + 1 * jax.random.normal(jax.random.fold_in(_rk, 1), (8, 256, 512), jnp.float32)
        _lenS = 256 - jax.random.randint(jax.random.fold_in(_rk, 7), (8,), 0, max(1, 256 // 4) + 1, jnp.int32)
        _lenS2 = 256 - jax.random.randint(jax.random.fold_in(_rk, 8), (8,), 0, max(1, 256 // 4) + 1, jnp.int32)
        _ctx_2048P = jax.random.normal(jax.random.fold_in(_rk, 11), (8, 16, 512), jnp.float32)
        _ctx_2048c = jax.random.dirichlet(jax.random.fold_in(_rk, 511), 0.3 * jnp.ones((16,), jnp.float32), (8, 256))
        _ctx_2048t = jnp.einsum('bsk,bkd->bsd', _ctx_2048c, _ctx_2048P)
        _ctx_2048t = _ctx_2048t * jax.lax.rsqrt(jnp.mean(jnp.square(_ctx_2048t)) + 1e-12) * 0.953939
        ctx_2048 = -0.000292821 + 1.00034 * (_ctx_2048t + 0.3 * jax.random.normal(jax.random.fold_in(_rk, 611), (8, 256, 512), jnp.float32))
        return (x, ctx_2048)
    x, ctx_2048 = _rec_inputs()

    def _L0_xattn_setup():
        import jax, jax.numpy as jnp
        import numpy as np
        key = jax.random.key(seed)
        k1, k2, k3, k4, k5 = jax.random.split(key, 5)
        B, D_MODEL, L = (2, 256, 512)
        HEAD_DIM = 8
        H = D_MODEL // HEAD_DIM
        return {'k': jax.random.normal(k1, (B, D_MODEL, L), dtype=jnp.float32), 'v': jax.random.normal(k2, (B, D_MODEL, L), dtype=jnp.float32), 'q': jax.random.normal(k3, (B, D_MODEL, L), dtype=jnp.float32), 'ssm_kernel': jax.random.normal(k4, (H, L), dtype=jnp.float32), 'D': jax.random.normal(k5, (H,), dtype=jnp.float32), 'head_dim': HEAD_DIM}
    _L0_xattn_all = _L0_xattn_setup()
    _L0_xattn_in = {k: v for k, v in _L0_xattn_all.items() if k in ('ssm_kernel', 'D')}
    del _L0_xattn_all

    def _L0_ffn_setup():
        import jax, jax.numpy as jnp
        import numpy as np
        NUM_EXPERTS = 16
        C = 1.0
        key = jax.random.key(seed)
        k1, k2, k3 = jax.random.split(key, 3)
        b, s, h = (4, 512, 512)
        return {'x': jax.random.normal(k1, (b, s, h), dtype=jnp.float32), 'router_w': jax.random.normal(k2, (h, NUM_EXPERTS), dtype=jnp.float32) * 0.02, 'router_b': jnp.zeros((NUM_EXPERTS,), dtype=jnp.float32), 'expert_w': jax.random.normal(k3, (h, h), dtype=jnp.float32) * 0.02, 'expert_b': jnp.zeros((h,), dtype=jnp.float32)}
    _L0_ffn_all = _L0_ffn_setup()
    _L0_ffn_in = {k: v for k, v in _L0_ffn_all.items() if k in ('router_w', 'router_b', 'expert_w', 'expert_b')}
    del _L0_ffn_all

    def _L1_xattn_setup():
        import jax, jax.numpy as jnp
        import numpy as np
        B, S, DIM, HD = (4, 256, 512, 128)
        H = DIM // HD
        GN_EPS = 0.001

        def _decay_masks(n_heads, seq_len):
            gam = 1.0 - 2.0 ** (-5.0 - jnp.arange(n_heads, dtype=jnp.float32))
            idx = jnp.arange(seq_len, dtype=jnp.float32)
            expo = idx[None, :] - idx[:, None]
            D = jnp.where(expo[None, :, :] <= 0, gam[:, None, None] ** expo[None, :, :], 0.0)
            return D / jnp.sqrt(D.sum(axis=-1))[:, None, :]
        key = jax.random.key(seed)
        ks = jax.random.split(key, 8)
        x = jax.random.normal(ks[0], (B, S, DIM), dtype=jnp.float32)
        k = jax.random.normal(ks[1], (B, S, DIM), dtype=jnp.float32)
        v = jax.random.normal(ks[2], (B, S, DIM), dtype=jnp.float32)
        Wh = jax.random.normal(ks[3], (H, HD, HD), dtype=jnp.float32) / np.sqrt(HD)
        wg_w = jax.random.normal(ks[4], (DIM, DIM), dtype=jnp.float32) / np.sqrt(DIM)
        wo_w = jax.random.normal(ks[5], (DIM, DIM), dtype=jnp.float32) / np.sqrt(DIM)
        gn_gamma = jnp.ones((DIM,), dtype=jnp.float32)
        gn_beta = jnp.zeros((DIM,), dtype=jnp.float32)
        return {'x': x, 'k': k, 'v': v, 'Wh': Wh, 'wg_w': wg_w, 'wo_w': wo_w, 'gn_gamma': gn_gamma, 'gn_beta': gn_beta}
    _L1_xattn_all = _L1_xattn_setup()
    _L1_xattn_in = {k: v for k, v in _L1_xattn_all.items() if k in ('Wh', 'wg_w', 'wo_w', 'gn_gamma', 'gn_beta')}
    del _L1_xattn_all

    def _L1_ffn_setup():
        import jax, jax.numpy as jnp
        import numpy as np
        B, S, D = (4, 512, 512)
        DFF = 1408
        E, K, R = (8, 2, 16)
        SCALING = 32.0 / 16.0
        key = jax.random.key(seed)
        ks = jax.random.split(key, 12)
        s = lambda k, shape, scale: jax.random.normal(k, shape, dtype=jnp.float32) * scale
        return {'x': s(ks[0], (B, S, D), 1.0), 'Wg': s(ks[1], (DFF, D), 0.02), 'Wu': s(ks[2], (DFF, D), 0.02), 'Wd': s(ks[3], (D, DFF), 0.02), 'Wr': s(ks[4], (E, D), 0.02), 'Ag': s(ks[5], (E, R, D), 0.02), 'Bg': s(ks[6], (E, DFF, R), 0.02), 'Au': s(ks[7], (E, R, D), 0.02), 'Bu': s(ks[8], (E, DFF, R), 0.02), 'Ad': s(ks[9], (E, R, DFF), 0.02), 'Bd': s(ks[10], (E, D, R), 0.02)}
    _L1_ffn_all = _L1_ffn_setup()
    _L1_ffn_in = {k: v for k, v in _L1_ffn_all.items() if k in ('Wg', 'Wu', 'Wd', 'Wr', 'Ag', 'Bg', 'Au', 'Bu', 'Ad', 'Bd')}
    del _L1_ffn_all
    return {'x': x, 'ctx_2048': ctx_2048, 'L0_xattn_ssm_kernel': _L0_xattn_in['ssm_kernel'], 'L0_xattn_D': _L0_xattn_in['D'], 'L0_ffn_router_w': _L0_ffn_in['router_w'], 'L0_ffn_router_b': _L0_ffn_in['router_b'], 'L0_ffn_expert_w': _L0_ffn_in['expert_w'], 'L0_ffn_expert_b': _L0_ffn_in['expert_b'], 'L1_xattn_Wh': _L1_xattn_in['Wh'], 'L1_xattn_wg_w': _L1_xattn_in['wg_w'], 'L1_xattn_wo_w': _L1_xattn_in['wo_w'], 'L1_xattn_gn_gamma': _L1_xattn_in['gn_gamma'], 'L1_xattn_gn_beta': _L1_xattn_in['gn_beta'], 'L1_ffn_Wg': _L1_ffn_in['Wg'], 'L1_ffn_Wu': _L1_ffn_in['Wu'], 'L1_ffn_Wd': _L1_ffn_in['Wd'], 'L1_ffn_Wr': _L1_ffn_in['Wr'], 'L1_ffn_Ag': _L1_ffn_in['Ag'], 'L1_ffn_Bg': _L1_ffn_in['Bg'], 'L1_ffn_Au': _L1_ffn_in['Au'], 'L1_ffn_Bu': _L1_ffn_in['Bu'], 'L1_ffn_Ad': _L1_ffn_in['Ad'], 'L1_ffn_Bd': _L1_ffn_in['Bd']}

def reference(x, ctx_2048, L0_xattn_ssm_kernel, L0_xattn_D, L0_ffn_router_w, L0_ffn_router_b, L0_ffn_expert_w, L0_ffn_expert_b, L1_xattn_Wh, L1_xattn_wg_w, L1_xattn_wo_w, L1_xattn_gn_gamma, L1_xattn_gn_beta, L1_ffn_Wg, L1_ffn_Wu, L1_ffn_Wd, L1_ffn_Wr, L1_ffn_Ag, L1_ffn_Bg, L1_ffn_Au, L1_ffn_Bu, L1_ffn_Ad, L1_ffn_Bd):
    import jax
    import jax.numpy as jnp

    def _L0_xattn_ref(k, v, q, ssm_kernel, D, head_dim):
        import jax, jax.numpy as jnp
        import numpy as np
        B, HD, L = k.shape
        H = HD // head_dim
        fft_size = 2 * L
        k_ = k.reshape(B, H, head_dim, L)
        v_ = v.reshape(B, H, head_dim, L)
        q_ = q.reshape(B, H, head_dim, L)
        kv = jnp.einsum('bhil,bhjl->bijhl', k_, v_)
        kv_f = jnp.fft.rfft(kv, n=fft_size)
        kernel_f = jnp.fft.rfft(ssm_kernel, n=fft_size)
        y = jnp.fft.irfft(kv_f * kernel_f, n=fft_size)[..., :L]
        out = y + kv * D[None, None, None, :, None]
        out = jnp.einsum('bijhl,bhil->bjhl', out, q_)
        out = jnp.transpose(out, (0, 2, 1, 3)).reshape(B, H * head_dim, L)
        return out.astype(k.dtype)

    def _L0_ffn_ref(x, router_w, router_b, expert_w, expert_b):
        import jax, jax.numpy as jnp
        import numpy as np
        NUM_EXPERTS = 16
        C = 1.0
        b, s, h = x.shape
        bs = b * s
        k = min(int(bs * C / NUM_EXPERTS), bs)
        xf = x.reshape(bs, h)
        logits = xf @ router_w + router_b
        S = jax.nn.softmax(logits, axis=-1)
        G, idx = jax.lax.top_k(S.T, k)
        tokens = xf[idx]
        out = jnp.einsum('ekh,hd->ekd', tokens, expert_w) + expert_b
        weighted = G[..., None] * out
        y = jnp.zeros((bs, h), dtype=x.dtype).at[idx.reshape(-1)].add(weighted.reshape(-1, h))
        return y.reshape(b, s, h)

    def _L1_xattn_ref(x, k, v, Wh, wg_w, wo_w, gn_gamma, gn_beta):
        import jax, jax.numpy as jnp
        import numpy as np
        B, S, DIM, HD = (4, 256, 512, 128)
        H = DIM // HD
        GN_EPS = 0.001

        def _decay_masks(n_heads, seq_len):
            gam = 1.0 - 2.0 ** (-5.0 - jnp.arange(n_heads, dtype=jnp.float32))
            idx = jnp.arange(seq_len, dtype=jnp.float32)
            expo = idx[None, :] - idx[:, None]
            D = jnp.where(expo[None, :, :] <= 0, gam[:, None, None] ** expo[None, :, :], 0.0)
            return D / jnp.sqrt(D.sum(axis=-1))[:, None, :]
        b, s, dim = x.shape
        h, hd, _ = Wh.shape
        xh = x.reshape(b, s, h, hd)
        kh = k.reshape(b, s, h, hd)
        vh = v.reshape(b, s, h, hd)
        Q = jnp.einsum('bshd,hde->bshe', xh, Wh)
        K = jnp.einsum('bshd,hde->bshe', kh, Wh)
        V = jnp.einsum('bshd,hde->bshe', vh, Wh)
        scores = jnp.einsum('bshe,bthe->bhst', Q, K) / jnp.sqrt(jnp.float32(hd))
        Dn = _decay_masks(h, s)
        masked = scores * Dn[None, :, :, :]
        A = jnp.maximum(jnp.abs(masked.sum(axis=0)), 1.0)
        O = jnp.einsum('hst,bthe->bshe', A, V).reshape(b, s, dim)
        mu = O.mean(axis=-1, keepdims=True)
        var = O.var(axis=-1, keepdims=True)
        Y = (O - mu) / jnp.sqrt(var + GN_EPS) * gn_gamma + gn_beta
        W = jax.nn.relu(x @ wg_w)
        return W * Y @ wo_w

    def _L1_ffn_ref(x, Wg, Wu, Wd, Wr, Ag, Bg, Au, Bu, Ad, Bd):
        import jax, jax.numpy as jnp
        import numpy as np
        B, S, D = (4, 512, 512)
        DFF = 1408
        E, K, R = (8, 2, 16)
        SCALING = 32.0 / 16.0
        b, s, d = x.shape
        xf = x.reshape(-1, d)
        gate_base = xf @ Wg.T
        up_base = xf @ Wu.T
        base_out = jax.nn.silu(gate_base) * up_base @ Wd.T
        router_logits = xf @ Wr.T
        probs = jax.nn.softmax(router_logits.astype(jnp.float32), axis=-1)
        topw, topi = jax.lax.top_k(probs, K)
        topw = topw.astype(x.dtype)
        expert_w = jnp.sum(jax.nn.one_hot(topi, E, dtype=x.dtype) * topw[..., None], axis=1)

        def expert_step(acc, params):
            Ag_e, Bg_e, Au_e, Bu_e, Ad_e, Bd_e, we = params
            g_lora = xf @ Ag_e.T @ Bg_e.T * SCALING
            u_lora = xf @ Au_e.T @ Bu_e.T * SCALING
            h = jax.nn.silu(gate_base + g_lora) * (up_base + u_lora)
            d_delta = h @ Ad_e.T @ Bd_e.T * SCALING
            return (acc + d_delta * we[:, None], None)
        acc0 = jnp.zeros_like(base_out)
        acc, _ = jax.lax.scan(expert_step, acc0, (Ag, Bg, Au, Bu, Ad, Bd, expert_w.T))
        return (base_out + acc).reshape(b, s, d)
    x = x + _L0_xattn_ref(ctx_2048, ctx_2048, _layernorm(x, axis=-1), L0_xattn_ssm_kernel, L0_xattn_D, 8)
    x = x + _L0_ffn_ref(_layernorm(x, axis=-1), L0_ffn_router_w, L0_ffn_router_b, L0_ffn_expert_w, L0_ffn_expert_b)
    x = x + _L1_xattn_ref(_layernorm(x, axis=-1), ctx_2048, ctx_2048, L1_xattn_Wh, L1_xattn_wg_w, L1_xattn_wo_w, L1_xattn_gn_gamma, L1_xattn_gn_beta)
    x = x + _L1_ffn_ref(_layernorm(x, axis=-1), L1_ffn_Wg, L1_ffn_Wu, L1_ffn_Wd, L1_ffn_Wr, L1_ffn_Ag, L1_ffn_Bg, L1_ffn_Au, L1_ffn_Bu, L1_ffn_Ad, L1_ffn_Bd)
    return x

_drawn_inputs = setup_inputs


def setup_inputs(seed=0):
    import zlib

    import numpy as np

    out = dict(_drawn_inputs(seed))
    spreads = {'L0_ffn_router_b': (0.0, 0.8),
     'L0_ffn_expert_b': (0.0, 0.8),
     'L1_xattn_gn_gamma': (1.0, 0.6),
     'L1_xattn_gn_beta': (0.0, 0.8)}
    factors = {'L0_ffn_router_w': 8.0,
     'L0_ffn_expert_w': 8.0,
     'L1_xattn_Wh': 4.212,
     'L1_xattn_wg_w': 5.111,
     'L1_xattn_wo_w': 4.196,
     'L1_ffn_Wg': 8.0,
     'L1_ffn_Wu': 8.0,
     'L1_ffn_Wd': 8.0,
     'L1_ffn_Wr': 8.0,
     'L1_ffn_Ag': 8.0,
     'L1_ffn_Bg': 8.0,
     'L1_ffn_Au': 8.0,
     'L1_ffn_Bu': 8.0,
     'L1_ffn_Ad': 8.0,
     'L1_ffn_Bd': 8.0}
    for name, (base, spread) in spreads.items():
        noise = np.random.default_rng([zlib.crc32(name.encode()), seed]).standard_normal(out[name].shape)
        drawn = base * np.exp(spread * noise) if base else spread * noise
        out[name] = jnp.asarray(drawn.astype(out[name].dtype))
    for name, factor in factors.items():
        out[name] = (out[name] * factor).astype(out[name].dtype)
    return out
```

```python
from contextlib import ExitStack

import concourse.bass as bass
from concourse import mybir

F32 = mybir.dt.float32
F32R = mybir.dt.float32r
I32 = mybir.dt.int32
ALU = mybir.AluOpType
ACT = mybir.ActivationFunctionType
X_AXIS = mybir.AxisListType.X

P = 128
BATCH, SEQ, DIM = 8, 256, 512
TOKENS = BATCH * SEQ
TILES = TOKENS // P
KB = DIM // P
GROUP = 4
GROUPS = TILES // GROUP
GTOK = GROUP * P
EPS = 1e-5
GN_EPS = 1e-3

HEADS, HD = 32, 8
WRAP = 3
PAIRS = 4 * HD + HD // 2
MB = KB * BATCH

EXPERTS = 16
CAPACITY = TOKENS // EXPERTS
BITS = 30

RHEADS = DIM // P

FE, RANK = 8, 16
DFF = 1408
CHUNKS = DFF // P
SCALING = 2.0
GU_W = 2 * DIM + 2 * P
DN_W = DIM + P


def build(nc, x, ctx_in, strips, d_bc, consts, bits, rw, rb, ew, eb, wh, decay, wg, wo, gb,
          wr, ag, au, bd, chunk_w, out):
    xr = x.rearrange("b (s p) d -> (b s) p d", p=P)
    cr = ctx_in.rearrange("b (s p) d -> (b s) p d", p=P)
    outr = out.rearrange("b (s p) d -> (b s) p d", p=P)

    stack = ExitStack()
    with stack:
        start_of, primed = {}, []

        def sem(name, start=0):
            s = stack.enter_context(nc.semaphore(name))
            if start:
                start_of[s.name] = start
                primed.append((s, start))
            return s

        def sems(name, n, start=0):
            return [sem(f"{name}{i}", start) for i in range(n)]

        def keep(name, shape, dt=F32):
            return stack.enter_context(nc.sbuf_tensor(name, shape, dt))

        banks = stack.enter_context(nc.psum_tensor("banks", [P, 8, 512], F32))

        xres = keep("xres", [P, TILES, DIM])
        cst = keep("cst", [P, 3 * P + 8 + 32])
        ident, same_e, lower_e = (cst[:, i * P:(i + 1) * P] for i in range(3))
        tile_sel = cst[:, 3 * P:3 * P + 8]
        rank8 = cst[:, 3 * P + 8:3 * P + 40]
        mhalf = keep("mhalf", [P, GROUP])
        stat6 = keep("stat6", [P, GROUP, 6])
        mom = keep("mom", [P, GROUP, 2])
        vare = keep("vare", [P, GROUP])
        rstd = keep("rstd", [P, GROUP])
        gate = keep("gate", [P, TILES])
        xn = keep("xn", [P, GROUP, DIM])

        mid = ExitStack()

        def alloc(st, name, shape, dt=F32):
            return st.enter_context(nc.sbuf_tensor(name, shape, dt))

        qt = alloc(mid, "qt", [P, KB * TOKENS])
        ct = alloc(mid, "ct", [P, KB * TOKENS])

        sa = ExitStack()
        cin = alloc(sa, "cin", [P, GROUP, DIM])
        sa.close()
        sc = ExitStack()
        strip = alloc(sc, "strip", [P, 2, DIM])
        dcol = alloc(sc, "dcol", [P, HEADS])
        kx = alloc(sc, "kx", [P, 2, MB * 2 * HD])
        qx = alloc(sc, "qx", [P, 2, MB * 2 * HD])
        kv = alloc(sc, "kv", [P, 2, MB * PAIRS])
        YP_ = 4 * (HD + WRAP) + 4
        yx = alloc(sc, "yx", [P, 2, MB * YP_])
        pr = alloc(sc, "pr", [P, 2, MB * HD * HD])
        sc.close()
        sbk = ExitStack()
        ost = alloc(sbk, "ost", [P, GROUP, DIM])
        xth = alloc(sbk, "xth", [P, GROUP, DIM], F32R)
        xtl = alloc(sbk, "xtl", [P, GROUP, DIM], F32R)
        ewf = alloc(sbk, "ewf", [P, KB, DIM])
        ewh = alloc(sbk, "ewh", [P, KB, DIM], F32R)
        ewl = alloc(sbk, "ewl", [P, KB, DIM], F32R)
        rwf = alloc(sbk, "rwf", [P, KB * EXPERTS])
        rwh = alloc(sbk, "rwh", [P, KB * EXPERTS], F32R)
        rwl = alloc(sbk, "rwl", [P, KB * EXPERTS], F32R)
        rbb = alloc(sbk, "rbb", [P, EXPERTS])
        ebb = alloc(sbk, "ebb", [P, DIM])
        lg = alloc(sbk, "lg", [P, TILES * EXPERTS])
        lsc = alloc(sbk, "lsc", [P, 2 * TILES])
        st_ = alloc(sbk, "st_", [P, 2 * P])
        junk = alloc(sbk, "junk", [P, 2 * P])
        eqs = alloc(sbk, "eqs", [P, 2 * P])
        scan = alloc(sbk, "scan", [P, 2 * P])
        onesr = alloc(sbk, "onesr", [P, P])
        cnt = alloc(sbk, "cnt", [P, 8])
        pre = alloc(sbk, "pre", [P, 4], I32)
        bitc = alloc(sbk, "bitc", [P, BITS], I32)
        sbk.close()
        sd = ExitStack()
        xt = alloc(sd, "xt", [P, KB * TOKENS])
        sd1 = ExitStack()
        dmask = alloc(sd1, "dmask", [P, RHEADS, 2 * SEQ])
        whf = alloc(sd1, "whf", [P, RHEADS, P])
        whs = alloc(sd1, "whs", [P, P])
        wht = alloc(sd1, "wht", [P, P])
        whh = alloc(sd1, "whh", [P, P], F32R)
        whl = alloc(sd1, "whl", [P, P], F32R)
        grh = alloc(sd1, "grh", [P, P], F32R)
        grl = alloc(sd1, "grl", [P, P], F32R)
        cch = alloc(sd1, "cch", [P, 2, GTOK], F32R)
        ccl = alloc(sd1, "ccl", [P, 2, GTOK], F32R)
        xxh = alloc(sd1, "xxh", [P, 2, GTOK], F32R)
        xxl = alloc(sd1, "xxl", [P, 2, GTOK], F32R)
        mth = alloc(sd1, "mth", [P, 2, GTOK], F32R)
        mtl = alloc(sd1, "mtl", [P, 2, GTOK], F32R)
        vh = alloc(sd1, "vh", [P, TILES, P], F32R)
        vl = alloc(sd1, "vl", [P, TILES, P], F32R)
        aw = alloc(sd1, "aw", [P, 2 * SEQ])
        ah = alloc(sd1, "ah", [P, 2 * SEQ], F32R)
        al = alloc(sd1, "al", [P, 2 * SEQ], F32R)
        sd1.close()
        mid2 = ExitStack()
        wgf = alloc(mid2, "wgf", [P, KB, DIM])
        wgh = alloc(mid2, "wgh", [P, KB, DIM], F32R)
        wgl = alloc(mid2, "wgl", [P, KB, DIM], F32R)
        woh = alloc(mid2, "woh", [P, KB, DIM], F32R)
        wol = alloc(mid2, "wol", [P, KB, DIM], F32R)
        gbc = alloc(mid2, "gbc", [P, 2 * KB])
        xeh = alloc(mid2, "xeh", [P, KB, GTOK], F32R)
        xel = alloc(mid2, "xel", [P, KB, GTOK], F32R)
        zt = alloc(mid2, "zt", [P, KB, GTOK])
        mid2.close()
        sd.close()
        mid.close()
        so = ExitStack()
        alloc(so, "over_qt", [P, KB * TOKENS])
        uh = alloc(so, "uh", [P, KB, GTOK], F32R)
        ul = alloc(so, "ul", [P, KB, GTOK], F32R)
        wof = alloc(so, "wof", [P, KB, DIM])
        so.close()
        sf = ExitStack()
        wst = alloc(sf, "wst", [P, 2, GU_W + DN_W])
        guh = alloc(sf, "guh", [P, 2, GU_W], F32R)
        gul = alloc(sf, "gul", [P, 2, GU_W], F32R)
        dnh = alloc(sf, "dnh", [P, 2, DN_W], F32R)
        dnl = alloc(sf, "dnl", [P, 2, DN_W], F32R)
        xfh = alloc(sf, "xfh", [P, KB, GTOK], F32R)
        xfl = alloc(sf, "xfl", [P, KB, GTOK], F32R)
        LW = KB * FE + 2 * DIM + DIM
        lwf = alloc(sf, "lwf", [P, LW])
        lwh = alloc(sf, "lwh", [P, LW], F32R)
        lwl = alloc(sf, "lwl", [P, LW], F32R)
        rt = alloc(sf, "rt", [P, 12, GROUP * FE])
        rsm = alloc(sf, "rsm", [P, 6, GROUP])
        ex = alloc(sf, "ex", [P, 4, GTOK])
        mk = alloc(sf, "mk", [P, 4, GTOK])
        rf = alloc(sf, "rf", [P, 4, GTOK])
        rh = alloc(sf, "rh", [P, 4, GTOK], F32R)
        rl = alloc(sf, "rl", [P, 4, GTOK], F32R)
        silu = alloc(sf, "silu", [P, 2, GTOK])
        hf = alloc(sf, "hf", [P, 3, GTOK])
        hh = alloc(sf, "hh", [P, 2, 3, GTOK], F32R)
        hl = alloc(sf, "hl", [P, 2, 3, GTOK], F32R)
        zf = alloc(sf, "zf", [P, 2, GTOK])
        zh = alloc(sf, "zh", [P, GTOK], F32R)
        zl = alloc(sf, "zl", [P, GTOK], F32R)
        sf.close()

        def f(ap):
            return ap.bitcast(F32)

        def turned(t, tile):
            return t[:, :].rearrange("p (k n) -> p k n", k=KB)[:, :, bass.ts(tile, P)]

        def split(ap):
            return ap.rearrange("p (k n) -> p k n", k=KB)

        def turned_group(t, g):
            return t[:, :].rearrange("p (k n) -> p k n", k=KB)[:, :, bass.ts(g, GTOK)]

        def tile_rows(t, tile):
            return t[:, :].rearrange("p (t n) -> p t n", t=TILES)[:, tile, :]

        def head_cols(t, h):
            return t[:, :].rearrange("p (m c) -> p m c", m=MB)[:, :, bass.ts(h, HD)]

        def view(t, u, offset, dims):
            n = t.shape[2]
            return bass.AP(t[:, :, :].tensor, u * n + offset, [[2 * n, P]] + dims)

        s_const = sem("const_in")
        s_mh = sem("mhalf_set")
        passed = sem("passed")
        ln = {st: {k: sem(f"{st}_{k}", 1 if k == "xn" else 0) for k in ("stats", "var", "rstd", "xn")} for st in "ABCEF"}
        x_in, c_in = sems("x_in", 4, 16), sems("c_in", 4, 16)
        ctx_turned, ct_copied = sem("ctx_turned", GROUP), sem("ct_copied", GROUP)
        xa_turned, qt_copied = sem("xa_turned", GROUP), sem("qt_copied", GROUP)
        d_in = sem("d_in")
        strip_in, strip_ready = sems("strip_in", 2), sems("strip_ready", 2)
        kqx_ready, kv_ready = sems("kqx_ready", 2), sems("kv_ready", 2, 1)
        conv_done, y_copied = sems("conv_done", 2, 1), sems("y_copied", 2, 1)
        pr_vec, pr_pool, conv_out = sems("pr_vec", 2), sems("pr_pool", 2), sems("conv_out", 2, 1)
        wB_in, wB_high, wB_ready = sem("wB_in"), sem("wB_high"), sem("wB_ready")
        ost_ready, o_turned, x1_ready = sem("ost_ready"), sem("o_turned", GROUP), sem("x1_ready")
        xb_turned, xth_ready, xtl_ready = sem("xb_turned", GROUP), sem("xth_ready", GROUP), sem("xtl_ready", GROUP)
        yw_done, yw_copied = sem("yw_done", GROUP), sem("yw_copied", GROUP)
        t_vec, t_exp, t_pe = sem("t_vec"), sem("t_exp"), sem("t_pe")
        bit_vec, bit_cnt, bit_sum = sem("bit_vec", 1), sem("bit_cnt"), sem("bit_sum")
        x2_ready, xc_turned, xt_copied = sem("x2_ready"), sem("xc_turned", GROUP), sem("xt_copied", GROUP)

        wh_in, whs_ready, whl_ready, wh_turned, wht_ready, g_done = (
            sem(n) for n in ("wh_in", "whs_ready", "whl_ready", "wh_turned", "wht_ready", "g_done"))
        grh_ready, grl_ready, cxh_ready, cxl_ready = (sem(n) for n in ("grh_ready", "grl_ready", "cxh_ready", "cxl_ready"))
        m_done = sem("m_done")
        mv_done, sc_done = sems("mv_done", 2, 1), sems("sc_done", 2, 1)
        mth_ready, vh_ready = sem("mth_ready"), sem("vh_ready")
        mtl_ready, vl_ready = sems("mtl_ready", 2, 1), sems("vl_ready", 2, 1)
        ones_set, a_read, a_abs, a_ready, ah_ready = sem("ones_set"), sem("a_read", 1), sem("a_abs"), sem("a_ready"), sem("ah_ready")
        al_ready, ao_done = sem("al_ready", 1), sem("ao_done", 1)
        ro_act, ro_vec = sem("ro_act", 1), sem("ro_vec", 1)
        wE_in, wE_high, wE_ready = sem("wE_in"), sem("wE_high"), sem("wE_ready")
        xeh_ready, xel_ready, wt_done = sem("xeh_ready"), sem("xel_ready"), sem("wt_done", 1)
        y_turned, zt_ready, zu_ready, uh_ready = sem("y_turned", GROUP), sem("zt_ready"), sem("zu_ready", 1), sem("uh_ready")
        ul_ready, wo_done, x3_ready = sem("ul_ready", 1), sem("wo_done", 1), sem("x3_ready", 1)
        lw_in, lwh_ready, lwl_ready = sem("lw_in"), sem("lwh_ready"), sem("lwl_ready")
        wst_in = sems("wst_in", 2)
        xf_turned, xfh_ready, xfl_ready = sem("xf_turned", GROUP), sem("xfh_ready"), sem("xfl_ready")
        lgt_done, ra_done, r_vec, r_exp = sem("lgt_done"), sem("ra_done"), sem("r_vec", 1), sem("r_exp")
        mk_turned, mk_ready, rf_ready, rh_ready, rl_ready = (
            sem(n) for n in ("mk_turned", "mk_ready", "rf_ready", "rh_ready", "rl_ready"))
        guh_ready, gul_ready, dnh_ready, dnl_ready = sem("guh_ready"), sem("gul_ready"), sem("dnh_ready"), sem("dnl_ready", 2)
        gu_ready, silu_done, mul_done, hh_ready = sem("gu_ready", 1), sem("silu_done"), sem("mul_done", 1), sem("hh_ready")
        hl_ready, down_done = sems("hl_ready", 3, 1), sem("down_done", 2)
        z_done, z_vec, zh_ready, zl_ready = sem("z_done"), sem("z_vec", 1), sem("zh_ready"), sem("zl_ready")
        fo_done, xo_ready, out_written = sem("fo_done"), sem("xo_ready", 1), sem("out_written")


        def raised(s):
            return start_of.get(s.name, 0)

        def hold(eng, s, value):
            eng.wait_ge(s, raised(s) + value)
            eng.sem_inc(passed, 1)

        def ln_stats(dve, st, g, src, ready, eps):
            s = ln[st]
            dve.wait_ge(s["xn"], raised(s["xn"]) + GROUP * g)
            dve.sem_inc(passed, 1)
            for j in range(GROUP):
                ready(j)
                i = dve.bn_stats(stat6[:, j, :], src(j))
            i.then_inc(s["stats"], 1)
            dve.wait_ge(s["stats"], 2 * g + 1)
            dve.sem_inc(passed, 1)
            for j in range(GROUP):
                i = dve.bn_aggr(mom[:, j, :], stat6[:, j, :])
            i.then_inc(s["stats"], 1)
            dve.wait_ge(s["stats"], 2 * g + 2)
            dve.tensor_scalar(vare[:, :], mom[:, :, 1], eps, None, ALU.add).then_inc(s["var"], 1)
            dve.wait_ge(s["rstd"], g + 1)

        def ln_apply(dve, st, j, src):
            dve.tensor_scalar(xn[:, j, :], src, mom[:, j, 0:1], rstd[:, j:j + 1],
                              ALU.subtract, ALU.mult).then_inc(ln[st]["xn"], 1)

        def ln_rstd(pool, st):
            with pool.Fori(0, GROUPS, 1) as g:
                pool.wait_ge(ln[st]["var"], g + 1)
                pool.tensor_tensor(rstd[:, :], vare[:, :], mhalf[:, :], ALU.pow).then_inc(ln[st]["rstd"], 1)

        def turn(pe, bank, src, signal):
            for k in range(KB):
                i = pe.transpose(banks[:, bank, k * P:(k + 1) * P], src[:, k * P:(k + 1) * P], ident)
            i.then_inc(signal, 1)

        def product(pe, dst, wh_, wl_, mh_, ml_, first, last, check=False):
            pe.matmul(dst, wh_, mh_, start=first, stop=False, skip_group_check=check)
            pe.matmul(dst, wh_, ml_, start=False, stop=False, skip_group_check=check)
            return pe.matmul(dst, wl_, mh_, start=False, stop=last, skip_group_check=check)

        def skewed(eng, early, late):
            early(0, 0, 0)
            with eng.Fori(0, HEADS // 2 - 1, 1) as i:
                early(2 * i + 1, i, 1)
                late(2 * i, i, 0)
                early(2 * i + 2, i + 1, 0)
                late(2 * i + 1, i, 1)
            n = HEADS // 2 - 1
            early(2 * n + 1, n, 1)
            late(2 * n, n, 0)
            late(2 * n + 1, n, 1)

        def after(eng, ends):
            for s, v in ends:
                eng.wait_ge(s, raised(s) + v)

        END_A = [(ct_copied, TILES), (qt_copied, TILES), (xa_turned, TILES)]
        END_CONV = [(conv_out[0], HEADS // 2), (conv_out[1], HEADS // 2)]
        END_B = [(yw_copied, TILES)]
        END_T = [(t_vec, T_GATED + 1)]
        END_C = [(xt_copied, TILES)]

        END_D = [(ro_act, 2 * RHEADS), (ro_vec, 2 * RHEADS)]
        END_E = [(x3_ready, TILES)]

        def batches(t):
            return t.rearrange("p (b t) e -> p b t e", t=2)

        ret_out = qt[:, :].rearrange("p (t n) -> p t n", t=TILES)

        def chunks(slot):
            def run(eng, g):
                slot(g, 0, 0, 0)
                slot(g, 1, 0, 1)
                slot(g, 2, 1, 0)
                with eng.Fori(1, (CHUNKS - 3) // 2, 1) as p:
                    slot(g, 2 * p + 1, p, 1)
                    slot(g, 2 * p + 2, p + 1, 0)
                slot(g, CHUNKS - 2, (CHUNKS - 3) // 2, 1)
                slot(g, CHUNKS - 1, (CHUNKS - 1) // 2, 0)
            return run

        def loads(g, half, u):
            return (6 * g + half + 1) if u == 0 else (5 * g + half + 1)

        block = stack.enter_context(nc.Block())

        @block.sync
        def _(sp):
            sp.dma_start(cst[:, :], consts).then_inc(s_const, 16)
            with sp.Fori(0, GROUPS, 1) as g:
                for j in range(GROUP):
                    sp.wait_ge(c_in[j], raised(c_in[j]) + 16 * g)
                    sp.sem_inc(passed, 1)
                    sp.wait_ge(ctx_turned, raised(ctx_turned) + GROUP * g + j + 1 - GROUP)
                    sp.sem_inc(passed, 1)
                    sp.dma_start(cin[:, j, :], cr[GROUP * g + j]).then_inc(c_in[j], 16)
                    sp.wait_ge(x_in[j], raised(x_in[j]) + 16 * g)
                    sp.sem_inc(passed, 1)
                    sp.dma_start(xres[:, GROUP * g + j, :], xr[GROUP * g + j]).then_inc(x_in[j], 16)
            after(sp, END_A)
            sp.dma_start(dcol[:, :], d_bc).then_inc(d_in, 16)
            with sp.Fori(0, HEADS // 2, 1) as i:
                for u in range(2):
                    sp.wait_ge(conv_done[u], raised(conv_done[u]) + i)
                    sp.sem_inc(passed, 1)
                    sp.dma_start(strip[:, u, :], strips[2 * i + u]).then_inc(strip_in[u], 16)
            after(sp, END_CONV)
            for dst, src in ((ewf[:, :, :], ew), (rwf[:, :], rw), (rbb[:, :], rb), (ebb[:, :], eb), (bitc[:, :], bits)):
                sp.dma_start(dst, src).then_inc(wB_in, 16)
            after(sp, END_C)
            sp.dma_start(whf[:, :, :], wh).then_inc(wh_in, 16)
            sp.dma_start(dmask[:, :, :], decay).then_inc(wh_in, 16)
            after(sp, END_D)
            sp.dma_start(wgf[:, :, :], wg).then_inc(wE_in, 16)
            sp.dma_start(wof[:, :, :], wo).then_inc(wE_in, 16)
            sp.dma_start(gbc[:, :], gb).then_inc(wE_in, 16)
            after(sp, END_E)
            for a, src in ((0, wr), (KB * FE, ag), (KB * FE + DIM, au), (KB * FE + 2 * DIM, bd)):
                sp.dma_start(lwf[:, a:a + src.shape[1]], src).then_inc(lw_in, 16)

            def slot(g, c, half, u):
                n = CHUNKS * g + c
                first = isinstance(c, int) and c == 0
                sp.wait_ge(dnl_ready, raised(dnl_ready) + (n if first else n - 1))
                sp.sem_inc(passed, 1)
                sp.dma_start(wst[:, u, :], chunk_w[c]).then_inc(wst_in[u], 16)

            with sp.Fori(0, GROUPS, 1) as g:
                chunks(slot)(sp, g)
            with sp.Fori(0, GROUPS, 1) as g:
                for j in range(GROUP):
                    sp.wait_ge(xo_ready, raised(xo_ready) + GROUP * g + j + 1)
                    sp.sem_inc(passed, 1)
                    sp.dma_start(outr[GROUP * g + j], xres[:, GROUP * g + j, :]).then_inc(out_written, 16)
            sp.wait_ge(out_written, 16 * TILES)

        @block.gpsimd
        def _(pool):
            for s, start in primed:
                pool.sem_inc(s, start)
            pool.memset(mhalf[:, :], -0.5).then_inc(s_mh, 1)
            pool.wait_ge(s_mh, 1)
            ln_rstd(pool, "A")
            after(pool, END_A)

            def kv_of(h, n, u):
                pool.wait_ge(kqx_ready[u], n + 1)
                pool.wait_ge(conv_done[u], raised(conv_done[u]) + n)
                pool.tensor_tensor(view(kv, u, 0, [[PAIRS, MB], [HD, 4], [1, HD]]),
                                   view(kx, u, 0, [[2 * HD, MB], [0, 4], [1, HD]]),
                                   view(kx, u, 0, [[2 * HD, MB], [1, 4], [1, HD]]), ALU.mult)
                pool.tensor_tensor(view(kv, u, 4 * HD, [[PAIRS, MB], [1, 4]]),
                                   view(kx, u, 0, [[2 * HD, MB], [1, 4]]),
                                   view(kx, u, 4, [[2 * HD, MB], [1, 4]]), ALU.mult).then_inc(kv_ready[u], 1)

            def opposite(h, n, u):
                pool.wait_ge(y_copied[u], raised(y_copied[u]) + n + 1)
                pool.wait_ge(conv_out[u], raised(conv_out[u]) + n)
                pool.tensor_tensor(view(pr, u, 7 * HD, [[HD * HD, MB], [4, 2], [1, 4]]),
                                   view(yx, u, 4 * (HD + WRAP), [[YP_, MB], [0, 2], [1, 4]]),
                                   view(qx, u, 4, [[2 * HD, MB], [-4, 2], [1, 4]]), ALU.mult)\
                    .then_inc(pr_pool[u], 1)

            skewed(pool, kv_of, opposite)
            after(pool, END_CONV)
            ln_rstd(pool, "B")
            after(pool, END_B)
            ln_rstd(pool, "C")
            pool.wait_ge(wh_in, 32)
            with pool.Fori(0, RHEADS, 1) as h:
                for q in range(4):
                    pool.wait_ge(cxh_ready, 4 * h + q + 1)
                    pool.sem_inc(passed, 1)
                    part = bass.ds(h * TOKENS + q * GTOK, GTOK)
                    pool.tensor_tensor(ccl[:, q % 2, :], ct[:, part], f(cch[:, q % 2, :]), ALU.subtract)
                    pool.tensor_tensor(xxl[:, q % 2, :], xt[:, part], f(xxh[:, q % 2, :]), ALU.subtract)\
                        .then_inc(cxl_ready, 1)
            after(pool, END_D)
            with pool.Fori(0, GROUPS, 1) as g:
                pool.wait_ge(xeh_ready, g + 1)
                pool.sem_inc(passed, 1)
                pool.tensor_tensor(xel[:, :, :], turned_group(xt, g), f(xeh[:, :, :]), ALU.subtract).then_inc(xel_ready, 1)
                pool.wait_ge(ln["E"]["var"], g + 1)
                pool.tensor_tensor(rstd[:, :], vare[:, :], mhalf[:, :], ALU.pow).then_inc(ln["E"]["rstd"], 1)
            after(pool, END_E)

            def cut_gu(g, c, u):
                pool.wait_ge(guh_ready, CHUNKS * g + c + 1)
                pool.tensor_tensor(gul[:, u, :], wst[:, u, 0:GU_W], f(guh[:, u, :]), ALU.subtract).then_inc(gul_ready, 1)

            def slot(g, c, half, u):
                n = CHUNKS * g + c
                if not (isinstance(c, int) and c == CHUNKS - 1):
                    cut_gu(g, c + 1, 1 - u)
                for s in range(3):
                    pool.wait_ge(hh_ready, 3 * n + s + 1)
                    pool.tensor_tensor(hl[:, u, s, :], hf[:, s, :], f(hh[:, u, s, :]), ALU.subtract)\
                        .then_inc(hl_ready[s], 1)
                    if s == 1:
                        pool.wait_ge(dnh_ready, n + 1)
                        pool.tensor_tensor(dnl[:, u, :], wst[:, u, GU_W:], f(dnh[:, u, :]), ALU.subtract)\
                            .then_inc(dnl_ready, 1)

            with pool.Fori(0, GROUPS, 1) as g:
                pool.wait_ge(ln["F"]["var"], g + 1)
                pool.tensor_tensor(rstd[:, :], vare[:, :], mhalf[:, :], ALU.pow).then_inc(ln["F"]["rstd"], 1)
                cut_gu(g, 0, 0)
                chunks(slot)(pool, g)

        @block.scalar
        def _(act):
            with act.Fori(0, GROUPS, 1) as g:
                for j in range(GROUP):
                    act.wait_ge(ctx_turned, raised(ctx_turned) + GROUP * g + j + 1)
                    act.sem_inc(passed, 1)
                    act.activation(turned(ct, GROUP * g + j), split(banks[:, j, :]),
                                   ACT.Copy).then_inc(ct_copied, 1)
            after(act, END_A)

            def doubled(h, n, u):
                act.wait_ge(kv_ready[u], raised(kv_ready[u]) + n)
                act.sem_inc(passed, 1)
                act.wait_ge(conv_out[u], raised(conv_out[u]) + n)
                act.sem_inc(passed, 1)
                for dst, src in ((kx, ct), (qx, qt)):
                    part = head_cols(src, h)
                    for rep in range(2):
                        i = act.activation(view(dst, u, rep * HD, [[2 * HD, MB], [1, HD]]), part, ACT.Copy)
                i.then_inc(kqx_ready[u], 1)

            def spread(h, n, u):
                act.wait_ge(conv_done[u], raised(conv_done[u]) + n + 1)
                act.sem_inc(passed, 1)
                act.wait_ge(conv_out[u], raised(conv_out[u]) + n)
                act.sem_inc(passed, 1)
                y = banks[:, 4 * u:4 * u + 4, :].rearrange("p l (b c) -> p (l b) c", b=BATCH)
                rows = y[:, :, 0:4 * HD].rearrange("p m (d i) -> p m d i", d=4)
                act.activation(view(yx, u, WRAP, [[YP_, MB], [HD + WRAP, 4], [1, HD]]), rows, ACT.Copy)
                act.activation(view(yx, u, HD + WRAP, [[YP_, MB], [HD + WRAP, 3], [1, WRAP]]),
                               rows[:, :, 1:4, HD - WRAP:HD], ACT.Copy)
                act.activation(view(yx, u, 4 * (HD + WRAP), [[YP_, MB], [1, 4]]),
                               y[:, :, 4 * HD:PAIRS], ACT.Copy).then_inc(y_copied[u], 1)

            skewed(act, doubled, spread)
            after(act, END_CONV)
            act.wait_ge(wB_in, 80)
            act.activation(ewh[:, :, :], ewf[:, :, :], ACT.Copy)
            act.activation(rwh[:, :], rwf[:, :], ACT.Copy).then_inc(wB_high, 1)
            with act.Fori(0, GROUPS, 1) as g:
                for j in range(GROUP):
                    act.wait_ge(o_turned, raised(o_turned) + GROUP * g + j + 1 - GROUP)
                    act.sem_inc(passed, 1)
                    act.activation(ost[:, j, :].rearrange("p (k n) -> p k n", k=KB), turned(qt, GROUP * g + j),
                                   ACT.Copy).then_inc(ost_ready, 1)
                for j in range(GROUP):
                    act.wait_ge(xb_turned, raised(xb_turned) + GROUP * g + j + 1)
                    act.sem_inc(passed, 1)
                    act.wait_ge(yw_done, raised(yw_done) + GROUP * g + j + 1 - GROUP)
                    act.sem_inc(passed, 1)
                    act.activation(xth[:, j, :], banks[:, 4 + j, :], ACT.Copy).then_inc(xth_ready, 1)
            act.wait_ge(t_vec, 2)
            act.activation(lg[:, :], lg[:, :], ACT.Exp).then_inc(t_exp, 1)
            with act.Fori(0, GROUPS, 1) as g:
                for j in range(GROUP):
                    act.wait_ge(xc_turned, raised(xc_turned) + GROUP * g + j + 1)
                    act.sem_inc(passed, 1)
                    if j == 0:
                        after(act, END_T)
                    act.activation(turned(xt, GROUP * g + j), split(banks[:, j, :]),
                                   ACT.Copy).then_inc(xt_copied, 1)
            act.wait_ge(wh_in, 32)

            def cut(h, q):
                act.wait_ge(mv_done[q % 2], raised(mv_done[q % 2]) + 2 * h + q // 2)
                act.sem_inc(passed, 1)
                act.wait_ge(sc_done[q % 2], raised(sc_done[q % 2]) + 2 * h + q // 2)
                act.sem_inc(passed, 1)
                part = bass.ds(h * TOKENS + q * GTOK, GTOK)
                act.activation(cch[:, q % 2, :], ct[:, part], ACT.Copy)
                act.activation(xxh[:, q % 2, :], xt[:, part], ACT.Copy).then_inc(cxh_ready, 1)

            def evac(h, q):
                act.wait_ge(m_done, 4 * h + q + 1)
                act.wait_ge(sc_done[q % 2], raised(sc_done[q % 2]) + 2 * h + q // 2)
                act.activation(mth[:, q % 2, :], banks[:, q % 2, :], ACT.Copy).then_inc(mth_ready, 1)
                act.wait_ge(mv_done[q % 2], raised(mv_done[q % 2]) + 2 * h + q // 2 + 1)
                act.wait_ge(ao_done, raised(ao_done) + 4 * h)
                act.activation(vh[:, 4 * q:4 * q + 4, :], banks[:, 2 + q % 2, :].rearrange("p (i e) -> p i e", i=4),
                               ACT.Copy).then_inc(vh_ready, 1)

            with act.Fori(0, RHEADS, 1) as h:
                act.wait_ge(mv_done[1], raised(mv_done[1]) + 2 * h)
                act.sem_inc(passed, 1)
                act.activation(whh[:, :], whf[:, h, :], ACT.Copy)
                act.activation(whs[:, :], whf[:, h, :], ACT.Copy).then_inc(whs_ready, 1)
                cut(h, 0)
                act.wait_ge(g_done, h + 1)
                act.activation(grh[:, :], banks[:, 7, 0:P], ACT.Copy).then_inc(grh_ready, 1)
                cut(h, 1)
                evac(h, 0)
                cut(h, 2)
                evac(h, 1)
                cut(h, 3)
                evac(h, 2)
                evac(h, 3)
                act.wait_ge(a_ready, h + 1)
                act.activation(ah[:, :], aw[:, :], ACT.Copy).then_inc(ah_ready, 1)
                for i in range(2):
                    act.wait_ge(ao_done, raised(ao_done) + 4 * h + i + 1)
                    act.sem_inc(passed, 1)
                    act.activation(batches(ret_out)[:, 4 * i:4 * i + 4, 0, bass.ts(h, P)],
                                   banks[:, i, :].rearrange("p (b e) -> p b e", b=4), ACT.Copy).then_inc(ro_act, 1)
            after(act, END_D)
            act.wait_ge(wE_in, 48)
            act.activation(wgh[:, :, :], wgf[:, :, :], ACT.Copy)
            act.activation(woh[:, :, :], wof[:, :, :], ACT.Copy).then_inc(wE_high, 1)
            with act.Fori(0, GROUPS, 1) as g:
                act.wait_ge(wt_done, raised(wt_done) + KB * g)
                act.sem_inc(passed, 1)
                act.activation(xeh[:, :, :], turned_group(xt, g), ACT.Copy).then_inc(xeh_ready, 1)
                act.wait_ge(ul_ready, raised(ul_ready) + g)
                for j in range(GROUP):
                    act.wait_ge(y_turned, raised(y_turned) + GROUP * g + j + 1)
                    for k in range(KB):
                        i = act.activation(zt[:, k, j * P:(j + 1) * P], banks[:, j, k * P:(k + 1) * P], ACT.Identity,
                                           bias=gbc[:, KB + k:KB + k + 1], scale=gbc[:, k:k + 1])
                    i.then_inc(zt_ready, 1)
                act.wait_ge(zu_ready, raised(zu_ready) + KB * g + KB)
                act.wait_ge(wo_done, raised(wo_done) + GROUP * g)
                act.activation(uh[:, :, :], zt[:, :, :], ACT.Copy).then_inc(uh_ready, 1)
            after(act, END_E)
            act.wait_ge(lw_in, 64)
            act.activation(lwh[:, :], lwf[:, :], ACT.Copy).then_inc(lwh_ready, 1)

            def slot(g, c, half, u):
                n = CHUNKS * g + c
                for s in range(3):
                    act.wait_ge(gu_ready, raised(gu_ready) + 3 * n + s + 1)
                    act.activation(silu[:, s % 2, :], banks[:, 6, :], ACT.Silu).then_inc(silu_done, 1)
                    act.wait_ge(mul_done, raised(mul_done) + 3 * n + s + 1)
                    act.activation(hh[:, u, s, :], hf[:, s, :], ACT.Copy).then_inc(hh_ready, 1)

            with act.Fori(0, GROUPS, 1) as g:
                for j in range(GROUP):
                    act.wait_ge(xf_turned, raised(xf_turned) + GROUP * g + j + 1)
                    act.activation(xfh[:, :, j * P:(j + 1) * P], split(banks[:, j, :]), ACT.Copy).then_inc(xfh_ready, 1)
                act.wait_ge(r_vec, raised(r_vec) + R_STEPS * g + 3)
                act.activation(rt[:, 0, :], rt[:, 0, :], ACT.Exp).then_inc(r_exp, 1)
                act.wait_ge(mk_turned, g + 1)
                act.activation(mk[:, :, :], banks[:, 0:4, :], ACT.Copy).then_inc(mk_ready, 1)
                act.wait_ge(rf_ready, g + 1)
                act.activation(rh[:, :, :], rf[:, :, :], ACT.Copy).then_inc(rh_ready, 1)
                chunks(slot)(act, g)
                act.wait_ge(z_vec, raised(z_vec) + 2 * g + 2)
                act.activation(zh[:, :], zf[:, 0, :], ACT.Copy).then_inc(zh_ready, 1)

        @block.tensor
        def _(pe):
            pe.wait_ge(s_const, 16)
            with pe.Fori(0, GROUPS, 1) as g:
                for j in range(GROUP):
                    pe.wait_ge(c_in[j], raised(c_in[j]) + 16 * (g + 1))
                    pe.wait_ge(ct_copied, raised(ct_copied) + GROUP * g + j + 1 - GROUP)
                    turn(pe, j, cin[:, j, :], ctx_turned)
                for j in range(GROUP):
                    pe.wait_ge(ln["A"]["xn"], raised(ln["A"]["xn"]) + GROUP * g + j + 1)
                    pe.wait_ge(qt_copied, raised(qt_copied) + GROUP * g + j + 1 - GROUP)
                    turn(pe, 4 + j, xn[:, j, :], xa_turned)
            after(pe, END_A)
            with pe.Fori(0, HEADS // 2, 1) as i:
                for u in range(2):
                    pe.wait_ge(strip_ready[u], i + 1)
                    pe.wait_ge(kv_ready[u], raised(kv_ready[u]) + i + 1)
                    pe.wait_ge(y_copied[u], raised(y_copied[u]) + i)
                    for lb in range(KB):
                        dst = banks[:, 4 * u + lb, :].rearrange("p (b c) -> p b c", b=BATCH)[:, :, 0:PAIRS]
                        for m in range(lb + 1):
                            mm = pe.matmul(dst, strip[:, u, (lb - m) * P:(lb - m + 1) * P],
                                           view(kv, u, m * BATCH * PAIRS, [[PAIRS, BATCH], [1, PAIRS]]),
                                           start=m == 0, stop=m == lb)
                    mm.then_inc(conv_done[u], 1)
            after(pe, END_CONV)
            pe.wait_ge(wB_ready, 1)
            with pe.Fori(0, GROUPS, 1) as g:
                for j in range(GROUP):
                    pe.wait_ge(ost_ready, GROUP * g + j + 1)
                    pe.wait_ge(yw_copied, raised(yw_copied) + GROUP * g + j + 1 - GROUP)
                    turn(pe, j, ost[:, j, :], o_turned)
                for j in range(GROUP):
                    pe.wait_ge(ln["B"]["xn"], raised(ln["B"]["xn"]) + GROUP * g + j + 1)
                    turn(pe, 4 + j, xn[:, j, :], xb_turned)
                for j in range(GROUP):
                    pe.wait_ge(xtl_ready, raised(xtl_ready) + GROUP * g + j + 1)
                    for k in range(KB):
                        a, b = k * P, (k + 1) * P
                        product(pe, banks[:, j, :], xth[:, j, a:b], xtl[:, j, a:b], ewh[:, k, :], ewl[:, k, :],
                                k == 0, k == KB - 1)
                    for k in range(KB):
                        a, b = k * P, (k + 1) * P
                        e = slice(k * EXPERTS, (k + 1) * EXPERTS)
                        mm = product(pe, banks[:, 4 + j, 0:EXPERTS], xth[:, j, a:b], xtl[:, j, a:b],
                                     rwh[:, e], rwl[:, e], k == 0, k == KB - 1)
                    mm.then_inc(yw_done, 1)
            pe.wait_ge(t_vec, 5)
            for c in range(2):
                mm = pe.transpose(banks[:, 0, c * P:(c + 1) * P], lg[:, c * P:(c + 1) * P], ident)
            mm.then_inc(t_pe, 1)
            with pe.Fori(0, BITS, 1) as i:
                pe.wait_ge(bit_cnt, i + 1)
                pe.matmul(banks[:, 1, 0:2], same_e, cnt[:, 0:2], start=True, stop=True).then_inc(bit_sum, 1)
            pe.wait_ge(t_vec, 10)
            pe.matmul(banks[:, 2, 0:1], same_e, cnt[:, 2:3], start=True, stop=True)
            pe.matmul(banks[:, 3, 0:1], lower_e, cnt[:, 3:4], start=True, stop=True)
            pe.matmul(banks[:, 4, 0:1], lower_e, cnt[:, 4:5], start=True, stop=False)
            pe.matmul(banks[:, 4, 0:1], same_e, cnt[:, 3:4], start=False, stop=True).then_inc(t_pe, 1)
            pe.wait_ge(t_vec, T_GATED)
            for c in range(2):
                mm = pe.matmul(banks[:, 5, c * 8:(c + 1) * 8], st_[:, c * P:(c + 1) * P], tile_sel,
                               start=True, stop=True)
            mm.then_inc(t_pe, 1)
            with pe.Fori(0, GROUPS, 1) as g:
                for j in range(GROUP):
                    pe.wait_ge(ln["C"]["xn"], raised(ln["C"]["xn"]) + GROUP * g + j + 1)
                    pe.wait_ge(xt_copied, raised(xt_copied) + GROUP * g + j + 1 - GROUP)
                    turn(pe, j, xn[:, j, :], xc_turned)
            def project(h, q):
                u = q % 2
                pe.wait_ge(cxl_ready, 4 * h + q + 1)
                pe.wait_ge(mtl_ready[u], raised(mtl_ready[u]) + 2 * h + q // 2)
                pe.wait_ge(vl_ready[u], raised(vl_ready[u]) + 2 * h + q // 2)
                if q == 0:
                    pe.wait_ge(grl_ready, h + 1)
                    pe.wait_ge(ro_act, raised(ro_act) + 2 * h)
                    pe.wait_ge(ro_vec, raised(ro_vec) + 2 * h)
                product(pe, banks[:, u, :], grh[:, :], grl[:, :], cch[:, u, :], ccl[:, u, :], True, True)\
                    .then_inc(m_done, 1)
                for i in range(4):
                    a, b = i * P, (i + 1) * P
                    mm = product(pe, banks[:, 2 + u, a:b], cch[:, u, a:b], ccl[:, u, a:b], whh[:, :], whl[:, :], True, True)
                mm.then_inc(mv_done[u], 1)

            def scores(h, q):
                u = q % 2
                pe.wait_ge(mtl_ready[u], raised(mtl_ready[u]) + 2 * h + q // 2 + 1)
                if q == 0:
                    pe.wait_ge(a_read, raised(a_read) + h)
                for b in range(2):
                    o = b * SEQ
                    first, last = q == 0 and b == 0, q == 3 and b == 1
                    product(pe, banks[:, 4, 0:SEQ], mth[:, u, o:o + P], mtl[:, u, o:o + P],
                            xxh[:, u, o:o + SEQ], xxl[:, u, o:o + SEQ], first, last)
                    mm = product(pe, banks[:, 5, 0:P], mth[:, u, o + P:o + SEQ], mtl[:, u, o + P:o + SEQ],
                                 xxh[:, u, o + P:o + SEQ], xxl[:, u, o + P:o + SEQ], first, last)
                mm.then_inc(sc_done[u], 1)

            with pe.Fori(0, RHEADS, 1) as h:
                pe.wait_ge(whl_ready, h + 1)
                pe.transpose(banks[:, 6, 0:P], whs[:, :], ident).then_inc(wh_turned, 1)
                pe.wait_ge(wht_ready, h + 1)
                pe.matmul(banks[:, 7, 0:P], wht[:, :], wht[:, :], start=True, stop=True).then_inc(g_done, 1)
                project(h, 0)
                project(h, 1)
                scores(h, 0)
                project(h, 2)
                scores(h, 1)
                project(h, 3)
                scores(h, 2)
                scores(h, 3)
                pe.wait_ge(al_ready, raised(al_ready) + h + 1)
                pe.wait_ge(vl_ready[0], raised(vl_ready[0]) + 2 * h + 2)
                pe.wait_ge(vl_ready[1], raised(vl_ready[1]) + 2 * h + 2)
                for half in range(2):
                    for i in range(2):
                        bank = 2 * half + i
                        for t in range(2):
                            a = t * SEQ + half * P
                            mm = product(pe, banks[:, bank, :].rearrange("p (b e) -> p b e", b=4), ah[:, a:a + P], al[:, a:a + P],
                                         batches(vh[:, :, :])[:, 4 * i:4 * i + 4, t, :],
                                         batches(vl[:, :, :])[:, 4 * i:4 * i + 4, t, :], t == 0, t == 1)
                        mm.then_inc(ao_done, 1)
            after(pe, END_D)
            pe.wait_ge(wE_ready, 1)
            with pe.Fori(0, GROUPS, 1) as g:
                pe.wait_ge(xel_ready, g + 1)
                for jb in range(KB):
                    pe.wait_ge(zu_ready, raised(zu_ready) + KB * g)
                    for k in range(KB):
                        mm = product(pe, banks[:, 4 + jb, :], wgh[:, k, jb * P:(jb + 1) * P], wgl[:, k, jb * P:(jb + 1) * P],
                                     xeh[:, k, :], xel[:, k, :], k == 0, k == KB - 1)
                    mm.then_inc(wt_done, 1)
                for j in range(GROUP):
                    pe.wait_ge(ln["E"]["xn"], raised(ln["E"]["xn"]) + GROUP * g + j + 1)
                    pe.wait_ge(x3_ready, raised(x3_ready) + GROUP * g)
                    turn(pe, j, xn[:, j, :], y_turned)
                pe.wait_ge(ul_ready, raised(ul_ready) + g + 1)
                for j in range(GROUP):
                    for k in range(KB):
                        mm = product(pe, banks[:, j, :], uh[:, k, j * P:(j + 1) * P], ul[:, k, j * P:(j + 1) * P],
                                     woh[:, k, :], wol[:, k, :], k == 0, k == KB - 1)
                    mm.then_inc(wo_done, 1)
            after(pe, END_E)
            R0, A0, U0, B0 = 0, KB * FE, KB * FE + DIM, KB * FE + 2 * DIM
            pe.wait_ge(lwl_ready, 1)

            def base(g, c, u):
                n = CHUNKS * g + c
                pe.wait_ge(gul_ready, n + 1)
                pe.wait_ge(mul_done, raised(mul_done) + 3 * n)
                for bank, o in ((6, 0), (7, DIM)):
                    for k in range(KB):
                        a, b = o + k * P, o + (k + 1) * P
                        mm = product(pe, banks[:, bank, :], guh[:, u, a:b], gul[:, u, a:b],
                                     xfh[:, k, :], xfl[:, k, :], k == 0, k == KB - 1)
                mm.then_inc(gu_ready, 1)

            def lora(g, c, u, s):
                n = CHUNKS * g + c
                pe.wait_ge(mul_done, raised(mul_done) + 3 * n + s + 1)
                for bank, o, r in ((6, 2 * DIM, s), (7, 2 * DIM + P, 2 + s)):
                    mm = product(pe, banks[:, bank, :], guh[:, u, o:o + P], gul[:, u, o:o + P],
                                 rh[:, r, :], rl[:, r, :], False, True, check=True)
                mm.then_inc(gu_ready, 1)

            def down(g, c, u, part):
                n = CHUNKS * g + c
                first, last = isinstance(c, int) and c == 0, isinstance(c, int) and c == CHUNKS - 1
                if part < 2:
                    if part == 0:
                        pe.wait_ge(dnl_ready, raised(dnl_ready) + n + 1)
                        pe.wait_ge(hl_ready[0], raised(hl_ready[0]) + n + 1)
                    for j in (2 * part, 2 * part + 1):
                        product(pe, banks[:, j, :], hh[:, u, 0, j * P:(j + 1) * P], hl[:, u, 0, j * P:(j + 1) * P],
                                dnh[:, u, 0:DIM], dnl[:, u, 0:DIM], first, False, check=True)
                    return
                for s in (1, 2):
                    pe.wait_ge(hl_ready[s], raised(hl_ready[s]) + n + 1)
                    mm = product(pe, banks[:, 3 + s, :], dnh[:, u, DIM:], dnl[:, u, DIM:],
                                 hh[:, u, s, :], hl[:, u, s, :], first, last, check=True)
                mm.then_inc(down_done, 1)

            def slot(g, c, half, u):
                if isinstance(c, int) and c == 0:
                    pe.wait_ge(rl_ready, g + 1)
                    lora(g, c, u, 0)
                    lora(g, c, u, 1)
                    return
                before = c - 1
                base(g, c, u)
                down(g, before, 1 - u, 0)
                lora(g, c, u, 0)
                down(g, before, 1 - u, 1)
                lora(g, c, u, 1)
                down(g, before, 1 - u, 2)

            with pe.Fori(0, GROUPS, 1) as g:
                for j in range(GROUP):
                    pe.wait_ge(ln["F"]["xn"], raised(ln["F"]["xn"]) + GROUP * g + j + 1)
                    pe.wait_ge(xo_ready, raised(xo_ready) + GROUP * g)
                    turn(pe, j, xn[:, j, :], xf_turned)
                pe.wait_ge(xfl_ready, GROUP * g + GROUP)
                for j in range(GROUP):
                    for k in range(KB):
                        a, b = j * P, (j + 1) * P
                        r = slice(R0 + k * FE, R0 + (k + 1) * FE)
                        mm = product(pe, banks[:, 0, j * FE:(j + 1) * FE], xfh[:, k, a:b], xfl[:, k, a:b],
                                     lwh[:, r], lwl[:, r], k == 0, k == KB - 1)
                mm.then_inc(lgt_done, 1)
                pe.wait_ge(z_vec, raised(z_vec) + 2 * g)
                for bank, o in ((4, A0), (5, U0)):
                    for k in range(KB):
                        mm = product(pe, banks[:, bank, :], lwh[:, o + k * P:o + (k + 1) * P], lwl[:, o + k * P:o + (k + 1) * P],
                                     xfh[:, k, :], xfl[:, k, :], k == 0, k == KB - 1)
                mm.then_inc(ra_done, 1)
                base(g, 0, 0)
                pe.wait_ge(r_vec, raised(r_vec) + R_STEPS * g + R_STEPS)
                for q in range(4):
                    for j in range(GROUP):
                        mm = pe.transpose(banks[:, q, j * P:(j + 1) * P], ex[:, q, j * P:(j + 1) * P], ident)
                mm.then_inc(mk_turned, 1)
                chunks(slot)(pe, g)
                for part in range(3):
                    down(g, CHUNKS - 1, 0, part)
                pe.wait_ge(zl_ready, g + 1)
                for j in range(GROUP):
                    mm = product(pe, banks[:, j, :], zh[:, j * P:(j + 1) * P], zl[:, j * P:(j + 1) * P],
                                 lwh[:, B0:B0 + DIM], lwl[:, B0:B0 + DIM], False, True, check=True)
                mm.then_inc(fo_done, 1)

        @block.vector
        def _(dve):
            dve.wait_ge(s_mh, 1)
            with dve.Fori(0, GROUPS, 1) as g:
                ln_stats(dve, "A", g, lambda j: xres[:, GROUP * g + j, :],
                         lambda j: hold(dve, x_in[j], 16 * (g + 1)), EPS)
                for j in range(GROUP):
                    dve.wait_ge(xa_turned, raised(xa_turned) + GROUP * g + j + 1 - GROUP)
                    ln_apply(dve, "A", j, xres[:, GROUP * g + j, :])
                for j in range(GROUP):
                    dve.wait_ge(xa_turned, raised(xa_turned) + GROUP * g + j + 1)
                    dve.tensor_copy(turned(qt, GROUP * g + j),
                                    banks[:, 4 + j, :].rearrange("p (k n) -> p k n", k=KB)).then_inc(qt_copied, 1)
            after(dve, END_A)
            dve.wait_ge(d_in, 16)

            def diagonal(h, n, u):
                dve.wait_ge(strip_in[u], 16 * (n + 1))
                dve.scalar_tensor_tensor(strip[:, u, 0:P], ident, dcol[:, bass.ds(h, 1)], strip[:, u, 0:P],
                                         ALU.mult, ALU.add).then_inc(strip_ready[u], 1)

            def weigh(h, n, u):
                dve.wait_ge(y_copied[u], raised(y_copied[u]) + n + 1)
                dve.wait_ge(conv_out[u], raised(conv_out[u]) + n)
                dve.tensor_tensor(view(pr, u, 0, [[HD * HD, MB], [HD, 4], [1, HD]]),
                                  view(yx, u, WRAP, [[YP_, MB], [HD + WRAP, 4], [1, HD]]),
                                  view(qx, u, 0, [[2 * HD, MB], [1, 4], [1, HD]]), ALU.mult)
                dve.tensor_tensor(view(pr, u, 4 * HD, [[HD * HD, MB], [HD, 3], [1, HD]]),
                                  view(yx, u, HD + 2 * WRAP - 1, [[YP_, MB], [HD + WRAP - 1, 3], [1, HD]]),
                                  view(qx, u, HD - 1, [[2 * HD, MB], [-1, 3], [1, HD]]), ALU.mult)\
                    .then_inc(pr_vec[u], 1)
                dve.wait_ge(pr_vec[u], n + 1)
                dve.wait_ge(pr_pool[u], n + 1)
                dve.tensor_reduce(head_cols(qt, h), view(pr, u, 0, [[HD * HD, MB], [1, HD], [HD, HD]]),
                                  X_AXIS, ALU.add).then_inc(conv_out[u], 1)

            skewed(dve, diagonal, weigh)
            after(dve, END_CONV)
            dve.wait_ge(wB_high, 1)
            dve.tensor_tensor(ewl[:, :, :], ewf[:, :, :], f(ewh[:, :, :]), ALU.subtract)
            dve.tensor_tensor(rwl[:, :], rwf[:, :], f(rwh[:, :]), ALU.subtract).then_inc(wB_ready, 1)
            with dve.Fori(0, GROUPS, 1) as g:
                for j in range(GROUP):
                    dve.wait_ge(o_turned, raised(o_turned) + GROUP * g + j + 1)
                    dve.tensor_tensor(xres[:, GROUP * g + j, :], xres[:, GROUP * g + j, :], banks[:, j, :],
                                      ALU.add).then_inc(x1_ready, 1)
                ln_stats(dve, "B", g, lambda j: xres[:, GROUP * g + j, :],
                         lambda j: hold(dve, x1_ready, GROUP * g + j + 1), EPS)
                for j in range(GROUP):
                    dve.wait_ge(xb_turned, raised(xb_turned) + GROUP * g + j + 1 - GROUP)
                    ln_apply(dve, "B", j, xres[:, GROUP * g + j, :])
                for j in range(GROUP):
                    dve.wait_ge(xth_ready, raised(xth_ready) + GROUP * g + j + 1)
                    dve.tensor_tensor(xtl[:, j, :], banks[:, 4 + j, :], f(xth[:, j, :]), ALU.subtract)\
                        .then_inc(xtl_ready, 1)
                for j in range(GROUP):
                    dve.wait_ge(yw_done, raised(yw_done) + GROUP * g + j + 1)
                    dve.tensor_tensor(turned(qt, GROUP * g + j), split(banks[:, j, :]), split(ebb[:, :]), ALU.add)
                    dve.tensor_tensor(lg[:, bass.ts(GROUP * g + j, EXPERTS)], banks[:, 4 + j, 0:EXPERTS], rbb[:, :],
                                      ALU.add).then_inc(yw_copied, 1)
            n_vec = [0]

            def step(ins):
                n_vec[0] += 1
                ins.then_inc(t_vec, 1)
                dve.wait_ge(t_vec, n_vec[0])

            lg3 = lg[:, :].rearrange("p (t e) -> p t e", e=EXPERTS)

            def over_experts(ap):
                return ap.unsqueeze(2).to_broadcast([P, TILES, EXPERTS])

            dve.wait_ge(yw_copied, raised(yw_copied) + TILES)
            step(dve.tensor_reduce(lsc[:, 0:TILES], lg3, X_AXIS, ALU.max))
            step(dve.tensor_tensor(lg3, lg3, over_experts(lsc[:, 0:TILES]), ALU.subtract))
            dve.wait_ge(t_exp, 1)
            step(dve.tensor_reduce(lsc[:, TILES:], lg3, X_AXIS, ALU.add))
            step(dve.reciprocal(lsc[:, 0:TILES], lsc[:, TILES:]))
            step(dve.tensor_tensor(lg3, lg3, over_experts(lsc[:, 0:TILES]), ALU.mult))
            dve.memset(onesr[:, :], 1.0)
            dve.memset(cnt[:, :], 0.0)
            step(dve.memset(pre[:, :], 0))
            dve.wait_ge(t_pe, 1)
            step(dve.tensor_copy(st_[:, :], banks[:, 0, 0:2 * P]))
            with dve.Fori(0, BITS, 1) as i:
                bit = bitc[:, bass.ds(i, 1)]
                dve.wait_ge(bit_vec, raised(bit_vec) + 3 * i)
                dve.tensor_tensor(pre[:, 1:2], pre[:, 0:1], bit, ALU.bitwise_or).then_inc(bit_vec, 1)
                dve.wait_ge(bit_vec, raised(bit_vec) + 3 * i + 1)
                dve.tensor_scalar(junk[:, :], st_[:, :], f(pre[:, 1:2]), None, ALU.is_ge, ALU.add,
                                  accum_out=cnt[:, 0:1]).then_inc(bit_cnt, 1)
                dve.wait_ge(bit_sum, i + 1)
                dve.scalar_tensor_tensor(pre[:, 2:3], banks[:, 1, 0:1], CAPACITY - 0.5, bit, ALU.is_ge, ALU.mult)\
                    .then_inc(bit_vec, 1)
                dve.wait_ge(bit_vec, raised(bit_vec) + 3 * i + 2)
                dve.tensor_tensor(pre[:, 0:1], pre[:, 0:1], pre[:, 2:3], ALU.bitwise_or).then_inc(bit_vec, 1)
            dve.wait_ge(bit_vec, raised(bit_vec) + 3 * BITS)
            thr = f(pre[:, 0:1])
            step(dve.tensor_scalar(junk[:, :], st_[:, :], thr, None, ALU.is_gt, ALU.add, accum_out=cnt[:, 2:3]))
            step(dve.tensor_scalar(eqs[:, 0:P], st_[:, 0:P], thr, None, ALU.is_equal, ALU.add, accum_out=cnt[:, 3:4]))
            step(dve.tensor_scalar(eqs[:, P:], st_[:, P:], thr, None, ALU.is_equal, ALU.add, accum_out=cnt[:, 4:5]))
            dve.wait_ge(t_pe, 2)
            step(dve.tensor_scalar(cnt[:, 5:6], banks[:, 2, 0:1], -1.0, float(CAPACITY), ALU.mult, ALU.add))
            step(dve.tensor_copy(cnt[:, 6:7], banks[:, 3, 0:1]))
            step(dve.tensor_copy(cnt[:, 7:8], banks[:, 4, 0:1]))
            for c in range(2):
                step(dve.tensor_tensor_scan(scan[:, c * P:(c + 1) * P], onesr[:, :], eqs[:, c * P:(c + 1) * P],
                                            cnt[:, 6 + c:7 + c], ALU.mult, ALU.add))
            step(dve.scalar_tensor_tensor(scan[:, :], scan[:, :], cnt[:, 5:6], eqs[:, :], ALU.is_le, ALU.mult))
            step(dve.tensor_tensor(scan[:, :], scan[:, :], junk[:, :], ALU.add))
            step(dve.tensor_tensor(st_[:, :], st_[:, :], scan[:, :], ALU.mult))
            assert n_vec[0] == T_GATED
            dve.wait_ge(t_pe, 3)
            step(dve.tensor_copy(gate[:, :], banks[:, 5, 0:TILES]))
            assert n_vec[0] == END_T[0][1]
            with dve.Fori(0, GROUPS, 1) as g:
                for j in range(GROUP):
                    t = GROUP * g + j
                    dve.scalar_tensor_tensor(split(xres[:, t, :]), turned(qt, t), gate[:, bass.ds(t, 1)], split(xres[:, t, :]),
                                             ALU.mult, ALU.add).then_inc(x2_ready, 1)
                ln_stats(dve, "C", g, lambda j: xres[:, GROUP * g + j, :],
                         lambda j: hold(dve, x2_ready, GROUP * g + j + 1), EPS)
                for j in range(GROUP):
                    dve.wait_ge(xc_turned, raised(xc_turned) + GROUP * g + j + 1 - GROUP)
                    ln_apply(dve, "C", j, xres[:, GROUP * g + j, :])
            dve.wait_ge(wh_in, 32)
            dve.memset(aw[:, :], 1.0).then_inc(ones_set, 1)
            dve.wait_ge(ones_set, 1)

            def low(h, q):
                u = q % 2
                dve.wait_ge(mth_ready, 4 * h + q + 1)
                dve.tensor_tensor(mtl[:, u, :], banks[:, u, :], f(mth[:, u, :]), ALU.subtract).then_inc(mtl_ready[u], 1)
                dve.wait_ge(vh_ready, 4 * h + q + 1)
                dve.tensor_tensor(vl[:, 4 * q:4 * q + 4, :], banks[:, 2 + u, :].rearrange("p (i e) -> p i e", i=4),
                                  f(vh[:, 4 * q:4 * q + 4, :]), ALU.subtract).then_inc(vl_ready[u], 1)

            with dve.Fori(0, RHEADS, 1) as h:
                dve.wait_ge(whs_ready, h + 1)
                dve.tensor_tensor(whl[:, :], whf[:, h, :], f(whh[:, :]), ALU.subtract).then_inc(whl_ready, 1)
                dve.wait_ge(wh_turned, h + 1)
                dve.tensor_copy(wht[:, :], banks[:, 6, 0:P]).then_inc(wht_ready, 1)
                dve.wait_ge(grh_ready, h + 1)
                dve.tensor_tensor(grl[:, :], banks[:, 7, 0:P], f(grh[:, :]), ALU.subtract).then_inc(grl_ready, 1)
                for q in range(4):
                    low(h, q)
                dve.wait_ge(al_ready, raised(al_ready) + h)
                for u in range(2):
                    dve.wait_ge(sc_done[u], raised(sc_done[u]) + 2 * h + 2)
                dve.tensor_tensor(aw[:, 0:SEQ], banks[:, 4, 0:SEQ], dmask[:, h, 0:SEQ], ALU.mult)
                dve.tensor_tensor(aw[:, SEQ + P:], banks[:, 5, 0:P], dmask[:, h, SEQ + P:], ALU.mult).then_inc(a_read, 1)
                dve.wait_ge(a_read, raised(a_read) + h + 1)
                dve.scalar_tensor_tensor(aw[:, :], aw[:, :], -1.0, aw[:, :], ALU.mult, ALU.max).then_inc(a_abs, 1)
                dve.wait_ge(a_abs, h + 1)
                dve.tensor_scalar(aw[:, :], aw[:, :], 1.0, None, ALU.max).then_inc(a_ready, 1)
                dve.wait_ge(ah_ready, h + 1)
                dve.tensor_tensor(al[:, :], aw[:, :], f(ah[:, :]), ALU.subtract).then_inc(al_ready, 1)
                for i in range(2):
                    dve.wait_ge(ao_done, raised(ao_done) + 4 * h + 2 + i + 1)
                    dve.sem_inc(passed, 1)
                    dve.tensor_copy(batches(ret_out)[:, 4 * i:4 * i + 4, 1, bass.ts(h, P)],
                                    banks[:, 2 + i, :].rearrange("p (b e) -> p b e", b=4)).then_inc(ro_vec, 1)
            after(dve, END_D)
            dve.wait_ge(wE_high, 1)
            dve.tensor_tensor(wgl[:, :, :], wgf[:, :, :], f(wgh[:, :, :]), ALU.subtract)
            dve.tensor_tensor(wol[:, :, :], wof[:, :, :], f(woh[:, :, :]), ALU.subtract).then_inc(wE_ready, 1)
            with dve.Fori(0, GROUPS, 1) as g:
                ln_stats(dve, "E", g, lambda j: tile_rows(qt, GROUP * g + j), lambda j: None, GN_EPS)
                for j in range(GROUP):
                    dve.wait_ge(y_turned, raised(y_turned) + GROUP * g + j + 1 - GROUP)
                    ln_apply(dve, "E", j, tile_rows(qt, GROUP * g + j))
                for jb in range(KB):
                    dve.wait_ge(wt_done, raised(wt_done) + KB * g + jb + 1)
                    dve.wait_ge(zt_ready, GROUP * g + GROUP)
                    dve.scalar_tensor_tensor(zt[:, jb, :], banks[:, 4 + jb, :], 0.0, zt[:, jb, :], ALU.max, ALU.mult)\
                        .then_inc(zu_ready, 1)
                dve.wait_ge(uh_ready, g + 1)
                dve.tensor_tensor(ul[:, :, :], zt[:, :, :], f(uh[:, :, :]), ALU.subtract).then_inc(ul_ready, 1)
                for j in range(GROUP):
                    dve.wait_ge(wo_done, raised(wo_done) + GROUP * g + j + 1)
                    dve.tensor_tensor(xres[:, GROUP * g + j, :], xres[:, GROUP * g + j, :], banks[:, j, :], ALU.add)\
                        .then_inc(x3_ready, 1)
            after(dve, END_E)
            dve.wait_ge(lwh_ready, 1)
            dve.tensor_tensor(lwl[:, :], lwf[:, :], f(lwh[:, :]), ALU.subtract).then_inc(lwl_ready, 1)

            def cut_gu(g, c, half, u, uses):
                dve.wait_ge(wst_in[u], 16 * loads(g, half, u))
                dve.wait_ge(gu_ready, raised(gu_ready) + uses)
                dve.tensor_copy(guh[:, u, :], wst[:, u, 0:GU_W]).then_inc(guh_ready, 1)

            def slot(g, c, half, u):
                n = CHUNKS * g + c
                for s in range(3):
                    dve.wait_ge(silu_done, 3 * n + s + 1)
                    dve.wait_ge(hl_ready[s], raised(hl_ready[s]) + n)
                    dve.tensor_tensor(hf[:, s, :], banks[:, 7, :], silu[:, s % 2, :], ALU.mult).then_inc(mul_done, 1)
                    if s == 0 and not (isinstance(c, int) and c == CHUNKS - 1):
                        cut_gu(g, c + 1, half + (1 if u == 1 else 0), 1 - u, 3 * n)
                    if s == 1:
                        first = isinstance(c, int) and c == 0
                        dve.wait_ge(down_done, raised(down_done) + (n if first else n - 1))
                        dve.tensor_copy(dnh[:, u, :], wst[:, u, GU_W:]).then_inc(dnh_ready, 1)

            with dve.Fori(0, GROUPS, 1) as g:
                ln_stats(dve, "F", g, lambda j: xres[:, GROUP * g + j, :], lambda j: None, EPS)
                for j in range(GROUP):
                    dve.wait_ge(xf_turned, raised(xf_turned) + GROUP * g + j + 1 - GROUP)
                    ln_apply(dve, "F", j, xres[:, GROUP * g + j, :])
                for j in range(GROUP):
                    dve.wait_ge(xfh_ready, GROUP * g + j + 1)
                    dve.tensor_tensor(xfl[:, :, j * P:(j + 1) * P], split(banks[:, j, :]),
                                      f(xfh[:, :, j * P:(j + 1) * P]), ALU.subtract).then_inc(xfl_ready, 1)
                cut_gu(g, 0, 0, 0, 3 * CHUNKS * g)
                k_vec = [0]

                def link(ins):
                    k_vec[0] += 1
                    ins.then_inc(r_vec, 1)
                    dve.wait_ge(r_vec, raised(r_vec) + R_STEPS * g + k_vec[0])

                def by_e(i):
                    return rt[:, i, :].rearrange("p (t e) -> p t e", e=FE)

                def per_token(i):
                    return rsm[:, i, :].unsqueeze(2).to_broadcast([P, GROUP, FE])

                dve.wait_ge(lgt_done, g + 1)
                link(dve.tensor_copy(rt[:, 0, :], banks[:, 0, 0:GROUP * FE]))
                link(dve.tensor_reduce(rsm[:, 0, :], by_e(0), X_AXIS, ALU.max))
                link(dve.tensor_tensor(by_e(0), by_e(0), per_token(0), ALU.subtract))
                dve.wait_ge(r_exp, g + 1)
                link(dve.tensor_reduce(rsm[:, 1, :], by_e(0), X_AXIS, ALU.add))
                link(dve.reciprocal(rsm[:, 2, :], rsm[:, 1, :]))
                link(dve.tensor_tensor(by_e(0), by_e(0), per_token(2), ALU.mult))
                for probs, hot in ((0, 3), (4, 5)):
                    link(dve.tensor_reduce(rsm[:, 3, :], by_e(probs), X_AXIS, ALU.max))
                    link(dve.tensor_tensor(by_e(1), by_e(probs), per_token(3), ALU.is_equal))
                    link(dve.tensor_tensor(rt[:, 2, :], rt[:, 1, :], rank8, ALU.mult))
                    link(dve.tensor_reduce(rsm[:, 4, :], by_e(2), X_AXIS, ALU.max))
                    link(dve.tensor_tensor(by_e(hot), by_e(2), per_token(4), ALU.is_equal))
                    if probs == 0:
                        link(dve.scalar_tensor_tensor(rt[:, 4, :], rt[:, 3, :], -2.0, rt[:, 0, :], ALU.mult, ALU.add))
                link(dve.tensor_scalar(rt[:, 6, :], rt[:, 3, :], SCALING, None, ALU.mult))
                link(dve.scalar_tensor_tensor(rt[:, 7, :], rt[:, 5, :], SCALING, rt[:, 6, :], ALU.mult, ALU.subtract))
                link(dve.scalar_tensor_tensor(rt[:, 8, :], rt[:, 3, :], SCALING, rt[:, 0, :], ALU.mult, ALU.mult))
                link(dve.scalar_tensor_tensor(rt[:, 9, :], rt[:, 5, :], SCALING, rt[:, 0, :], ALU.mult, ALU.mult))
                for q in range(4):
                    link(dve.tensor_copy(ex[:, q, :].rearrange("p (e r) -> p e r", r=RANK),
                                         rt[:, 6 + q, :].unsqueeze(2).to_broadcast([P, GROUP * FE, RANK])))
                assert k_vec[0] == R_STEPS
                dve.wait_ge(mk_ready, g + 1)
                dve.wait_ge(ra_done, g + 1)
                for q in range(4):
                    i = dve.tensor_tensor(rf[:, q, :], banks[:, 4 + q // 2, :], mk[:, q % 2, :], ALU.mult)
                i.then_inc(rf_ready, 1)
                dve.wait_ge(rh_ready, g + 1)
                dve.tensor_tensor(rl[:, :, :], rf[:, :, :], f(rh[:, :, :]), ALU.subtract).then_inc(rl_ready, 1)
                chunks(slot)(dve, g)
                dve.wait_ge(down_done, raised(down_done) + CHUNKS * g + CHUNKS)
                for s in range(2):
                    i = dve.tensor_tensor(zf[:, s, :], banks[:, 4 + s, :], mk[:, 2 + s, :], ALU.mult)
                i.then_inc(z_vec, 1)
                dve.wait_ge(z_vec, raised(z_vec) + 2 * g + 1)
                dve.tensor_tensor(zf[:, 0, :], zf[:, 0, :], zf[:, 1, :], ALU.add).then_inc(z_vec, 1)
                dve.wait_ge(zh_ready, g + 1)
                dve.tensor_tensor(zl[:, :], zf[:, 0, :], f(zh[:, :]), ALU.subtract).then_inc(zl_ready, 1)
                dve.wait_ge(fo_done, g + 1)
                for j in range(GROUP):
                    dve.tensor_tensor(xres[:, GROUP * g + j, :], xres[:, GROUP * g + j, :], banks[:, j, :], ALU.add)\
                        .then_inc(xo_ready, 1)


T_GATED = 18
R_STEPS = 25

_OUT = (BATCH, SEQ, DIM)


def kernel(**inputs):
    import numpy as _np
    import concourse.bacc as _bacc
    from concourse import mybir as _mybir
    from concourse.bass_utils import run_bass_kernel_spmd as _run

    def blocks(w):
        return w.reshape(-1, P, w.shape[1]).transpose(1, 0, 2)

    a = {n: _np.asarray(v) for n, v in inputs.items()}
    padded = _np.concatenate([_np.zeros((HEADS, P - 1), _np.float32), a["L0_xattn_ssm_kernel"]], axis=1)
    strips = _np.stack([padded[:, P - 1 - p:P - 1 - p + DIM] for p in range(P)], axis=1)
    r = _np.arange(P)
    same = (r[:, None] % EXPERTS == r[None, :] % EXPERTS)
    earlier = same & (r[:, None] // EXPERTS < r[None, :] // EXPERTS)
    selector = r[:, None] // EXPERTS == _np.arange(8)[None, :]
    ranks = _np.tile(FE - _np.arange(FE), GROUP)[None, :].repeat(P, axis=0)
    consts = _np.concatenate([_np.eye(P), same, earlier, selector, ranks], axis=1).astype(_np.float32)
    bits = _np.tile((1 << _np.arange(BITS - 1, -1, -1)).astype(_np.int32), (P, 1))
    gam = 1.0 - 2.0 ** (-5.0 - _np.arange(RHEADS))
    i = _np.arange(SEQ, dtype=_np.float64)
    expo = i[None, :] - i[:, None]
    dm = _np.where(expo[None] <= 0, gam[:, None, None] ** _np.minimum(expo, 0)[None], 0.0)
    dm = dm / _np.sqrt(dm.sum(axis=-1))[:, None, :] / _np.sqrt(float(P))
    decay = dm.transpose(0, 2, 1).reshape(RHEADS, 2, P, SEQ).transpose(2, 0, 1, 3).reshape(P, RHEADS, 2 * SEQ)
    decay = decay.astype(_np.float32)
    ffg, ffu = (a[n].T.reshape(KB, P, CHUNKS, P).transpose(2, 1, 0, 3).reshape(CHUNKS, P, DIM)
                for n in ("L1_ffn_Wg", "L1_ffn_Wu"))
    bg, bu = (a[n].transpose(0, 2, 1).reshape(P, CHUNKS, P).transpose(1, 0, 2) for n in ("L1_ffn_Bg", "L1_ffn_Bu"))
    wd = a["L1_ffn_Wd"].T.reshape(CHUNKS, P, DIM)
    ad = a["L1_ffn_Ad"].reshape(FE * RANK, CHUNKS, P).transpose(1, 2, 0)
    chunk_w = _np.concatenate([ffg, ffu, bg, bu, wd, ad], axis=2)
    values = [
        ("x", a["x"]), ("ctx", a["ctx_2048"]), ("strips", strips),
        ("d_bc", _np.broadcast_to(a["L0_xattn_D"], (P, HEADS))), ("consts", consts), ("bits", bits),
        ("rw", blocks(a["L0_ffn_router_w"]).reshape(P, -1)),
        ("rb", _np.broadcast_to(a["L0_ffn_router_b"], (P, EXPERTS))),
        ("ew", blocks(a["L0_ffn_expert_w"])), ("eb", _np.broadcast_to(a["L0_ffn_expert_b"], (P, DIM))),
        ("wh", a["L1_xattn_Wh"].transpose(1, 0, 2)), ("decay", decay),
        ("wg", blocks(a["L1_xattn_wg_w"])), ("wo", blocks(a["L1_xattn_wo_w"])),
        ("gb", _np.concatenate([a["L1_xattn_gn_gamma"].reshape(KB, P).T, a["L1_xattn_gn_beta"].reshape(KB, P).T], axis=1)),
        ("wr", blocks(a["L1_ffn_Wr"].T).reshape(P, -1)),
        ("ag", blocks(a["L1_ffn_Ag"].reshape(FE * RANK, DIM).T).reshape(P, -1)),
        ("au", blocks(a["L1_ffn_Au"].reshape(FE * RANK, DIM).T).reshape(P, -1)),
        ("bd", a["L1_ffn_Bd"].transpose(0, 2, 1).reshape(FE * RANK, DIM)),
        ("chunk_w", chunk_w),
    ]
    nc = _bacc.Bacc("TRN2", target_bir_lowering=False, num_devices=1)
    arrays, args = {}, []
    for name, v in values:
        v = _np.ascontiguousarray(v)
        arrays[f"in_{name}"] = v
        args.append(nc.dram_tensor(f"in_{name}", v.shape, _mybir.dt.from_np(v.dtype), kind="ExternalInput").ap())
    args.append(nc.dram_tensor("out_0", _OUT, _mybir.dt.float32, kind="ExternalOutput").ap())
    build(nc, *args)
    res = _run(nc, [arrays], core_ids=[0])
    return res.results[0]["out_0"]
```

```python
from contextlib import ExitStack

import concourse.bass as bass
from concourse import mybir

F32 = mybir.dt.float32
F32R = mybir.dt.float32r
I32 = mybir.dt.int32
ALU = mybir.AluOpType
ACT = mybir.ActivationFunctionType
X_AXIS = mybir.AxisListType.X

P = 128
BATCH, SEQ, DIM = 8, 256, 512
TOKENS = BATCH * SEQ
TILES = TOKENS // P
KB = DIM // P
GROUP = 4
GROUPS = TILES // GROUP
GTOK = GROUP * P
EPS = 1e-5
GN_EPS = 1e-3

HEADS, HD = 32, 8
WRAP = 3
PAIRS = 4 * HD + HD // 2
MB = KB * BATCH

EXPERTS = 16
CAPACITY = TOKENS // EXPERTS
BITS = 30

RHEADS = DIM // P

FE, RANK = 8, 16
DFF = 1408
CHUNKS = DFF // P
SCALING = 2.0
GU_W = 2 * DIM + 2 * P
DN_W = DIM + P


def build(nc, x, ctx_in, strips, d_bc, consts, bits, rw, rb, ew, eb, wh, decay, wg, wo, gb,
          wr, ag, au, bd, chunk_w, out):
    xr = x.rearrange("b (s p) d -> (b s) p d", p=P)
    cr = ctx_in.rearrange("b (s p) d -> (b s) p d", p=P)
    outr = out.rearrange("b (s p) d -> (b s) p d", p=P)

    stack = ExitStack()
    with stack:
        start_of, primed = {}, []

        def sem(name, start=0):
            s = stack.enter_context(nc.semaphore(name))
            if start:
                start_of[s.name] = start
                primed.append((s, start))
            return s

        def sems(name, n, start=0):
            return [sem(f"{name}{i}", start) for i in range(n)]

        def keep(name, shape, dt=F32):
            return stack.enter_context(nc.sbuf_tensor(name, shape, dt))

        banks = stack.enter_context(nc.psum_tensor("banks", [P, 8, 512], F32))

        xres = keep("xres", [P, TILES, DIM])
        cst = keep("cst", [P, 3 * P + 8 + 32])
        ident, same_e, lower_e = (cst[:, i * P:(i + 1) * P] for i in range(3))
        tile_sel = cst[:, 3 * P:3 * P + 8]
        rank8 = cst[:, 3 * P + 8:3 * P + 40]
        mhalf = keep("mhalf", [P, GROUP])
        stat6 = keep("stat6", [P, GROUP, 6])
        mom = keep("mom", [P, GROUP, 2])
        vare = keep("vare", [P, GROUP])
        rstd = keep("rstd", [P, GROUP])
        gate = keep("gate", [P, TILES])
        xn = keep("xn", [P, GROUP, DIM])

        mid = ExitStack()

        def alloc(st, name, shape, dt=F32):
            return st.enter_context(nc.sbuf_tensor(name, shape, dt))

        qt = alloc(mid, "qt", [P, KB * TOKENS])
        ct = alloc(mid, "ct", [P, KB * TOKENS])

        sa = ExitStack()
        cin = alloc(sa, "cin", [P, GROUP, DIM])
        sa.close()
        sc = ExitStack()
        strip = alloc(sc, "strip", [P, 2, DIM])
        dcol = alloc(sc, "dcol", [P, HEADS])
        kx = alloc(sc, "kx", [P, 2, MB * 2 * HD])
        qx = alloc(sc, "qx", [P, 2, MB * 2 * HD])
        kv = alloc(sc, "kv", [P, 2, MB * PAIRS])
        YP_ = 4 * (HD + WRAP) + 4
        yx = alloc(sc, "yx", [P, 2, MB * YP_])
        pr = alloc(sc, "pr", [P, 2, MB * HD * HD])
        sc.close()
        sbk = ExitStack()
        ost = alloc(sbk, "ost", [P, GROUP, DIM])
        xth = alloc(sbk, "xth", [P, GROUP, DIM], F32R)
        xtl = alloc(sbk, "xtl", [P, GROUP, DIM], F32R)
        ewf = alloc(sbk, "ewf", [P, KB, DIM])
        ewh = alloc(sbk, "ewh", [P, KB, DIM], F32R)
        ewl = alloc(sbk, "ewl", [P, KB, DIM], F32R)
        rwf = alloc(sbk, "rwf", [P, KB * EXPERTS])
        rwh = alloc(sbk, "rwh", [P, KB * EXPERTS], F32R)
        rwl = alloc(sbk, "rwl", [P, KB * EXPERTS], F32R)
        rbb = alloc(sbk, "rbb", [P, EXPERTS])
        ebb = alloc(sbk, "ebb", [P, DIM])
        lg = alloc(sbk, "lg", [P, TILES * EXPERTS])
        lsc = alloc(sbk, "lsc", [P, 2 * TILES])
        st_ = alloc(sbk, "st_", [P, 2 * P])
        junk = alloc(sbk, "junk", [P, 2 * P])
        eqs = alloc(sbk, "eqs", [P, 2 * P])
        scan = alloc(sbk, "scan", [P, 2 * P])
        onesr = alloc(sbk, "onesr", [P, P])
        cnt = alloc(sbk, "cnt", [P, 8])
        pre = alloc(sbk, "pre", [P, 4], I32)
        bitc = alloc(sbk, "bitc", [P, BITS], I32)
        sbk.close()
        sd = ExitStack()
        xt = alloc(sd, "xt", [P, KB * TOKENS])
        sd1 = ExitStack()
        dmask = alloc(sd1, "dmask", [P, RHEADS, 2 * SEQ])
        whf = alloc(sd1, "whf", [P, RHEADS, P])
        wht = alloc(sd1, "wht", [P, RHEADS, P])
        whh = alloc(sd1, "whh", [P, RHEADS, P], F32R)
        whl = alloc(sd1, "whl", [P, RHEADS, P], F32R)
        grh = alloc(sd1, "grh", [P, P], F32R)
        grl = alloc(sd1, "grl", [P, P], F32R)
        cch = alloc(sd1, "cch", [P, 2, GTOK], F32R)
        ccl = alloc(sd1, "ccl", [P, 2, GTOK], F32R)
        xxh = alloc(sd1, "xxh", [P, 2, GTOK], F32R)
        xxl = alloc(sd1, "xxl", [P, 2, GTOK], F32R)
        mth = alloc(sd1, "mth", [P, 2, GTOK], F32R)
        mtl = alloc(sd1, "mtl", [P, 2, GTOK], F32R)
        vh = alloc(sd1, "vh", [P, TILES, P], F32R)
        vl = alloc(sd1, "vl", [P, TILES, P], F32R)
        aw = alloc(sd1, "aw", [P, 2 * SEQ])
        ah = alloc(sd1, "ah", [P, 2 * SEQ], F32R)
        al = alloc(sd1, "al", [P, 2 * SEQ], F32R)
        sd1.close()
        mid2 = ExitStack()
        wgf = alloc(mid2, "wgf", [P, KB, DIM])
        wgh = alloc(mid2, "wgh", [P, KB, DIM], F32R)
        wgl = alloc(mid2, "wgl", [P, KB, DIM], F32R)
        woh = alloc(mid2, "woh", [P, KB, DIM], F32R)
        wol = alloc(mid2, "wol", [P, KB, DIM], F32R)
        gbc = alloc(mid2, "gbc", [P, 2 * KB])
        xeh = alloc(mid2, "xeh", [P, KB, GTOK], F32R)
        xel = alloc(mid2, "xel", [P, KB, GTOK], F32R)
        zt = alloc(mid2, "zt", [P, KB, GTOK])
        mid2.close()
        sd.close()
        mid.close()
        so = ExitStack()
        alloc(so, "over_qt", [P, KB * TOKENS])
        uh = alloc(so, "uh", [P, KB, GTOK], F32R)
        ul = alloc(so, "ul", [P, KB, GTOK], F32R)
        wof = alloc(so, "wof", [P, KB, DIM])
        so.close()
        sf = ExitStack()
        wst = alloc(sf, "wst", [P, 2, GU_W + DN_W])
        guh = alloc(sf, "guh", [P, 2, GU_W], F32R)
        gul = alloc(sf, "gul", [P, 2, GU_W], F32R)
        dnh = alloc(sf, "dnh", [P, 2, DN_W], F32R)
        dnl = alloc(sf, "dnl", [P, 2, DN_W], F32R)
        xfh = alloc(sf, "xfh", [P, KB, GTOK], F32R)
        xfl = alloc(sf, "xfl", [P, KB, GTOK], F32R)
        LW = KB * FE + 2 * DIM + DIM
        lwf = alloc(sf, "lwf", [P, LW])
        lwh = alloc(sf, "lwh", [P, LW], F32R)
        lwl = alloc(sf, "lwl", [P, LW], F32R)
        rt = alloc(sf, "rt", [P, 12, GROUP * FE])
        rsm = alloc(sf, "rsm", [P, 6, GROUP])
        ex = alloc(sf, "ex", [P, 4, GTOK])
        mk = alloc(sf, "mk", [P, 4, GTOK])
        rf = alloc(sf, "rf", [P, 4, GTOK])
        rh = alloc(sf, "rh", [P, 4, GTOK], F32R)
        rl = alloc(sf, "rl", [P, 4, GTOK], F32R)
        silu = alloc(sf, "silu", [P, 2, GTOK])
        hf = alloc(sf, "hf", [P, 3, GTOK])
        hh = alloc(sf, "hh", [P, 2, 3, GTOK], F32R)
        hl = alloc(sf, "hl", [P, 2, 3, GTOK], F32R)
        lt = alloc(sf, "lt", [FE, GTOK])
        zf = alloc(sf, "zf", [P, 2, GTOK])
        zh = alloc(sf, "zh", [P, GTOK], F32R)
        zl = alloc(sf, "zl", [P, GTOK], F32R)
        sf.close()

        def f(ap):
            return ap.bitcast(F32)

        def turned(t, tile):
            return t[:, :].rearrange("p (k n) -> p k n", k=KB)[:, :, bass.ts(tile, P)]

        def split(ap):
            return ap.rearrange("p (k n) -> p k n", k=KB)

        def turned_group(t, g):
            return t[:, :].rearrange("p (k n) -> p k n", k=KB)[:, :, bass.ts(g, GTOK)]

        def tile_rows(t, tile):
            return t[:, :].rearrange("p (t n) -> p t n", t=TILES)[:, tile, :]

        def head_cols(t, h):
            return t[:, :].rearrange("p (m c) -> p m c", m=MB)[:, :, bass.ts(h, HD)]

        def view(t, u, offset, dims):
            n = t.shape[2]
            return bass.AP(t[:, :, :].tensor, u * n + offset, [[2 * n, P]] + dims)

        s_const = sem("const_in")
        s_mh = sem("mhalf_set")
        passed = sem("passed")
        ln = {st: {k: sem(f"{st}_{k}", 1 if k == "xn" else 0) for k in ("stats", "var", "rstd", "xn")} for st in "ABCEF"}
        x_in, c_in = sems("x_in", 4, 16), sems("c_in", 4, 16)
        ctx_turned, ct_copied = sem("ctx_turned", GROUP), sem("ct_copied", GROUP)
        xa_turned, qt_copied = sem("xa_turned", GROUP), sem("qt_copied", GROUP)
        d_in = sem("d_in")
        strip_in, strip_ready = sems("strip_in", 2), sems("strip_ready", 2)
        kx_ready, kv_ready = sems("kx_ready", 2), sems("kv_ready", 2, 1)
        conv_done, y_copied = sems("conv_done", 2, 1), sems("y_copied", 2, 1)
        pr_vec, pr_pool, conv_out = sems("pr_vec", 2), sems("pr_pool", 2), sems("conv_out", 2, 1)
        wB_in, wB_high, wB_ready = sem("wB_in"), sem("wB_high"), sem("wB_ready")
        ost_ready, o_turned, x1_ready = sem("ost_ready"), sem("o_turned", GROUP), sem("x1_ready")
        xb_turned, xth_ready, xtl_ready = sem("xb_turned", GROUP), sem("xth_ready", GROUP), sem("xtl_ready", GROUP)
        yw_done, yw_copied = sem("yw_done", GROUP), sem("yw_copied", GROUP)
        t_vec, t_exp, t_pe = sem("t_vec"), sem("t_exp"), sem("t_pe")
        bit_vec, bit_cnt, bit_sum = sem("bit_vec", 1), sem("bit_cnt"), sem("bit_sum")
        x2_ready, xc_turned, xt_copied = sem("x2_ready"), sem("xc_turned", GROUP), sem("xt_copied", GROUP)

        wh_in, whh_ready, whl_ready, wh_turned, wht_ready, g_done = (
            sem(n) for n in ("wh_in", "whh_ready", "whl_ready", "wh_turned", "wht_ready", "g_done"))
        grh_ready, grl_ready, cch_ready, ccl_ready, xxh_ready, xxl_ready = (
            sem(n) for n in ("grh_ready", "grl_ready", "cch_ready", "ccl_ready", "xxh_ready", "xxl_ready"))
        m_done = sem("m_done")
        mv_done, sc_done = sems("mv_done", 2, 1), sems("sc_done", 2, 1)
        mth_ready, vh_ready = sem("mth_ready"), sem("vh_ready")
        mtl_ready, vl_ready = sems("mtl_ready", 2, 1), sems("vl_ready", 2, 1)
        a_read, a_abs, a_ready, ah_ready = sem("a_read", 1), sem("a_abs"), sem("a_ready"), sem("ah_ready")
        al_ready, ao_done = sem("al_ready", 1), sem("ao_done", 1)
        ro_act, ro_vec = sem("ro_act", 1), sem("ro_vec", 1)
        wE_in, wE_high, wE_ready = sem("wE_in"), sem("wE_high"), sem("wE_ready")
        xeh_ready, xel_ready, wt_done = sem("xeh_ready"), sem("xel_ready"), sem("wt_done", 1)
        y_turned, zt_ready, zu_ready, uh_ready = sem("y_turned", GROUP), sem("zt_ready"), sem("zu_ready", 1), sem("uh_ready")
        ul_ready, wo_done, x3_ready = sem("ul_ready", 1), sem("wo_done", 1), sem("x3_ready", 1)
        lw_in, lwh_ready, lwl_ready = sem("lw_in"), sem("lwh_ready"), sem("lwl_ready")
        wst_in = sems("wst_in", 2)
        xf_turned, xfh_ready, xfl_ready = sem("xf_turned", GROUP), sem("xfh_ready"), sem("xfl_ready")
        lgt_done, ra_done, r_vec, r_exp = sem("lgt_done"), sem("ra_done"), sem("r_vec", 1), sem("r_exp")
        mk_turned, mk_ready, rf_ready, rh_ready, rl_ready = (
            sem(n) for n in ("mk_turned", "mk_ready", "rf_ready", "rh_ready", "rl_ready"))
        guh_ready, gul_ready, dnh_ready, dnl_ready = sem("guh_ready"), sem("gul_ready"), sem("dnh_ready"), sem("dnl_ready", 2)
        gate_ready, up_ready, hh_ready = sem("gate_ready"), sem("up_ready", 1), sem("hh_ready")
        silu_done, mul_done = sem("silu_done", 1), sem("mul_done", 1)
        hl_ready, down_done = sems("hl_ready", 3, 1), sem("down_done", 2)
        lt_ready, z_vec, zh_ready, zl_ready = sem("lt_ready"), sem("z_vec", 1), sem("zh_ready"), sem("zl_ready")
        fo_done, xo_ready, out_written = sem("fo_done"), sem("xo_ready", 1), sem("out_written")


        def raised(s):
            return start_of.get(s.name, 0)

        def hold(eng, s, value):
            eng.wait_ge(s, raised(s) + value)
            eng.sem_inc(passed, 1)

        def ln_stats(dve, st, g, src, ready, eps, wait=True):
            s = ln[st]
            dve.wait_ge(s["xn"], raised(s["xn"]) + GROUP * g)
            dve.sem_inc(passed, 1)
            for j in range(GROUP):
                ready(j)
                i = dve.bn_stats(stat6[:, j, :], src(j))
            i.then_inc(s["stats"], 1)
            dve.wait_ge(s["stats"], 2 * g + 1)
            dve.sem_inc(passed, 1)
            for j in range(GROUP):
                i = dve.bn_aggr(mom[:, j, :], stat6[:, j, :])
            i.then_inc(s["stats"], 1)
            dve.wait_ge(s["stats"], 2 * g + 2)
            dve.tensor_scalar(vare[:, :], mom[:, :, 1], eps, None, ALU.add).then_inc(s["var"], 1)
            if wait:
                dve.wait_ge(s["rstd"], g + 1)

        def ln_apply(dve, st, j, src):
            dve.tensor_scalar(xn[:, j, :], src, mom[:, j, 0:1], rstd[:, j:j + 1],
                              ALU.subtract, ALU.mult).then_inc(ln[st]["xn"], 1)

        def ln_rstd(pool, st):
            with pool.Fori(0, GROUPS, 1) as g:
                pool.wait_ge(ln[st]["var"], g + 1)
                pool.tensor_tensor(rstd[:, :], vare[:, :], mhalf[:, :], ALU.pow).then_inc(ln[st]["rstd"], 1)

        def turn(pe, bank, src, signal):
            for k in range(KB):
                i = pe.transpose(banks[:, bank, k * P:(k + 1) * P], src[:, k * P:(k + 1) * P], ident)
            i.then_inc(signal, 1)

        def product(pe, dst, wh_, wl_, mh_, ml_, first, last, check=False):
            pe.matmul(dst, wh_, mh_, start=first, stop=False, skip_group_check=check)
            pe.matmul(dst, wh_, ml_, start=False, stop=False, skip_group_check=check)
            return pe.matmul(dst, wl_, mh_, start=False, stop=last, skip_group_check=check)

        def skewed2(eng, early, late):
            early(0, 0, 0)
            early(1, 0, 1)
            with eng.Fori(0, HEADS // 2 - 1, 1) as i:
                for u in range(2):
                    early(2 * i + 2 + u, i + 1, u)
                    late(2 * i + u, i, u)
            n = HEADS // 2 - 1
            late(2 * n, n, 0)
            late(2 * n + 1, n, 1)

        def skewed(eng, early, late):
            early(0, 0, 0)
            with eng.Fori(0, HEADS // 2 - 1, 1) as i:
                early(2 * i + 1, i, 1)
                late(2 * i, i, 0)
                early(2 * i + 2, i + 1, 0)
                late(2 * i + 1, i, 1)
            n = HEADS // 2 - 1
            early(2 * n + 1, n, 1)
            late(2 * n, n, 0)
            late(2 * n + 1, n, 1)

        def after(eng, ends):
            for s, v in ends:
                eng.wait_ge(s, raised(s) + v)

        def heads(eng, start, first, second, weigh):
            start()
            first(0)
            with eng.Fori(0, RHEADS - 1, 1) as h:
                second(h)
                first(h + 1)
                weigh(h)
            second(RHEADS - 1)
            weigh(RHEADS - 1)

        END_A = [(ct_copied, TILES), (qt_copied, TILES), (xa_turned, TILES)]
        END_CONV = [(conv_out[0], HEADS // 2), (conv_out[1], HEADS // 2)]
        END_B = [(yw_copied, TILES)]
        END_T = [(t_vec, T_GATED + 1)]
        END_C = [(xt_copied, TILES)]

        END_D = [(ro_act, 2 * RHEADS), (ro_vec, 2 * RHEADS)]
        END_E = [(x3_ready, TILES)]

        def batches(t):
            return t.rearrange("p (b t) e -> p b t e", t=2)

        ret_out = qt[:, :].rearrange("p (t n) -> p t n", t=TILES)

        def chunks(slot):
            def run(eng, g):
                slot(g, 0, 0, 0)
                slot(g, 1, 0, 1)
                slot(g, 2, 1, 0)
                with eng.Fori(1, (CHUNKS - 3) // 2, 1) as p:
                    slot(g, 2 * p + 1, p, 1)
                    slot(g, 2 * p + 2, p + 1, 0)
                slot(g, CHUNKS - 2, (CHUNKS - 3) // 2, 1)
                slot(g, CHUNKS - 1, (CHUNKS - 1) // 2, 0)
            return run

        def groups(eng, mid, joint):
            joint(None, 0)
            with eng.Fori(0, GROUPS - 1, 1) as g:
                mid(g, True)
                joint(g, g + 1)
            mid(GROUPS - 1, False)
            joint(GROUPS - 1, None)

        def loads(g, half, u):
            return (6 * g + half + 1) if u == 0 else (5 * g + half + 1)

        block = stack.enter_context(nc.Block())

        @block.sync
        def _(sp):
            sp.dma_start(cst[:, :], consts).then_inc(s_const, 16)
            with sp.Fori(0, GROUPS, 1) as g:
                for j in range(GROUP):
                    sp.wait_ge(c_in[j], raised(c_in[j]) + 16 * g)
                    sp.sem_inc(passed, 1)
                    sp.wait_ge(ctx_turned, raised(ctx_turned) + GROUP * g + j + 1 - GROUP)
                    sp.sem_inc(passed, 1)
                    sp.dma_start(cin[:, j, :], cr[GROUP * g + j]).then_inc(c_in[j], 16)
                    sp.wait_ge(x_in[j], raised(x_in[j]) + 16 * g)
                    sp.sem_inc(passed, 1)
                    sp.dma_start(xres[:, GROUP * g + j, :], xr[GROUP * g + j]).then_inc(x_in[j], 16)
            after(sp, END_A)
            sp.dma_start(dcol[:, :], d_bc).then_inc(d_in, 16)
            with sp.Fori(0, HEADS // 2, 1) as i:
                for u in range(2):
                    sp.wait_ge(conv_done[u], raised(conv_done[u]) + i)
                    sp.sem_inc(passed, 1)
                    sp.dma_start(strip[:, u, :], strips[2 * i + u]).then_inc(strip_in[u], 16)
            after(sp, END_CONV)
            for dst, src in ((ewf[:, :, :], ew), (rwf[:, :], rw), (rbb[:, :], rb), (ebb[:, :], eb), (bitc[:, :], bits)):
                sp.dma_start(dst, src).then_inc(wB_in, 16)
            after(sp, END_C)
            sp.dma_start(whf[:, :, :], wh).then_inc(wh_in, 16)
            sp.dma_start(dmask[:, :, :], decay).then_inc(wh_in, 16)
            after(sp, END_D)
            sp.dma_start(wgf[:, :, :], wg).then_inc(wE_in, 16)
            sp.dma_start(wof[:, :, :], wo).then_inc(wE_in, 16)
            sp.dma_start(gbc[:, :], gb).then_inc(wE_in, 16)
            after(sp, END_E)
            for a, src in ((0, wr), (KB * FE, ag), (KB * FE + DIM, au), (KB * FE + 2 * DIM, bd)):
                sp.dma_start(lwf[:, a:a + src.shape[1]], src).then_inc(lw_in, 16)

            def load(g, c, u):
                n = CHUNKS * g + c
                first = isinstance(c, int) and c == 0
                sp.wait_ge(dnl_ready, raised(dnl_ready) + (n if first else n - 1))
                sp.sem_inc(passed, 1)
                sp.dma_start(wst[:, u, :], chunk_w[c]).then_inc(wst_in[u], 16)

            def slot(g, c, half, u):
                if not isinstance(c, int) or c >= 2:
                    load(g, c, u)

            def mid(g, more):
                chunks(slot)(sp, g)

            def joint(g, nxt):
                if nxt is not None:
                    load(nxt, 0, 0)
                    load(nxt, 1, 1)
                if g is not None:
                    for j in range(GROUP):
                        sp.wait_ge(xo_ready, raised(xo_ready) + GROUP * g + j + 1)
                        sp.sem_inc(passed, 1)
                        sp.dma_start(outr[GROUP * g + j], xres[:, GROUP * g + j, :]).then_inc(out_written, 16)

            groups(sp, mid, joint)
            sp.wait_ge(out_written, 16 * TILES)

        @block.gpsimd
        def _(pool):
            for s, start in primed:
                pool.sem_inc(s, start)
            pool.memset(mhalf[:, :], -0.5).then_inc(s_mh, 1)
            pool.wait_ge(s_mh, 1)
            ln_rstd(pool, "A")
            after(pool, END_A)

            def kv_of(h, n, u):
                pool.wait_ge(kx_ready[u], n + 1)
                pool.wait_ge(conv_done[u], raised(conv_done[u]) + n)
                pool.tensor_tensor(view(kv, u, 0, [[PAIRS, MB], [HD, 4], [1, HD]]),
                                   view(kx, u, 0, [[2 * HD, MB], [0, 4], [1, HD]]),
                                   view(kx, u, 0, [[2 * HD, MB], [1, 4], [1, HD]]), ALU.mult)
                pool.tensor_tensor(view(kv, u, 4 * HD, [[PAIRS, MB], [1, 4]]),
                                   view(kx, u, 0, [[2 * HD, MB], [1, 4]]),
                                   view(kx, u, 4, [[2 * HD, MB], [1, 4]]), ALU.mult).then_inc(kv_ready[u], 1)

            def opposite(h, n, u):
                pool.wait_ge(y_copied[u], raised(y_copied[u]) + n + 1)
                pool.wait_ge(conv_out[u], raised(conv_out[u]) + n)
                pool.tensor_tensor(view(pr, u, 7 * HD, [[HD * HD, MB], [4, 2], [1, 4]]),
                                   view(yx, u, 4 * (HD + WRAP), [[YP_, MB], [0, 2], [1, 4]]),
                                   view(qx, u, 4, [[2 * HD, MB], [-4, 2], [1, 4]]), ALU.mult)\
                    .then_inc(pr_pool[u], 1)

            skewed2(pool, kv_of, opposite)
            after(pool, END_CONV)
            ln_rstd(pool, "B")
            after(pool, END_B)
            ln_rstd(pool, "C")
            pool.wait_ge(wh_in, 32)

            def low(h, q):
                pool.wait_ge(cch_ready, 4 * h + q + 1)
                pool.sem_inc(passed, 1)
                pool.tensor_tensor(ccl[:, q % 2, :], ct[:, bass.ds(h * TOKENS + q * GTOK, GTOK)],
                                   f(cch[:, q % 2, :]), ALU.subtract).then_inc(ccl_ready, 1)

            with pool.Fori(0, RHEADS, 1) as h:
                for q in range(4):
                    low(h, q)
            after(pool, END_D)
            with pool.Fori(0, GROUPS, 1) as g:
                pool.wait_ge(xeh_ready, g + 1)
                pool.sem_inc(passed, 1)
                pool.tensor_tensor(xel[:, :, :], turned_group(xt, g), f(xeh[:, :, :]), ALU.subtract).then_inc(xel_ready, 1)
                pool.wait_ge(ln["E"]["var"], g + 1)
                pool.tensor_tensor(rstd[:, :], vare[:, :], mhalf[:, :], ALU.pow).then_inc(ln["E"]["rstd"], 1)
            after(pool, END_E)

            def cut_gu(g, c, u):
                pool.wait_ge(guh_ready, CHUNKS * g + c + 1)
                pool.tensor_tensor(gul[:, u, :], wst[:, u, 0:GU_W], f(guh[:, u, :]), ALU.subtract).then_inc(gul_ready, 1)

            def slot(g, c, half, u):
                n = CHUNKS * g + c
                pool.wait_ge(dnh_ready, n + 1)
                pool.tensor_tensor(dnl[:, u, :], wst[:, u, GU_W:], f(dnh[:, u, :]), ALU.subtract).then_inc(dnl_ready, 1)
                if not (isinstance(c, int) and c == CHUNKS - 1):
                    cut_gu(g, c + 1, 1 - u)
                for s in range(3):
                    pool.wait_ge(hh_ready, 3 * n + s + 1)
                    pool.tensor_tensor(hl[:, u, s, :], hf[:, s, :], f(hh[:, u, s, :]), ALU.subtract)\
                        .then_inc(hl_ready[s], 1)

            def rstd_f(g):
                pool.wait_ge(ln["F"]["var"], g + 1)
                pool.tensor_tensor(rstd[:, :], vare[:, :], mhalf[:, :], ALU.pow).then_inc(ln["F"]["rstd"], 1)

            def mid(g, more):
                def slots(g, c, half, u):
                    slot(g, c, half, u)
                    if more and isinstance(c, int) and c == 1:
                        rstd_f(g + 1)

                chunks(slots)(pool, g)

            def joint(g, nxt):
                if nxt is not None:
                    cut_gu(nxt, 0, 0)

            rstd_f(0)
            groups(pool, mid, joint)

        @block.scalar
        def _(act):
            with act.Fori(0, GROUPS, 1) as g:
                for j in range(GROUP):
                    act.wait_ge(ctx_turned, raised(ctx_turned) + GROUP * g + j + 1)
                    act.sem_inc(passed, 1)
                    act.activation(turned(ct, GROUP * g + j), split(banks[:, j, :]),
                                   ACT.Copy).then_inc(ct_copied, 1)
            after(act, END_A)

            def doubled(dst, src, h, u):
                for rep in range(2):
                    i = act.activation(view(dst, u, rep * HD, [[2 * HD, MB], [1, HD]]), head_cols(src, h), ACT.Copy)
                return i

            def doubled_k(h, n, u):
                act.wait_ge(kv_ready[u], raised(kv_ready[u]) + n)
                act.sem_inc(passed, 1)
                doubled(kx, ct, h, u).then_inc(kx_ready[u], 1)

            def spread(h, n, u):
                act.wait_ge(conv_out[u], raised(conv_out[u]) + n)
                act.sem_inc(passed, 1)
                doubled(qx, qt, h, u)
                act.wait_ge(conv_done[u], raised(conv_done[u]) + n + 1)
                act.sem_inc(passed, 1)
                y = banks[:, 4 * u:4 * u + 4, :].rearrange("p l (b c) -> p (l b) c", b=BATCH)
                rows = y[:, :, 0:4 * HD].rearrange("p m (d i) -> p m d i", d=4)
                act.activation(view(yx, u, WRAP, [[YP_, MB], [HD + WRAP, 4], [1, HD]]), rows, ACT.Copy)
                act.activation(view(yx, u, HD + WRAP, [[YP_, MB], [HD + WRAP, 3], [1, WRAP]]),
                               rows[:, :, 1:4, HD - WRAP:HD], ACT.Copy)
                act.activation(view(yx, u, 4 * (HD + WRAP), [[YP_, MB], [1, 4]]),
                               y[:, :, 4 * HD:PAIRS], ACT.Copy).then_inc(y_copied[u], 1)

            skewed2(act, doubled_k, spread)
            after(act, END_CONV)
            act.wait_ge(wB_in, 80)
            act.activation(ewh[:, :, :], ewf[:, :, :], ACT.Copy)
            act.activation(rwh[:, :], rwf[:, :], ACT.Copy).then_inc(wB_high, 1)
            with act.Fori(0, GROUPS, 1) as g:
                for j in range(GROUP):
                    act.wait_ge(o_turned, raised(o_turned) + GROUP * g + j + 1 - GROUP)
                    act.sem_inc(passed, 1)
                    act.activation(ost[:, j, :].rearrange("p (k n) -> p k n", k=KB), turned(qt, GROUP * g + j),
                                   ACT.Copy).then_inc(ost_ready, 1)
                for j in range(GROUP):
                    act.wait_ge(xb_turned, raised(xb_turned) + GROUP * g + j + 1)
                    act.sem_inc(passed, 1)
                    act.wait_ge(yw_done, raised(yw_done) + GROUP * g + j + 1 - GROUP)
                    act.sem_inc(passed, 1)
                    act.activation(xth[:, j, :], banks[:, 4 + j, :], ACT.Copy).then_inc(xth_ready, 1)
            act.wait_ge(t_vec, 2)
            act.activation(lg[:, :], lg[:, :], ACT.Exp).then_inc(t_exp, 1)
            with act.Fori(0, GROUPS, 1) as g:
                for j in range(GROUP):
                    act.wait_ge(xc_turned, raised(xc_turned) + GROUP * g + j + 1)
                    act.sem_inc(passed, 1)
                    if j == 0:
                        after(act, END_T)
                    act.activation(turned(xt, GROUP * g + j), split(banks[:, j, :]),
                                   ACT.Copy).then_inc(xt_copied, 1)
            act.wait_ge(wh_in, 32)

            def high(dst, src, used, h, q):
                act.wait_ge(used[q % 2], raised(used[q % 2]) + 2 * h + q // 2)
                act.sem_inc(passed, 1)
                return act.activation(dst[:, q % 2, :], src[:, bass.ds(h * TOKENS + q * GTOK, GTOK)], ACT.Copy)

            def high_c(h, q):
                high(cch, ct, mv_done, h, q).then_inc(cch_ready, 1)

            def high_x(h, q):
                high(xxh, xt, sc_done, h, q).then_inc(xxh_ready, 1)

            def evac_m(h, q):
                act.wait_ge(m_done, 4 * h + q + 1)
                act.wait_ge(sc_done[q % 2], raised(sc_done[q % 2]) + 2 * h + q // 2)
                act.activation(mth[:, q % 2, :], banks[:, q % 2, :], ACT.Copy).then_inc(mth_ready, 1)

            def evac_v(h, q):
                act.wait_ge(mv_done[q % 2], raised(mv_done[q % 2]) + 2 * h + q // 2 + 1)
                act.wait_ge(ao_done, raised(ao_done) + 4 * h)
                act.activation(vh[:, 4 * q:4 * q + 4, :], banks[:, 2 + q % 2, :].rearrange("p (i e) -> p i e", i=4),
                               ACT.Copy).then_inc(vh_ready, 1)

            def start():
                act.activation(whh[:, :, :], whf[:, :, :], ACT.Copy).then_inc(whh_ready, 1)
                act.wait_ge(g_done, 1)

            def first(h):
                act.wait_ge(mv_done[1], raised(mv_done[1]) + 2 * h)
                act.sem_inc(passed, 1)
                act.activation(grh[:, :], banks[:, 7, bass.ts(h, P)], ACT.Copy).then_inc(grh_ready, 1)
                high_c(h, 0)
                high_c(h, 1)
                high_x(h, 0)
                high_x(h, 1)
                if not isinstance(h, int):
                    act.wait_ge(a_ready, h)
                    act.activation(ah[:, :], aw[:, :], ACT.Copy).then_inc(ah_ready, 1)
                evac_m(h, 0)
                evac_m(h, 1)

            def second(h):
                high_c(h, 2)
                high_c(h, 3)
                evac_v(h, 0)
                evac_v(h, 1)
                high_x(h, 2)
                evac_m(h, 2)
                high_x(h, 3)
                evac_m(h, 3)
                evac_v(h, 2)
                evac_v(h, 3)

            def weigh(h):
                if isinstance(h, int):
                    act.wait_ge(a_ready, h + 1)
                    act.activation(ah[:, :], aw[:, :], ACT.Copy).then_inc(ah_ready, 1)
                for half, bank in ((0, 6), (1, 4)):
                    act.wait_ge(ao_done, raised(ao_done) + 4 * h + 2 * half + 1)
                    act.sem_inc(passed, 1)
                    act.activation(batches(ret_out)[:, 0:4, half, bass.ts(h, P)],
                                   banks[:, bank, :].rearrange("p (b e) -> p b e", b=4), ACT.Copy).then_inc(ro_act, 1)

            heads(act, start, first, second, weigh)
            after(act, END_D)
            act.wait_ge(wE_in, 48)
            act.activation(wgh[:, :, :], wgf[:, :, :], ACT.Copy)
            act.activation(woh[:, :, :], wof[:, :, :], ACT.Copy).then_inc(wE_high, 1)
            with act.Fori(0, GROUPS, 1) as g:
                act.wait_ge(wt_done, raised(wt_done) + KB * g)
                act.sem_inc(passed, 1)
                act.activation(xeh[:, :, :], turned_group(xt, g), ACT.Copy).then_inc(xeh_ready, 1)
                act.wait_ge(ul_ready, raised(ul_ready) + g)
                for j in range(GROUP):
                    act.wait_ge(y_turned, raised(y_turned) + GROUP * g + j + 1)
                    for k in range(KB):
                        i = act.activation(zt[:, k, j * P:(j + 1) * P], banks[:, j, k * P:(k + 1) * P], ACT.Identity,
                                           bias=gbc[:, KB + k:KB + k + 1], scale=gbc[:, k:k + 1])
                    i.then_inc(zt_ready, 1)
                act.wait_ge(zu_ready, raised(zu_ready) + KB * g + KB)
                act.wait_ge(wo_done, raised(wo_done) + GROUP * g)
                act.activation(uh[:, :, :], zt[:, :, :], ACT.Copy).then_inc(uh_ready, 1)
            after(act, END_E)
            act.wait_ge(lw_in, 64)
            act.activation(lwh[:, :], lwf[:, :], ACT.Copy).then_inc(lwh_ready, 1)

            def slot(g, c, half, u):
                n = CHUNKS * g + c
                for s in range(3):
                    act.wait_ge(gate_ready, 3 * n + s + 1)
                    act.activation(silu[:, s % 2, :], banks[:, 6, :], ACT.Silu).then_inc(silu_done, 1)
                    act.wait_ge(mul_done, raised(mul_done) + 3 * n + s + 1)
                    act.activation(hh[:, u, s, :], hf[:, s, :], ACT.Copy).then_inc(hh_ready, 1)
                    if s == 1 and isinstance(c, int) and c == 0:
                        for q in range(2, 4):
                            act.wait_ge(mk_turned, 4 * g + q + 1)
                            act.activation(mk[:, q, :], banks[:, q, :], ACT.Copy).then_inc(mk_ready, 1)

            def mid(g, more):
                act.wait_ge(r_vec, raised(r_vec) + R_STEPS * g + 3)
                act.activation(rt[:, 0, :], rt[:, 0, :], ACT.Exp).then_inc(r_exp, 1)
                for q in range(2):
                    act.wait_ge(mk_turned, 4 * g + q + 1)
                    act.activation(mk[:, q, :], banks[:, q, :], ACT.Copy).then_inc(mk_ready, 1)
                for q in range(2):
                    act.wait_ge(rf_ready, 2 * g + q + 1)
                    act.activation(rh[:, q:4:2, :], rf[:, q:4:2, :], ACT.Copy).then_inc(rh_ready, 1)
                chunks(slot)(act, g)

            def joint(g, nxt):
                if nxt is not None:
                    for j in range(GROUP):
                        act.wait_ge(xf_turned, raised(xf_turned) + GROUP * nxt + j + 1)
                        act.activation(xfh[:, :, j * P:(j + 1) * P], split(banks[:, 6 + j % 2, :]), ACT.Copy)\
                            .then_inc(xfh_ready, 1)
                if g is not None:
                    act.wait_ge(z_vec, raised(z_vec) + 2 * g + 2)
                    act.activation(zh[:, :], zf[:, 0, :], ACT.Copy).then_inc(zh_ready, 1)

            groups(act, mid, joint)

        @block.tensor
        def _(pe):
            pe.wait_ge(s_const, 16)
            with pe.Fori(0, GROUPS, 1) as g:
                for j in range(GROUP):
                    pe.wait_ge(c_in[j], raised(c_in[j]) + 16 * (g + 1))
                    pe.wait_ge(ct_copied, raised(ct_copied) + GROUP * g + j + 1 - GROUP)
                    turn(pe, j, cin[:, j, :], ctx_turned)
                for j in range(GROUP):
                    pe.wait_ge(ln["A"]["xn"], raised(ln["A"]["xn"]) + GROUP * g + j + 1)
                    pe.wait_ge(qt_copied, raised(qt_copied) + GROUP * g + j + 1 - GROUP)
                    turn(pe, 4 + j, xn[:, j, :], xa_turned)
            after(pe, END_A)
            with pe.Fori(0, HEADS // 2, 1) as i:
                for u in range(2):
                    pe.wait_ge(strip_ready[u], i + 1)
                    pe.wait_ge(kv_ready[u], raised(kv_ready[u]) + i + 1)
                    pe.wait_ge(y_copied[u], raised(y_copied[u]) + i)
                    for lb in range(KB):
                        dst = banks[:, 4 * u + lb, :].rearrange("p (b c) -> p b c", b=BATCH)[:, :, 0:PAIRS]
                        for m in range(lb + 1):
                            mm = pe.matmul(dst, strip[:, u, (lb - m) * P:(lb - m + 1) * P],
                                           view(kv, u, m * BATCH * PAIRS, [[PAIRS, BATCH], [1, PAIRS]]),
                                           start=m == 0, stop=m == lb)
                    mm.then_inc(conv_done[u], 1)
            after(pe, END_CONV)
            pe.wait_ge(wB_ready, 1)
            with pe.Fori(0, GROUPS, 1) as g:
                for j in range(GROUP):
                    pe.wait_ge(ost_ready, GROUP * g + j + 1)
                    pe.wait_ge(yw_copied, raised(yw_copied) + GROUP * g + j + 1 - GROUP)
                    turn(pe, j, ost[:, j, :], o_turned)
                for j in range(GROUP):
                    pe.wait_ge(ln["B"]["xn"], raised(ln["B"]["xn"]) + GROUP * g + j + 1)
                    turn(pe, 4 + j, xn[:, j, :], xb_turned)
                for j in range(GROUP):
                    pe.wait_ge(xtl_ready, raised(xtl_ready) + GROUP * g + j + 1)
                    for k in range(KB):
                        a, b = k * P, (k + 1) * P
                        product(pe, banks[:, j, :], xth[:, j, a:b], xtl[:, j, a:b], ewh[:, k, :], ewl[:, k, :],
                                k == 0, k == KB - 1)
                    for k in range(KB):
                        a, b = k * P, (k + 1) * P
                        e = slice(k * EXPERTS, (k + 1) * EXPERTS)
                        mm = product(pe, banks[:, 4 + j, 0:EXPERTS], xth[:, j, a:b], xtl[:, j, a:b],
                                     rwh[:, e], rwl[:, e], k == 0, k == KB - 1)
                    mm.then_inc(yw_done, 1)
            pe.wait_ge(t_vec, 5)
            for c in range(2):
                mm = pe.transpose(banks[:, 0, c * P:(c + 1) * P], lg[:, c * P:(c + 1) * P], ident)
            mm.then_inc(t_pe, 1)
            with pe.Fori(0, BITS, 1) as i:
                pe.wait_ge(bit_cnt, i + 1)
                pe.matmul(banks[:, 1, 0:2], same_e, cnt[:, 0:2], start=True, stop=True).then_inc(bit_sum, 1)
            pe.wait_ge(t_vec, 10)
            pe.matmul(banks[:, 2, 0:1], same_e, cnt[:, 2:3], start=True, stop=True)
            pe.matmul(banks[:, 3, 0:1], lower_e, cnt[:, 3:4], start=True, stop=True)
            pe.matmul(banks[:, 4, 0:1], lower_e, cnt[:, 4:5], start=True, stop=False)
            pe.matmul(banks[:, 4, 0:1], same_e, cnt[:, 3:4], start=False, stop=True).then_inc(t_pe, 1)
            pe.wait_ge(t_vec, T_GATED)
            for c in range(2):
                mm = pe.matmul(banks[:, 5, c * 8:(c + 1) * 8], st_[:, c * P:(c + 1) * P], tile_sel,
                               start=True, stop=True)
            mm.then_inc(t_pe, 1)
            with pe.Fori(0, GROUPS, 1) as g:
                for j in range(GROUP):
                    pe.wait_ge(ln["C"]["xn"], raised(ln["C"]["xn"]) + GROUP * g + j + 1)
                    pe.wait_ge(xt_copied, raised(xt_copied) + GROUP * g + j + 1 - GROUP)
                    turn(pe, j, xn[:, j, :], xc_turned)
            def project(h, q):
                u = q % 2
                pe.wait_ge(ccl_ready, 4 * h + q + 1)
                pe.wait_ge(mtl_ready[u], raised(mtl_ready[u]) + 2 * h + q // 2)
                pe.wait_ge(vl_ready[u], raised(vl_ready[u]) + 2 * h + q // 2)
                if q == 0:
                    pe.wait_ge(grl_ready, h + 1)
                product(pe, banks[:, u, :], grh[:, :], grl[:, :], cch[:, u, :], ccl[:, u, :], True, True)\
                    .then_inc(m_done, 1)
                for i in range(4):
                    a, b = i * P, (i + 1) * P
                    mm = product(pe, banks[:, 2 + u, a:b], cch[:, u, a:b], ccl[:, u, a:b],
                                 whh[:, h, :], whl[:, h, :], True, True)
                mm.then_inc(mv_done[u], 1)

            def scores(h, q):
                u = q % 2
                pe.wait_ge(mtl_ready[u], raised(mtl_ready[u]) + 2 * h + q // 2 + 1)
                pe.wait_ge(xxl_ready, 4 * h + q + 1)
                if q == 0:
                    pe.wait_ge(a_read, raised(a_read) + h)
                    pe.wait_ge(ro_act, raised(ro_act) + 2 * h)
                    pe.wait_ge(ro_vec, raised(ro_vec) + 2 * h)
                for b in range(2):
                    o = b * SEQ
                    first, last = q == 0 and b == 0, q == 3 and b == 1
                    product(pe, banks[:, 4, 0:SEQ], mth[:, u, o:o + P], mtl[:, u, o:o + P],
                            xxh[:, u, o:o + SEQ], xxl[:, u, o:o + SEQ], first, last)
                    mm = product(pe, banks[:, 5, 0:SEQ], mth[:, u, o + P:o + SEQ], mtl[:, u, o + P:o + SEQ],
                                 xxh[:, u, o:o + SEQ], xxl[:, u, o:o + SEQ], first, last)
                mm.then_inc(sc_done[u], 1)

            def start():
                pe.wait_ge(wh_in, 32)
                for h in range(RHEADS):
                    mm = pe.transpose(banks[:, 6, h * P:(h + 1) * P], whf[:, h, :], ident)
                mm.then_inc(wh_turned, 1)
                pe.wait_ge(wht_ready, 1)
                for h in range(RHEADS):
                    mm = pe.matmul(banks[:, 7, h * P:(h + 1) * P], wht[:, h, :], wht[:, h, :], start=True, stop=True)
                mm.then_inc(g_done, 1)
                pe.wait_ge(whl_ready, 1)

            def first(h):
                project(h, 0)
                project(h, 1)

            def second(h):
                scores(h, 0)
                scores(h, 1)
                project(h, 2)
                project(h, 3)
                scores(h, 2)
                scores(h, 3)

            def weigh(h):
                pe.wait_ge(al_ready, raised(al_ready) + h + 1)
                pe.wait_ge(vl_ready[0], raised(vl_ready[0]) + 2 * h + 2)
                pe.wait_ge(vl_ready[1], raised(vl_ready[1]) + 2 * h + 2)
                pe.wait_ge(ro_vec, raised(ro_vec) + 2 * h)
                for o, bank in enumerate((6, 5, 4, 6)):
                    half, i = o // 2, o % 2
                    if o == 3:
                        pe.wait_ge(ro_act, raised(ro_act) + 2 * h + 1)
                    for t in range(2):
                        a = t * SEQ + half * P
                        mm = product(pe, banks[:, bank, :].rearrange("p (b e) -> p b e", b=4), ah[:, a:a + P], al[:, a:a + P],
                                     batches(vh[:, :, :])[:, 4 * i:4 * i + 4, t, :],
                                     batches(vl[:, :, :])[:, 4 * i:4 * i + 4, t, :], t == 0, t == 1)
                    mm.then_inc(ao_done, 1)

            heads(pe, start, first, second, weigh)
            after(pe, END_D)
            pe.wait_ge(wE_ready, 1)
            with pe.Fori(0, GROUPS, 1) as g:
                pe.wait_ge(xel_ready, g + 1)
                for jb in range(KB):
                    pe.wait_ge(zu_ready, raised(zu_ready) + KB * g)
                    for k in range(KB):
                        mm = product(pe, banks[:, 4 + jb, :], wgh[:, k, jb * P:(jb + 1) * P], wgl[:, k, jb * P:(jb + 1) * P],
                                     xeh[:, k, :], xel[:, k, :], k == 0, k == KB - 1)
                    mm.then_inc(wt_done, 1)
                for j in range(GROUP):
                    pe.wait_ge(ln["E"]["xn"], raised(ln["E"]["xn"]) + GROUP * g + j + 1)
                    pe.wait_ge(x3_ready, raised(x3_ready) + GROUP * g)
                    turn(pe, j, xn[:, j, :], y_turned)
                pe.wait_ge(ul_ready, raised(ul_ready) + g + 1)
                for j in range(GROUP):
                    for k in range(KB):
                        mm = product(pe, banks[:, j, :], uh[:, k, j * P:(j + 1) * P], ul[:, k, j * P:(j + 1) * P],
                                     woh[:, k, :], wol[:, k, :], k == 0, k == KB - 1)
                    mm.then_inc(wo_done, 1)
            after(pe, END_E)
            R0, A0, U0, B0 = 0, KB * FE, KB * FE + DIM, KB * FE + 2 * DIM
            pe.wait_ge(lwl_ready, 1)

            def turn_masks(g, q):
                pe.wait_ge(r_vec, raised(r_vec) + R_STEPS * g + MASK_STEPS[q])
                for j in range(GROUP):
                    mm = pe.transpose(banks[:, q, j * P:(j + 1) * P], ex[:, q, j * P:(j + 1) * P], ident)
                mm.then_inc(mk_turned, 1)

            def base(g, c, u, between=None):
                n = CHUNKS * g + c
                pe.wait_ge(gul_ready, n + 1)
                for bank, o in ((6, 0), (7, DIM)):
                    if bank == 7 and between:
                        between()
                    if bank == 6:
                        pe.wait_ge(silu_done, raised(silu_done) + 3 * n)
                    else:
                        pe.wait_ge(mul_done, raised(mul_done) + 3 * n)
                    for k in range(KB):
                        a, b = o + k * P, o + (k + 1) * P
                        mm = product(pe, banks[:, bank, :], guh[:, u, a:b], gul[:, u, a:b],
                                     xfh[:, k, :], xfl[:, k, :], k == 0, k == KB - 1)
                    mm.then_inc(gate_ready if bank == 6 else up_ready, 1)

            def lora(g, c, u, s):
                n = CHUNKS * g + c
                pe.wait_ge(silu_done, raised(silu_done) + 3 * n + s + 1)
                product(pe, banks[:, 6, :], guh[:, u, 2 * DIM:2 * DIM + P], gul[:, u, 2 * DIM:2 * DIM + P],
                        rh[:, s, :], rl[:, s, :], False, True, check=True).then_inc(gate_ready, 1)
                pe.wait_ge(mul_done, raised(mul_done) + 3 * n + s + 1)
                product(pe, banks[:, 7, :], guh[:, u, 2 * DIM + P:], gul[:, u, 2 * DIM + P:],
                        rh[:, 2 + s, :], rl[:, 2 + s, :], False, True, check=True).then_inc(up_ready, 1)

            def down(g, c, u, part):
                n = CHUNKS * g + c
                first, last = isinstance(c, int) and c == 0, isinstance(c, int) and c == CHUNKS - 1
                if part < 2:
                    if part == 0:
                        pe.wait_ge(dnl_ready, raised(dnl_ready) + n + 1)
                        pe.wait_ge(hl_ready[0], raised(hl_ready[0]) + n + 1)
                    for j in (2 * part, 2 * part + 1):
                        product(pe, banks[:, j, :], hh[:, u, 0, j * P:(j + 1) * P], hl[:, u, 0, j * P:(j + 1) * P],
                                dnh[:, u, 0:DIM], dnl[:, u, 0:DIM], first, False, check=True)
                    return
                for s in (1, 2):
                    pe.wait_ge(hl_ready[s], raised(hl_ready[s]) + n + 1)
                    mm = product(pe, banks[:, 3 + s, :], dnh[:, u, DIM:], dnl[:, u, DIM:],
                                 hh[:, u, s, :], hl[:, u, s, :], first, last, check=True)
                mm.then_inc(down_done, 1)

            def slot(g, c, half, u):
                if isinstance(c, int) and c == 0:
                    for s in range(2):
                        pe.wait_ge(rl_ready, 2 * g + s + 1)
                        lora(g, c, u, s)
                        if s == 0:
                            for q in range(2, 4):
                                turn_masks(g, q)
                    return
                before = c - 1
                base(g, c, u)
                down(g, before, 1 - u, 0)
                lora(g, c, u, 0)
                down(g, before, 1 - u, 1)
                lora(g, c, u, 1)
                down(g, before, 1 - u, 2)

            def turn_next(g, j):
                pe.wait_ge(ln["F"]["xn"], raised(ln["F"]["xn"]) + GROUP * g + j + 1)
                if j == 0:
                    pe.wait_ge(silu_done, raised(silu_done) + 3 * CHUNKS * g)
                elif j == 1:
                    pe.wait_ge(mul_done, raised(mul_done) + 3 * CHUNKS * g)
                else:
                    pe.wait_ge(xfl_ready, GROUP * g + j - 1)
                turn(pe, 6 + j % 2, xn[:, j, :], xf_turned)

            def mid(g, more):
                chunks(slot)(pe, g)

            def joint(g, nxt):
                if g is not None:
                    down(g, CHUNKS - 1, 0, 0)
                    down(g, CHUNKS - 1, 0, 1)
                if nxt is not None:
                    turn_next(nxt, 0)
                    turn_next(nxt, 1)
                if g is not None:
                    down(g, CHUNKS - 1, 0, 2)
                if nxt is not None:
                    turn_next(nxt, 2)
                    turn_next(nxt, 3)
                    pe.wait_ge(xfl_ready, GROUP * nxt + GROUP)
                    for k in range(KB):
                        r = slice(R0 + k * FE, R0 + (k + 1) * FE)
                        mm = product(pe, banks[0:FE, 6, :], lwh[:, r], lwl[:, r], xfh[:, k, :], xfl[:, k, :],
                                     k == 0, k == KB - 1)
                    mm.then_inc(lgt_done, 1)
                if g is not None:
                    pe.wait_ge(zl_ready, g + 1)
                    for j in range(GROUP):
                        mm = product(pe, banks[:, j, :], zh[:, j * P:(j + 1) * P], zl[:, j * P:(j + 1) * P],
                                     lwh[:, B0:B0 + DIM], lwl[:, B0:B0 + DIM], False, True, check=True)
                        mm.then_inc(fo_done, 1)
                if nxt is None:
                    return

                def lora_a(bank, o):
                    for k in range(KB):
                        mm = product(pe, banks[:, bank, :], lwh[:, o + k * P:o + (k + 1) * P],
                                     lwl[:, o + k * P:o + (k + 1) * P], xfh[:, k, :], xfl[:, k, :], k == 0, k == KB - 1)
                    mm.then_inc(ra_done, 1)

                pe.wait_ge(lt_ready, nxt + 1)
                pe.sem_inc(passed, 1)
                for j in range(GROUP):
                    mm = pe.transpose(banks[:, 7, j * FE:(j + 1) * FE], lt[:, j * P:(j + 1) * P], ident[0:FE, 0:FE])
                mm.then_inc(lgt_done, 1)
                if g is not None:
                    pe.wait_ge(z_vec, raised(z_vec) + 2 * g + 2)
                lora_a(4, A0)
                lora_a(5, U0)

                def masks():
                    for q in range(2):
                        pe.wait_ge(xo_ready, raised(xo_ready) + GROUP * nxt)
                        turn_masks(nxt, q)
                    pe.wait_ge(r_vec, raised(r_vec) + R_STEPS * nxt + 1)

                base(nxt, 0, 0, masks)

            groups(pe, mid, joint)

        @block.vector
        def _(dve):
            dve.wait_ge(s_mh, 1)
            with dve.Fori(0, GROUPS, 1) as g:
                ln_stats(dve, "A", g, lambda j: xres[:, GROUP * g + j, :],
                         lambda j: hold(dve, x_in[j], 16 * (g + 1)), EPS)
                for j in range(GROUP):
                    dve.wait_ge(xa_turned, raised(xa_turned) + GROUP * g + j + 1 - GROUP)
                    ln_apply(dve, "A", j, xres[:, GROUP * g + j, :])
                for j in range(GROUP):
                    dve.wait_ge(xa_turned, raised(xa_turned) + GROUP * g + j + 1)
                    dve.tensor_copy(turned(qt, GROUP * g + j),
                                    banks[:, 4 + j, :].rearrange("p (k n) -> p k n", k=KB)).then_inc(qt_copied, 1)
            after(dve, END_A)
            dve.wait_ge(d_in, 16)

            def diagonal(h, n, u):
                dve.wait_ge(strip_in[u], 16 * (n + 1))
                dve.scalar_tensor_tensor(strip[:, u, 0:P], ident, dcol[:, bass.ds(h, 1)], strip[:, u, 0:P],
                                         ALU.mult, ALU.add).then_inc(strip_ready[u], 1)

            def weigh(h, n, u):
                dve.wait_ge(y_copied[u], raised(y_copied[u]) + n + 1)
                dve.wait_ge(conv_out[u], raised(conv_out[u]) + n)
                dve.tensor_tensor(view(pr, u, 0, [[HD * HD, MB], [HD, 4], [1, HD]]),
                                  view(yx, u, WRAP, [[YP_, MB], [HD + WRAP, 4], [1, HD]]),
                                  view(qx, u, 0, [[2 * HD, MB], [1, 4], [1, HD]]), ALU.mult)
                dve.tensor_tensor(view(pr, u, 4 * HD, [[HD * HD, MB], [HD, 3], [1, HD]]),
                                  view(yx, u, HD + 2 * WRAP - 1, [[YP_, MB], [HD + WRAP - 1, 3], [1, HD]]),
                                  view(qx, u, HD - 1, [[2 * HD, MB], [-1, 3], [1, HD]]), ALU.mult)\
                    .then_inc(pr_vec[u], 1)
                dve.wait_ge(pr_vec[u], n + 1)
                dve.wait_ge(pr_pool[u], n + 1)
                dve.tensor_reduce(head_cols(qt, h), view(pr, u, 0, [[HD * HD, MB], [1, HD], [HD, HD]]),
                                  X_AXIS, ALU.add).then_inc(conv_out[u], 1)

            skewed(dve, diagonal, weigh)
            after(dve, END_CONV)
            dve.wait_ge(wB_high, 1)
            dve.tensor_tensor(ewl[:, :, :], ewf[:, :, :], f(ewh[:, :, :]), ALU.subtract)
            dve.tensor_tensor(rwl[:, :], rwf[:, :], f(rwh[:, :]), ALU.subtract).then_inc(wB_ready, 1)
            with dve.Fori(0, GROUPS, 1) as g:
                for j in range(GROUP):
                    dve.wait_ge(o_turned, raised(o_turned) + GROUP * g + j + 1)
                    dve.tensor_tensor(xres[:, GROUP * g + j, :], xres[:, GROUP * g + j, :], banks[:, j, :],
                                      ALU.add).then_inc(x1_ready, 1)
                ln_stats(dve, "B", g, lambda j: xres[:, GROUP * g + j, :],
                         lambda j: hold(dve, x1_ready, GROUP * g + j + 1), EPS)
                for j in range(GROUP):
                    dve.wait_ge(xb_turned, raised(xb_turned) + GROUP * g + j + 1 - GROUP)
                    ln_apply(dve, "B", j, xres[:, GROUP * g + j, :])
                for j in range(GROUP):
                    dve.wait_ge(xth_ready, raised(xth_ready) + GROUP * g + j + 1)
                    dve.tensor_tensor(xtl[:, j, :], banks[:, 4 + j, :], f(xth[:, j, :]), ALU.subtract)\
                        .then_inc(xtl_ready, 1)
                for j in range(GROUP):
                    dve.wait_ge(yw_done, raised(yw_done) + GROUP * g + j + 1)
                    dve.tensor_tensor(turned(qt, GROUP * g + j), split(banks[:, j, :]), split(ebb[:, :]), ALU.add)
                    dve.tensor_tensor(lg[:, bass.ts(GROUP * g + j, EXPERTS)], banks[:, 4 + j, 0:EXPERTS], rbb[:, :],
                                      ALU.add).then_inc(yw_copied, 1)
            n_vec = [0]

            def step(ins):
                n_vec[0] += 1
                ins.then_inc(t_vec, 1)
                dve.wait_ge(t_vec, n_vec[0])

            lg3 = lg[:, :].rearrange("p (t e) -> p t e", e=EXPERTS)

            def over_experts(ap):
                return ap.unsqueeze(2).to_broadcast([P, TILES, EXPERTS])

            dve.wait_ge(yw_copied, raised(yw_copied) + TILES)
            step(dve.tensor_reduce(lsc[:, 0:TILES], lg3, X_AXIS, ALU.max))
            step(dve.tensor_tensor(lg3, lg3, over_experts(lsc[:, 0:TILES]), ALU.subtract))
            dve.wait_ge(t_exp, 1)
            step(dve.tensor_reduce(lsc[:, TILES:], lg3, X_AXIS, ALU.add))
            step(dve.reciprocal(lsc[:, 0:TILES], lsc[:, TILES:]))
            step(dve.tensor_tensor(lg3, lg3, over_experts(lsc[:, 0:TILES]), ALU.mult))
            dve.memset(onesr[:, :], 1.0)
            dve.memset(cnt[:, :], 0.0)
            step(dve.memset(pre[:, :], 0))
            dve.wait_ge(t_pe, 1)
            step(dve.tensor_copy(st_[:, :], banks[:, 0, 0:2 * P]))
            with dve.Fori(0, BITS, 1) as i:
                bit = bitc[:, bass.ds(i, 1)]
                dve.wait_ge(bit_vec, raised(bit_vec) + 3 * i)
                dve.tensor_tensor(pre[:, 1:2], pre[:, 0:1], bit, ALU.bitwise_or).then_inc(bit_vec, 1)
                dve.wait_ge(bit_vec, raised(bit_vec) + 3 * i + 1)
                dve.tensor_scalar(junk[:, :], st_[:, :], f(pre[:, 1:2]), None, ALU.is_ge, ALU.add,
                                  accum_out=cnt[:, 0:1]).then_inc(bit_cnt, 1)
                dve.wait_ge(bit_sum, i + 1)
                dve.scalar_tensor_tensor(pre[:, 2:3], banks[:, 1, 0:1], CAPACITY - 0.5, bit, ALU.is_ge, ALU.mult)\
                    .then_inc(bit_vec, 1)
                dve.wait_ge(bit_vec, raised(bit_vec) + 3 * i + 2)
                dve.tensor_tensor(pre[:, 0:1], pre[:, 0:1], pre[:, 2:3], ALU.bitwise_or).then_inc(bit_vec, 1)
            dve.wait_ge(bit_vec, raised(bit_vec) + 3 * BITS)
            thr = f(pre[:, 0:1])
            step(dve.tensor_scalar(junk[:, :], st_[:, :], thr, None, ALU.is_gt, ALU.add, accum_out=cnt[:, 2:3]))
            step(dve.tensor_scalar(eqs[:, 0:P], st_[:, 0:P], thr, None, ALU.is_equal, ALU.add, accum_out=cnt[:, 3:4]))
            step(dve.tensor_scalar(eqs[:, P:], st_[:, P:], thr, None, ALU.is_equal, ALU.add, accum_out=cnt[:, 4:5]))
            dve.wait_ge(t_pe, 2)
            step(dve.tensor_scalar(cnt[:, 5:6], banks[:, 2, 0:1], -1.0, float(CAPACITY), ALU.mult, ALU.add))
            step(dve.tensor_copy(cnt[:, 6:7], banks[:, 3, 0:1]))
            step(dve.tensor_copy(cnt[:, 7:8], banks[:, 4, 0:1]))
            for c in range(2):
                step(dve.tensor_tensor_scan(scan[:, c * P:(c + 1) * P], onesr[:, :], eqs[:, c * P:(c + 1) * P],
                                            cnt[:, 6 + c:7 + c], ALU.mult, ALU.add))
            step(dve.scalar_tensor_tensor(scan[:, :], scan[:, :], cnt[:, 5:6], eqs[:, :], ALU.is_le, ALU.mult))
            step(dve.tensor_tensor(scan[:, :], scan[:, :], junk[:, :], ALU.add))
            step(dve.tensor_tensor(st_[:, :], st_[:, :], scan[:, :], ALU.mult))
            assert n_vec[0] == T_GATED
            dve.wait_ge(t_pe, 3)
            step(dve.tensor_copy(gate[:, :], banks[:, 5, 0:TILES]))
            assert n_vec[0] == END_T[0][1]
            with dve.Fori(0, GROUPS, 1) as g:
                for j in range(GROUP):
                    t = GROUP * g + j
                    dve.scalar_tensor_tensor(split(xres[:, t, :]), turned(qt, t), gate[:, bass.ds(t, 1)], split(xres[:, t, :]),
                                             ALU.mult, ALU.add).then_inc(x2_ready, 1)
                ln_stats(dve, "C", g, lambda j: xres[:, GROUP * g + j, :],
                         lambda j: hold(dve, x2_ready, GROUP * g + j + 1), EPS)
                for j in range(GROUP):
                    dve.wait_ge(xc_turned, raised(xc_turned) + GROUP * g + j + 1 - GROUP)
                    ln_apply(dve, "C", j, xres[:, GROUP * g + j, :])
            dve.wait_ge(wh_in, 32)

            def low_x(h, q):
                dve.wait_ge(xxh_ready, 4 * h + q + 1)
                dve.sem_inc(passed, 1)
                dve.tensor_tensor(xxl[:, q % 2, :], xt[:, bass.ds(h * TOKENS + q * GTOK, GTOK)],
                                  f(xxh[:, q % 2, :]), ALU.subtract).then_inc(xxl_ready, 1)

            def low_m(h, q):
                u = q % 2
                dve.wait_ge(mth_ready, 4 * h + q + 1)
                dve.tensor_tensor(mtl[:, u, :], banks[:, u, :], f(mth[:, u, :]), ALU.subtract).then_inc(mtl_ready[u], 1)

            def low_v(h, q):
                u = q % 2
                dve.wait_ge(vh_ready, 4 * h + q + 1)
                dve.tensor_tensor(vl[:, 4 * q:4 * q + 4, :], banks[:, 2 + u, :].rearrange("p (i e) -> p i e", i=4),
                                  f(vh[:, 4 * q:4 * q + 4, :]), ALU.subtract).then_inc(vl_ready[u], 1)

            def floor(h):
                dve.wait_ge(al_ready, raised(al_ready) + h)
                dve.sem_inc(passed, 1)
                for u in range(2):
                    dve.wait_ge(sc_done[u], raised(sc_done[u]) + 2 * h + 2)
                    dve.sem_inc(passed, 1)
                dve.tensor_tensor(aw[:, :].rearrange("p (t s) -> p t s", t=2), banks[:, 4:6, 0:SEQ],
                                  dmask[:, h, :].rearrange("p (t s) -> p t s", t=2), ALU.mult).then_inc(a_read, 1)
                dve.wait_ge(a_read, raised(a_read) + h + 1)
                dve.scalar_tensor_tensor(aw[:, :], aw[:, :], -1.0, aw[:, :], ALU.mult, ALU.max).then_inc(a_abs, 1)
                dve.wait_ge(a_abs, h + 1)
                dve.tensor_scalar(aw[:, :], aw[:, :], 1.0, None, ALU.max).then_inc(a_ready, 1)

            def low_a(h):
                dve.wait_ge(ah_ready, h + 1)
                dve.tensor_tensor(al[:, :], aw[:, :], f(ah[:, :]), ALU.subtract).then_inc(al_ready, 1)

            def start():
                dve.wait_ge(whh_ready, 1)
                dve.tensor_tensor(whl[:, :, :], whf[:, :, :], f(whh[:, :, :]), ALU.subtract).then_inc(whl_ready, 1)
                dve.wait_ge(wh_turned, 1)
                dve.tensor_copy(wht[:, :, :].rearrange("p h e -> p (h e)"), banks[:, 6, :]).then_inc(wht_ready, 1)

            def first(h):
                dve.wait_ge(grh_ready, h + 1)
                dve.sem_inc(passed, 1)
                dve.tensor_tensor(grl[:, :], banks[:, 7, bass.ts(h, P)], f(grh[:, :]), ALU.subtract).then_inc(grl_ready, 1)
                if not isinstance(h, int):
                    floor(h - 1)
                low_x(h, 0)
                low_x(h, 1)
                if not isinstance(h, int):
                    low_a(h - 1)
                low_m(h, 0)
                low_m(h, 1)

            def second(h):
                low_v(h, 0)
                low_v(h, 1)
                low_x(h, 2)
                low_m(h, 2)
                low_x(h, 3)
                low_m(h, 3)
                low_v(h, 2)
                low_v(h, 3)

            def weigh(h):
                if isinstance(h, int):
                    floor(h)
                    low_a(h)
                for half, bank in ((0, 5), (1, 6)):
                    dve.wait_ge(ao_done, raised(ao_done) + 4 * h + 2 * half + 2)
                    dve.sem_inc(passed, 1)
                    dve.tensor_copy(batches(ret_out)[:, 4:8, half, bass.ts(h, P)],
                                    banks[:, bank, :].rearrange("p (b e) -> p b e", b=4)).then_inc(ro_vec, 1)

            heads(dve, start, first, second, weigh)
            after(dve, END_D)
            dve.wait_ge(wE_high, 1)
            dve.tensor_tensor(wgl[:, :, :], wgf[:, :, :], f(wgh[:, :, :]), ALU.subtract)
            dve.tensor_tensor(wol[:, :, :], wof[:, :, :], f(woh[:, :, :]), ALU.subtract).then_inc(wE_ready, 1)
            with dve.Fori(0, GROUPS, 1) as g:
                ln_stats(dve, "E", g, lambda j: tile_rows(qt, GROUP * g + j), lambda j: None, GN_EPS)
                for j in range(GROUP):
                    dve.wait_ge(y_turned, raised(y_turned) + GROUP * g + j + 1 - GROUP)
                    ln_apply(dve, "E", j, tile_rows(qt, GROUP * g + j))
                for jb in range(KB):
                    dve.wait_ge(wt_done, raised(wt_done) + KB * g + jb + 1)
                    dve.wait_ge(zt_ready, GROUP * g + GROUP)
                    dve.scalar_tensor_tensor(zt[:, jb, :], banks[:, 4 + jb, :], 0.0, zt[:, jb, :], ALU.max, ALU.mult)\
                        .then_inc(zu_ready, 1)
                dve.wait_ge(uh_ready, g + 1)
                dve.tensor_tensor(ul[:, :, :], zt[:, :, :], f(uh[:, :, :]), ALU.subtract).then_inc(ul_ready, 1)
                for j in range(GROUP):
                    dve.wait_ge(wo_done, raised(wo_done) + GROUP * g + j + 1)
                    dve.tensor_tensor(xres[:, GROUP * g + j, :], xres[:, GROUP * g + j, :], banks[:, j, :], ALU.add)\
                        .then_inc(x3_ready, 1)
            after(dve, END_E)
            dve.wait_ge(lwh_ready, 1)
            dve.tensor_tensor(lwl[:, :], lwf[:, :], f(lwh[:, :]), ALU.subtract).then_inc(lwl_ready, 1)

            def cut_gu(g, c, half, u, uses):
                dve.wait_ge(wst_in[u], 16 * loads(g, half, u))
                dve.wait_ge(up_ready, raised(up_ready) + uses)
                dve.tensor_copy(guh[:, u, :], wst[:, u, 0:GU_W]).then_inc(guh_ready, 1)

            def slot(g, c, half, u):
                n = CHUNKS * g + c
                first = isinstance(c, int) and c == 0
                dve.wait_ge(down_done, raised(down_done) + (n if first else n - 1))
                dve.tensor_copy(dnh[:, u, :], wst[:, u, GU_W:]).then_inc(dnh_ready, 1)
                for s in range(3):
                    dve.wait_ge(up_ready, raised(up_ready) + 3 * n + s + 1)
                    dve.wait_ge(silu_done, raised(silu_done) + 3 * n + s + 1)
                    dve.wait_ge(hl_ready[s], raised(hl_ready[s]) + n)
                    dve.tensor_tensor(hf[:, s, :], banks[:, 7, :], silu[:, s % 2, :], ALU.mult).then_inc(mul_done, 1)
                    if s == 0 and not (isinstance(c, int) and c == CHUNKS - 1):
                        cut_gu(g, c + 1, half + (1 if u == 1 else 0), 1 - u, 3 * n)

            def norm(g, part):
                if part == 0:
                    ln_stats(dve, "F", g, lambda j: xres[:, GROUP * g + j, :], lambda j: None, EPS, wait=False)
                    return
                dve.wait_ge(ln["F"]["rstd"], g + 1)
                for j in range(GROUP):
                    dve.wait_ge(xf_turned, raised(xf_turned) + GROUP * g + j + 1 - GROUP)
                    ln_apply(dve, "F", j, xres[:, GROUP * g + j, :])

            def router(g):
                k_vec = [0]

                def link(ins):
                    k_vec[0] += 1
                    ins.then_inc(r_vec, 1)
                    dve.wait_ge(r_vec, raised(r_vec) + R_STEPS * g + k_vec[0])

                def by_e(i):
                    return rt[:, i, :].rearrange("p (t e) -> p t e", e=FE)

                def per_token(i):
                    return rsm[:, i, :].unsqueeze(2).to_broadcast([P, GROUP, FE])

                def spread_ranks(q):
                    link(dve.tensor_copy(ex[:, q, :].rearrange("p (e r) -> p e r", r=RANK),
                                         rt[:, 6 + q, :].unsqueeze(2).to_broadcast([P, GROUP * FE, RANK])))
                    assert k_vec[0] == MASK_STEPS[q]

                dve.wait_ge(lgt_done, 2 * g + 2)
                link(dve.tensor_copy(rt[:, 0, :], banks[:, 7, 0:GROUP * FE]))
                link(dve.tensor_reduce(rsm[:, 0, :], by_e(0), X_AXIS, ALU.max))
                link(dve.tensor_tensor(by_e(0), by_e(0), per_token(0), ALU.subtract))
                dve.wait_ge(r_exp, g + 1)
                link(dve.tensor_reduce(rsm[:, 1, :], by_e(0), X_AXIS, ALU.add))
                link(dve.reciprocal(rsm[:, 2, :], rsm[:, 1, :]))
                link(dve.tensor_tensor(by_e(0), by_e(0), per_token(2), ALU.mult))
                for probs, hot in ((0, 3), (4, 5)):
                    link(dve.tensor_reduce(rsm[:, 3, :], by_e(probs), X_AXIS, ALU.max))
                    link(dve.tensor_tensor(by_e(1), by_e(probs), per_token(3), ALU.is_equal))
                    link(dve.tensor_tensor(rt[:, 2, :], rt[:, 1, :], rank8, ALU.mult))
                    link(dve.tensor_reduce(rsm[:, 4, :], by_e(2), X_AXIS, ALU.max))
                    link(dve.tensor_tensor(by_e(hot), by_e(2), per_token(4), ALU.is_equal))
                    if probs == 0:
                        link(dve.scalar_tensor_tensor(rt[:, 4, :], rt[:, 3, :], -2.0, rt[:, 0, :], ALU.mult, ALU.add))
                for q, hot, other, op in ((0, 3, None, None), (1, 5, 6, ALU.subtract), (2, 3, 0, ALU.mult), (3, 5, 0, ALU.mult)):
                    if other is None:
                        link(dve.tensor_scalar(rt[:, 6 + q, :], rt[:, hot, :], SCALING, None, ALU.mult))
                    else:
                        link(dve.scalar_tensor_tensor(rt[:, 6 + q, :], rt[:, hot, :], SCALING, rt[:, other, :], ALU.mult, op))
                    if q < 2:
                        spread_ranks(q)
                for q in range(2):
                    dve.wait_ge(mk_ready, 4 * g + q + 1)
                    dve.wait_ge(ra_done, 2 * g + 2)
                    dve.tensor_tensor(rf[:, q, :], banks[:, 4, :], mk[:, q, :], ALU.mult)
                    dve.tensor_tensor(rf[:, 2 + q, :], banks[:, 5, :], mk[:, q, :], ALU.mult).then_inc(rf_ready, 1)
                for q in range(2):
                    dve.wait_ge(rh_ready, 2 * g + q + 1)
                    dve.tensor_tensor(rl[:, q:4:2, :], rf[:, q:4:2, :], f(rh[:, q:4:2, :]), ALU.subtract)\
                        .then_inc(rl_ready, 1)
                    if q == 0:
                        spread_ranks(2)
                        spread_ranks(3)
                assert k_vec[0] == R_STEPS

            def mid(g, more):
                router(g)

                def slots(g, c, half, u):
                    slot(g, c, half, u)
                    if more and isinstance(c, int) and c in (1, 2):
                        norm(g + 1, c - 1)

                chunks(slots)(dve, g)

            def joint(g, nxt):
                def low(j):
                    dve.wait_ge(xfh_ready, GROUP * nxt + j + 1)
                    dve.tensor_tensor(xfl[:, :, j * P:(j + 1) * P], split(banks[:, 6 + j % 2, :]),
                                      f(xfh[:, :, j * P:(j + 1) * P]), ALU.subtract).then_inc(xfl_ready, 1)

                if nxt is not None:
                    low(0)
                    low(1)
                if g is not None:
                    dve.wait_ge(down_done, raised(down_done) + CHUNKS * g + CHUNKS)
                    dve.wait_ge(mk_ready, 4 * g + 4)
                    for s in range(2):
                        i = dve.tensor_tensor(zf[:, s, :], banks[:, 4 + s, :], mk[:, 2 + s, :], ALU.mult)
                    i.then_inc(z_vec, 1)
                    dve.wait_ge(z_vec, raised(z_vec) + 2 * g + 1)
                    dve.tensor_tensor(zf[:, 0, :], zf[:, 0, :], zf[:, 1, :], ALU.add).then_inc(z_vec, 1)
                if nxt is not None:
                    low(2)
                    low(3)
                if g is not None:
                    dve.wait_ge(zh_ready, g + 1)
                    dve.tensor_tensor(zl[:, :], zf[:, 0, :], f(zh[:, :]), ALU.subtract).then_inc(zl_ready, 1)
                if nxt is not None:
                    dve.wait_ge(lgt_done, 2 * nxt + 1)
                    dve.tensor_copy(lt[:, :], banks[0:FE, 6, :]).then_inc(lt_ready, 1)
                if g is not None:
                    for j in range(GROUP):
                        dve.wait_ge(fo_done, GROUP * g + j + 1)
                        dve.tensor_tensor(xres[:, GROUP * g + j, :], xres[:, GROUP * g + j, :], banks[:, j, :], ALU.add)\
                            .then_inc(xo_ready, 1)
                if nxt is not None:
                    cut_gu(nxt, 0, 0, 0, 3 * CHUNKS * nxt)

            norm(0, 0)
            norm(0, 1)
            groups(dve, mid, joint)


T_GATED = 18
R_STEPS = 25
MASK_STEPS = (19, 21, 24, 25)

_OUT = (BATCH, SEQ, DIM)


def kernel(**inputs):
    import numpy as _np
    import concourse.bacc as _bacc
    from concourse import mybir as _mybir
    from concourse.bass_utils import run_bass_kernel_spmd as _run

    def blocks(w):
        return w.reshape(-1, P, w.shape[1]).transpose(1, 0, 2)

    a = {n: _np.asarray(v) for n, v in inputs.items()}
    padded = _np.concatenate([_np.zeros((HEADS, P - 1), _np.float32), a["L0_xattn_ssm_kernel"]], axis=1)
    strips = _np.stack([padded[:, P - 1 - p:P - 1 - p + DIM] for p in range(P)], axis=1)
    r = _np.arange(P)
    same = (r[:, None] % EXPERTS == r[None, :] % EXPERTS)
    earlier = same & (r[:, None] // EXPERTS < r[None, :] // EXPERTS)
    selector = r[:, None] // EXPERTS == _np.arange(8)[None, :]
    ranks = _np.tile(FE - _np.arange(FE), GROUP)[None, :].repeat(P, axis=0)
    consts = _np.concatenate([_np.eye(P), same, earlier, selector, ranks], axis=1).astype(_np.float32)
    bits = _np.tile((1 << _np.arange(BITS - 1, -1, -1)).astype(_np.int32), (P, 1))
    gam = 1.0 - 2.0 ** (-5.0 - _np.arange(RHEADS))
    i = _np.arange(SEQ, dtype=_np.float64)
    expo = i[None, :] - i[:, None]
    dm = _np.where(expo[None] <= 0, gam[:, None, None] ** _np.minimum(expo, 0)[None], 0.0)
    dm = dm / _np.sqrt(dm.sum(axis=-1))[:, None, :] / _np.sqrt(float(P))
    decay = dm.transpose(0, 2, 1).reshape(RHEADS, 2, P, SEQ).transpose(2, 0, 1, 3).reshape(P, RHEADS, 2 * SEQ)
    decay = decay.astype(_np.float32)
    ffg, ffu = (a[n].T.reshape(KB, P, CHUNKS, P).transpose(2, 1, 0, 3).reshape(CHUNKS, P, DIM)
                for n in ("L1_ffn_Wg", "L1_ffn_Wu"))
    bg, bu = (a[n].transpose(0, 2, 1).reshape(P, CHUNKS, P).transpose(1, 0, 2) for n in ("L1_ffn_Bg", "L1_ffn_Bu"))
    wd = a["L1_ffn_Wd"].T.reshape(CHUNKS, P, DIM)
    ad = a["L1_ffn_Ad"].reshape(FE * RANK, CHUNKS, P).transpose(1, 2, 0)
    chunk_w = _np.concatenate([ffg, ffu, bg, bu, wd, ad], axis=2)
    values = [
        ("x", a["x"]), ("ctx", a["ctx_2048"]), ("strips", strips),
        ("d_bc", _np.broadcast_to(a["L0_xattn_D"], (P, HEADS))), ("consts", consts), ("bits", bits),
        ("rw", blocks(a["L0_ffn_router_w"]).reshape(P, -1)),
        ("rb", _np.broadcast_to(a["L0_ffn_router_b"], (P, EXPERTS))),
        ("ew", blocks(a["L0_ffn_expert_w"])), ("eb", _np.broadcast_to(a["L0_ffn_expert_b"], (P, DIM))),
        ("wh", a["L1_xattn_Wh"].transpose(1, 0, 2)), ("decay", decay),
        ("wg", blocks(a["L1_xattn_wg_w"])), ("wo", blocks(a["L1_xattn_wo_w"])),
        ("gb", _np.concatenate([a["L1_xattn_gn_gamma"].reshape(KB, P).T, a["L1_xattn_gn_beta"].reshape(KB, P).T], axis=1)),
        ("wr", blocks(a["L1_ffn_Wr"].T).reshape(P, -1)),
        ("ag", blocks(a["L1_ffn_Ag"].reshape(FE * RANK, DIM).T).reshape(P, -1)),
        ("au", blocks(a["L1_ffn_Au"].reshape(FE * RANK, DIM).T).reshape(P, -1)),
        ("bd", a["L1_ffn_Bd"].transpose(0, 2, 1).reshape(FE * RANK, DIM)),
        ("chunk_w", chunk_w),
    ]
    nc = _bacc.Bacc("TRN2", target_bir_lowering=False, num_devices=1)
    arrays, args = {}, []
    for name, v in values:
        v = _np.ascontiguousarray(v)
        arrays[f"in_{name}"] = v
        args.append(nc.dram_tensor(f"in_{name}", v.shape, _mybir.dt.from_np(v.dtype), kind="ExternalInput").ap())
    args.append(nc.dram_tensor("out_0", _OUT, _mybir.dt.float32, kind="ExternalOutput").ap())
    build(nc, *args)
    res = _run(nc, [arrays], core_ids=[0])
    return res.results[0]["out_0"]
```

```python
from contextlib import ExitStack

import concourse.bass as bass
from concourse import mybir

F32 = mybir.dt.float32
F32R = mybir.dt.float32r
I32 = mybir.dt.int32
ALU = mybir.AluOpType
ACT = mybir.ActivationFunctionType
X_AXIS = mybir.AxisListType.X

P = 128
BATCH, SEQ, DIM = 8, 256, 512
TOKENS = BATCH * SEQ
TILES = TOKENS // P
KB = DIM // P
GROUP = 4
GROUPS = TILES // GROUP
GTOK = GROUP * P
EPS = 1e-5
GN_EPS = 1e-3

HEADS, HD = 32, 8
WRAP = 3
PAIRS = 4 * HD + HD // 2
MB = KB * BATCH

EXPERTS = 16
CAPACITY = TOKENS // EXPERTS
BITS = 30
STEPS = BITS // 2

RHEADS = DIM // P

FE, RANK = 8, 16
DFF = 1408
CHUNKS = DFF // P
SCALING = 2.0
GU_W = 2 * DIM + 2 * P
DN_W = DIM + P


def build(nc, x, ctx_in, strips, d_bc, consts, bits, rw, rb, ew, eb, wh, decay, wg, wo, gb,
          wr, ag, au, bd, chunk_w, out):
    xr = x.rearrange("b (s p) d -> (b s) p d", p=P)
    cr = ctx_in.rearrange("b (s p) d -> (b s) p d", p=P)
    outr = out.rearrange("b (s p) d -> (b s) p d", p=P)

    stack = ExitStack()
    with stack:
        start_of, primed = {}, []

        def sem(name, start=0):
            s = stack.enter_context(nc.semaphore(name))
            if start:
                start_of[s.name] = start
                primed.append((s, start))
            return s

        def sems(name, n, start=0):
            return [sem(f"{name}{i}", start) for i in range(n)]

        def keep(name, shape, dt=F32):
            return stack.enter_context(nc.sbuf_tensor(name, shape, dt))

        banks = stack.enter_context(nc.psum_tensor("banks", [P, 8, 512], F32))

        xres = keep("xres", [P, TILES, DIM])
        cst = keep("cst", [P, 3 * P + 8 + 32])
        ident, same_e, lower_e = (cst[:, i * P:(i + 1) * P] for i in range(3))
        tile_sel = cst[:, 3 * P:3 * P + 8]
        rank8 = cst[:, 3 * P + 8:3 * P + 40]
        mhalf = keep("mhalf", [P, GROUP])
        stat6 = keep("stat6", [P, GROUP, 6])
        mom = keep("mom", [P, GROUP, 2])
        vare = keep("vare", [P, GROUP])
        rstd = keep("rstd", [P, GROUP])
        gate = keep("gate", [P, TILES])
        xn = keep("xn", [P, GROUP, DIM])

        mid = ExitStack()

        def alloc(st, name, shape, dt=F32):
            return st.enter_context(nc.sbuf_tensor(name, shape, dt))

        qt = alloc(mid, "qt", [P, KB * TOKENS])
        ct = alloc(mid, "ct", [P, KB * TOKENS])

        sa = ExitStack()
        cin = alloc(sa, "cin", [P, GROUP, DIM])
        sa.close()
        sc = ExitStack()
        kx = alloc(sc, "kx", [P, 2, MB * 2 * HD])
        qx = alloc(sc, "qx", [P, 2, MB * 2 * HD])
        strip = alloc(sc, "strip", [P, 2, DIM])
        dcol = alloc(sc, "dcol", [P, HEADS])
        kv = alloc(sc, "kv", [P, 2, MB * PAIRS])
        YP_ = 4 * (HD + WRAP) + 4
        yx = alloc(sc, "yx", [P, 2, MB * YP_])
        pr = alloc(sc, "pr", [P, 2, MB * HD * HD])
        sc.close()
        sbk = ExitStack()
        ost = alloc(sbk, "ost", [P, GROUP, DIM])
        xth = alloc(sbk, "xth", [P, GROUP, DIM], F32R)
        xtl = alloc(sbk, "xtl", [P, GROUP, DIM], F32R)
        lg = alloc(sbk, "lg", [P, TILES * EXPERTS])
        lsc = alloc(sbk, "lsc", [P, 2 * TILES])
        st_ = alloc(sbk, "st_", [P, 2 * P])
        junk = alloc(sbk, "junk", [P, 3, 2 * P])
        eqs = alloc(sbk, "eqs", [P, 2 * P])
        scan = alloc(sbk, "scan", [P, 2 * P])
        onesr = alloc(sbk, "onesr", [P, P])
        cnt = alloc(sbk, "cnt", [P, 8])
        pre = alloc(sbk, "pre", [P, 8], I32)
        met = alloc(sbk, "met", [P, 4])
        over = alloc(sbk, "over", [P, 1])
        CONV_WORDS = 2 * (DIM + 2 * MB * 2 * HD + MB * PAIRS + MB * YP_ + MB * HD * HD) + HEADS
        used = 3 * GROUP * DIM + TILES * EXPERTS + 2 * TILES + 12 * P + P + 8 + 8 + 4 + 1
        alloc(sbk, "above_conv", [P, CONV_WORDS - used])
        bitc = alloc(sbk, "bitc", [P, 3 * STEPS], I32)
        ewf = alloc(sbk, "ewf", [P, KB, DIM])
        ewh = alloc(sbk, "ewh", [P, KB, DIM], F32R)
        ewl = alloc(sbk, "ewl", [P, KB, DIM], F32R)
        rwf = alloc(sbk, "rwf", [P, KB * EXPERTS])
        rwh = alloc(sbk, "rwh", [P, KB * EXPERTS], F32R)
        rwl = alloc(sbk, "rwl", [P, KB * EXPERTS], F32R)
        rbb = alloc(sbk, "rbb", [P, EXPERTS])
        ebb = alloc(sbk, "ebb", [P, DIM])
        sbk.close()
        sd = ExitStack()
        xt = alloc(sd, "xt", [P, KB * TOKENS])
        sd1 = ExitStack()
        dmask = alloc(sd1, "dmask", [P, RHEADS, 2 * SEQ])
        wht = alloc(sd1, "wht", [P, RHEADS, P])
        whh = alloc(sd1, "whh", [P, RHEADS, P], F32R)
        whl = alloc(sd1, "whl", [P, RHEADS, P], F32R)
        grh = alloc(sd1, "grh", [P, P], F32R)
        grl = alloc(sd1, "grl", [P, P], F32R)
        cch = alloc(sd1, "cch", [P, 2, GTOK], F32R)
        ccl = alloc(sd1, "ccl", [P, 2, GTOK], F32R)
        xxh = alloc(sd1, "xxh", [P, 2, GTOK], F32R)
        xxl = alloc(sd1, "xxl", [P, 2, GTOK], F32R)
        mth = alloc(sd1, "mth", [P, 2, GTOK], F32R)
        mtl = alloc(sd1, "mtl", [P, 2, GTOK], F32R)
        vh = alloc(sd1, "vh", [P, TILES, P], F32R)
        vl = alloc(sd1, "vl", [P, TILES, P], F32R)
        aw = alloc(sd1, "aw", [P, 2 * SEQ])
        ah = alloc(sd1, "ah", [P, 2 * SEQ], F32R)
        al = alloc(sd1, "al", [P, 2 * SEQ], F32R)
        whf = alloc(sd1, "whf", [P, RHEADS, P])
        sd1.close()
        mid2 = ExitStack()
        wgh = alloc(mid2, "wgh", [P, KB, DIM], F32R)
        wgl = alloc(mid2, "wgl", [P, KB, DIM], F32R)
        woh = alloc(mid2, "woh", [P, KB, DIM], F32R)
        wol = alloc(mid2, "wol", [P, KB, DIM], F32R)
        gbc = alloc(mid2, "gbc", [P, 2 * KB])
        xeh = alloc(mid2, "xeh", [P, KB, GTOK], F32R)
        xel = alloc(mid2, "xel", [P, KB, GTOK], F32R)
        zt = alloc(mid2, "zt", [P, KB, GTOK])
        mid2.close()
        sd.close()
        mid.close()
        so = ExitStack()
        alloc(so, "over_qt", [P, KB * TOKENS])
        uh = alloc(so, "uh", [P, KB, GTOK], F32R)
        ul = alloc(so, "ul", [P, KB, GTOK], F32R)
        wof = alloc(so, "wof", [P, KB, DIM])
        wgf = alloc(so, "wgf", [P, KB, DIM])
        so.close()
        sf = ExitStack()
        wst = alloc(sf, "wst", [P, 2, GU_W + DN_W])
        guh = alloc(sf, "guh", [P, 2, GU_W], F32R)
        gul = alloc(sf, "gul", [P, 2, GU_W], F32R)
        dnh = alloc(sf, "dnh", [P, 2, DN_W], F32R)
        dnl = alloc(sf, "dnl", [P, 2, DN_W], F32R)
        xfh = alloc(sf, "xfh", [P, KB, GTOK], F32R)
        xfl = alloc(sf, "xfl", [P, KB, GTOK], F32R)
        LW = KB * FE + 2 * DIM + DIM
        lwh = alloc(sf, "lwh", [P, LW], F32R)
        lwl = alloc(sf, "lwl", [P, LW], F32R)
        rt = alloc(sf, "rt", [P, 12, GROUP * FE])
        rsm = alloc(sf, "rsm", [P, 6, GROUP])
        ex = alloc(sf, "ex", [P, 4, GTOK])
        mk = alloc(sf, "mk", [P, 4, GTOK])
        rf = alloc(sf, "rf", [P, 4, GTOK])
        rh = alloc(sf, "rh", [P, 4, GTOK], F32R)
        rl = alloc(sf, "rl", [P, 4, GTOK], F32R)
        silu = alloc(sf, "silu", [P, 2, GTOK])
        hf = alloc(sf, "hf", [P, 3, GTOK])
        hh = alloc(sf, "hh", [P, 2, 3, GTOK], F32R)
        hl = alloc(sf, "hl", [P, 2, 3, GTOK], F32R)
        lt = alloc(sf, "lt", [FE, GTOK])
        zf = alloc(sf, "zf", [P, 2, GTOK])
        zh = alloc(sf, "zh", [P, GTOK], F32R)
        zl = alloc(sf, "zl", [P, GTOK], F32R)
        lwf = alloc(sf, "lwf", [P, LW])
        sf.close()

        def f(ap):
            return ap.bitcast(F32)

        def turned(t, tile):
            return t[:, :].rearrange("p (k n) -> p k n", k=KB)[:, :, bass.ts(tile, P)]

        def split(ap):
            return ap.rearrange("p (k n) -> p k n", k=KB)

        def turned_group(t, g):
            return t[:, :].rearrange("p (k n) -> p k n", k=KB)[:, :, bass.ts(g, GTOK)]

        def tile_rows(t, tile):
            return t[:, :].rearrange("p (t n) -> p t n", t=TILES)[:, tile, :]

        def head_cols(t, h):
            return t[:, :].rearrange("p (m c) -> p m c", m=MB)[:, :, bass.ts(h, HD)]

        def view(t, u, offset, dims):
            n = t.shape[2]
            return bass.AP(t[:, :, :].tensor, u * n + offset, [[2 * n, P]] + dims)

        s_const = sem("const_in")
        s_mh = sem("mhalf_set")
        passed = sem("passed")
        ln = {st: {k: sem(f"{st}_{k}", 1 if k == "xn" else 0) for k in ("stats", "var", "rstd", "xn")} for st in "ABCEF"}
        x_in, c_in = sems("x_in", 4, 16), sems("c_in", 4, 16)
        ctx_turned, ct_copied = sem("ctx_turned", GROUP), sem("ct_copied", GROUP)
        xa_turned, qt_copied = sem("xa_turned", GROUP), sem("qt_copied", GROUP)
        d_in = sem("d_in")
        strip_in, strip_ready = sems("strip_in", 2), sems("strip_ready", 2)
        kx_ready, kv_ready = sems("kx_ready", 2), sems("kv_ready", 2, 1)
        conv_done, y_copied = sems("conv_done", 2, 1), sems("y_copied", 2, 1)
        pr_vec, pr_pool, conv_out = sems("pr_vec", 2), sems("pr_pool", 2), sems("conv_out", 2, 1)
        wB_in, wB_high, wB_ready = sem("wB_in"), sem("wB_high"), sem("wB_ready")
        ost_ready, o_turned, x1_ready = sem("ost_ready"), sem("o_turned", GROUP), sem("x1_ready")
        xb_turned, xth_ready, xtl_ready = sem("xb_turned", GROUP), sem("xth_ready", GROUP), sem("xtl_ready", GROUP)
        yw_done, yw_copied = sem("yw_done", GROUP), sem("yw_copied", GROUP)
        t_vec, t_exp, t_pe = sem("t_vec"), sem("t_exp"), sem("t_pe")
        bit_vec, bit_cnt, bit_sum = sem("bit_vec", 1), sem("bit_cnt"), sem("bit_sum")
        x2_ready, xc_turned, xt_copied = sem("x2_ready"), sem("xc_turned", GROUP), sem("xt_copied", GROUP)

        decay_in = sem("decay_in")
        wh_in, whh_ready, whl_ready, wh_turned, wht_ready, g_done = (
            sem(n) for n in ("wh_in", "whh_ready", "whl_ready", "wh_turned", "wht_ready", "g_done"))
        grh_ready, grl_ready, cch_ready, ccl_ready, xxh_ready, xxl_ready = (
            sem(n) for n in ("grh_ready", "grl_ready", "cch_ready", "ccl_ready", "xxh_ready", "xxl_ready"))
        m_done = sem("m_done")
        mv_done, sc_done = sems("mv_done", 2, 1), sems("sc_done", 2, 1)
        mth_ready, vh_ready = sem("mth_ready"), sem("vh_ready")
        mtl_ready, vl_ready = sems("mtl_ready", 2, 1), sems("vl_ready", 2, 1)
        a_read, a_abs, a_ready, ah_ready = sem("a_read", 1), sem("a_abs"), sem("a_ready"), sem("ah_ready")
        al_ready, ao_done = sem("al_ready", 1), sem("ao_done", 1)
        ro_act, ro_vec = sem("ro_act", 1), sem("ro_vec", 1)
        wg_in, wo_in, wE_high, wE_ready = sem("wg_in"), sem("wo_in"), sem("wE_high"), sem("wE_ready")
        xeh_ready, xel_ready, wt_done = sem("xeh_ready"), sem("xel_ready"), sem("wt_done", 1)
        y_turned, zt_ready, zu_ready, uh_ready = sem("y_turned", GROUP), sem("zt_ready"), sem("zu_ready", 1), sem("uh_ready")
        ul_ready, wo_done, x3_ready = sem("ul_ready", 1), sem("wo_done", GROUP), sem("x3_ready", GROUP)
        lw_in, lwh_ready, lwl_ready = sem("lw_in"), sem("lwh_ready"), sem("lwl_ready")
        wst_in = sems("wst_in", 2)
        xf_turned, xfh_ready, xfl_ready = sem("xf_turned", GROUP), sem("xfh_ready"), sem("xfl_ready")
        lgt_done, ra_done, r_vec, r_exp = sem("lgt_done"), sem("ra_done"), sem("r_vec", 1), sem("r_exp")
        mk_turned, mk_ready, rf_ready, rh_ready, rl_ready = (
            sem(n) for n in ("mk_turned", "mk_ready", "rf_ready", "rh_ready", "rl_ready"))
        guh_ready, gul_ready, dnh_ready, dnl_ready = sem("guh_ready"), sem("gul_ready"), sem("dnh_ready"), sem("dnl_ready", 2)
        gate_ready, up_ready, hh_ready = sem("gate_ready"), sem("up_ready", 1), sem("hh_ready")
        silu_done, mul_done = sem("silu_done", 1), sem("mul_done", 1)
        hl_ready, down_done = sems("hl_ready", 3, 1), sem("down_done", 2)
        lt_ready, z_vec, zh_ready, zl_ready = sem("lt_ready"), sem("z_vec", 1), sem("zh_ready"), sem("zl_ready")
        fo_done, xo_ready, out_written = sem("fo_done"), sem("xo_ready", 1), sem("out_written")

        def raised(s):
            return start_of.get(s.name, 0)

        def hold(eng, s, value):
            eng.wait_ge(s, raised(s) + value)
            eng.sem_inc(passed, 1)

        def ln_stats(dve, st, g, src, ready, eps, wait=True):
            s = ln[st]
            dve.wait_ge(s["xn"], raised(s["xn"]) + GROUP * g)
            dve.sem_inc(passed, 1)
            for j in range(GROUP):
                ready(j)
                i = dve.bn_stats(stat6[:, j, :], src(j))
            i.then_inc(s["stats"], 1)
            dve.wait_ge(s["stats"], 2 * g + 1)
            dve.sem_inc(passed, 1)
            for j in range(GROUP):
                i = dve.bn_aggr(mom[:, j, :], stat6[:, j, :])
            i.then_inc(s["stats"], 1)
            dve.wait_ge(s["stats"], 2 * g + 2)
            dve.tensor_scalar(vare[:, :], mom[:, :, 1], eps, None, ALU.add).then_inc(s["var"], 1)
            if wait:
                dve.wait_ge(s["rstd"], g + 1)

        def ln_apply(dve, st, j, src):
            dve.tensor_scalar(xn[:, j, :], src, mom[:, j, 0:1], rstd[:, j:j + 1],
                              ALU.subtract, ALU.mult).then_inc(ln[st]["xn"], 1)

        def ln_rstd(pool, st):
            with pool.Fori(0, GROUPS, 1) as g:
                pool.wait_ge(ln[st]["var"], g + 1)
                pool.tensor_tensor(rstd[:, :], vare[:, :], mhalf[:, :], ALU.pow).then_inc(ln[st]["rstd"], 1)

        def turn(pe, bank, src, signal):
            for k in range(KB):
                i = pe.transpose(banks[:, bank, k * P:(k + 1) * P], src[:, k * P:(k + 1) * P], ident)
            i.then_inc(signal, 1)

        def product(pe, dst, wh_, wl_, mh_, ml_, first, last, check=False):
            pe.matmul(dst, wh_, mh_, start=first, stop=False, skip_group_check=check)
            pe.matmul(dst, wh_, ml_, start=False, stop=False, skip_group_check=check)
            return pe.matmul(dst, wl_, mh_, start=False, stop=last, skip_group_check=check)

        def skewed(eng, early, late):
            early(0, 0, 0)
            early(1, 0, 1)
            with eng.Fori(0, HEADS // 2 - 1, 1) as i:
                for u in range(2):
                    early(2 * i + 2 + u, i + 1, u)
                    late(2 * i + u, i, u)
            n = HEADS // 2 - 1
            late(2 * n, n, 0)
            late(2 * n + 1, n, 1)

        def after(eng, ends):
            for s, v in ends:
                eng.wait_ge(s, raised(s) + v)

        def heads(eng, start, first, second, weigh):
            start()
            with eng.Fori(0, RHEADS - 1, 1) as h:
                second(h)
                first(h + 1)
                weigh(h)
            second(RHEADS - 1)
            weigh(RHEADS - 1)

        END_A = [(ct_copied, TILES), (qt_copied, TILES), (xa_turned, TILES)]
        END_CONV = [(conv_out[0], HEADS // 2), (conv_out[1], HEADS // 2)]
        END_B = [(yw_copied, TILES)]
        END_T = [(t_vec, T_GATED + 1)]
        END_D = [(ro_act, 2 * RHEADS), (ro_vec, 2 * RHEADS)]
        END_E = [(x3_ready, TILES)]

        def batches(t):
            return t.rearrange("p (b t) e -> p b t e", t=2)

        ret_out = qt[:, :].rearrange("p (t n) -> p t n", t=TILES)

        def choice(eng, norm, mix):
            norm(0)
            with eng.Fori(0, GROUPS - 1, 1) as g:
                mix(g, g + 1)
            mix(GROUPS - 1, None)

        def gated(eng, start, turned_and_gate, out_rows):
            start()
            turned_and_gate(0, True)
            with eng.Fori(1, GROUPS - 1, 1) as g:
                turned_and_gate(g, True)
                out_rows(g - 1)
            turned_and_gate(GROUPS - 1, False)
            out_rows(GROUPS - 2)
            out_rows(GROUPS - 1)

        def chunks(slot):
            def run(eng, g):
                slot(g, 0, 0, 0)
                slot(g, 1, 0, 1)
                slot(g, 2, 1, 0)
                with eng.Fori(1, (CHUNKS - 3) // 2, 1) as p:
                    slot(g, 2 * p + 1, p, 1)
                    slot(g, 2 * p + 2, p + 1, 0)
                slot(g, CHUNKS - 2, (CHUNKS - 3) // 2, 1)
                slot(g, CHUNKS - 1, (CHUNKS - 1) // 2, 0)
            return run

        def groups(eng, mid, joint):
            joint(None, 0)
            with eng.Fori(0, GROUPS - 1, 1) as g:
                mid(g, True)
                joint(g, g + 1)
            mid(GROUPS - 1, False)
            joint(GROUPS - 1, None)

        def loads(g, half, u):
            return ((CHUNKS + 1) // 2 if u == 0 else CHUNKS // 2) * g + half + 1

        block = stack.enter_context(nc.Block())

        @block.sync
        def _(sp):
            sp.dma_start(cst[:, :], consts).then_inc(s_const, 16)
            with sp.Fori(0, GROUPS, 1) as g:
                for j in range(GROUP):
                    sp.wait_ge(c_in[j], raised(c_in[j]) + 16 * g)
                    sp.sem_inc(passed, 1)
                    sp.wait_ge(ctx_turned, raised(ctx_turned) + GROUP * g + j + 1 - GROUP)
                    sp.sem_inc(passed, 1)
                    sp.dma_start(cin[:, j, :], cr[GROUP * g + j]).then_inc(c_in[j], 16)
                    sp.wait_ge(x_in[j], raised(x_in[j]) + 16 * g)
                    sp.sem_inc(passed, 1)
                    sp.dma_start(xres[:, GROUP * g + j, :], xr[GROUP * g + j]).then_inc(x_in[j], 16)
            for dst, src in ((ewf[:, :, :], ew), (rwf[:, :], rw), (rbb[:, :], rb), (ebb[:, :], eb), (bitc[:, :], bits)):
                sp.dma_start(dst, src).then_inc(wB_in, 16)
            sp.dma_start(dcol[:, :], d_bc).then_inc(d_in, 16)
            with sp.Fori(0, HEADS // 2, 1) as i:
                for u in range(2):
                    sp.wait_ge(conv_done[u], raised(conv_done[u]) + i)
                    sp.sem_inc(passed, 1)
                    sp.dma_start(strip[:, u, :], strips[2 * i + u]).then_inc(strip_in[u], 16)
            sp.dma_start(whf[:, :, :], wh).then_inc(wh_in, 16)
            after(sp, END_T)
            sp.dma_start(dmask[:, :, :], decay).then_inc(decay_in, 16)
            sp.wait_ge(ccl_ready, 4 * RHEADS)
            sp.dma_start(wgf[:, :, :], wg).then_inc(wg_in, 16)
            sp.dma_start(wof[:, :, :], wo).then_inc(wo_in, 16)
            after(sp, END_D)
            sp.dma_start(gbc[:, :], gb).then_inc(wo_in, 16)
            for a, src in ((0, wr), (KB * FE, ag), (KB * FE + DIM, au), (KB * FE + 2 * DIM, bd)):
                sp.dma_start(lwf[:, a:a + src.shape[1]], src).then_inc(lw_in, 16)
            after(sp, END_E)

            def load(g, c, u):
                n = CHUNKS * g + c
                first = isinstance(c, int) and c == 0
                sp.wait_ge(dnl_ready, raised(dnl_ready) + (n if first else n - 1))
                sp.sem_inc(passed, 1)
                sp.dma_start(wst[:, u, :], chunk_w[c]).then_inc(wst_in[u], 16)

            def slot(g, c, half, u):
                if not isinstance(c, int) or c >= 2:
                    load(g, c, u)

            def mid(g, more):
                chunks(slot)(sp, g)

            def joint(g, nxt):
                if nxt is not None:
                    load(nxt, 0, 0)
                    load(nxt, 1, 1)
                if g is not None:
                    for j in range(GROUP):
                        sp.wait_ge(xo_ready, raised(xo_ready) + GROUP * g + j + 1)
                        sp.sem_inc(passed, 1)
                        sp.dma_start(outr[GROUP * g + j], xres[:, GROUP * g + j, :]).then_inc(out_written, 16)

            groups(sp, mid, joint)
            sp.wait_ge(out_written, 16 * TILES)

        @block.gpsimd
        def _(pool):
            for s, start in primed:
                pool.sem_inc(s, start)
            pool.memset(mhalf[:, :], -0.5).then_inc(s_mh, 1)
            pool.wait_ge(s_mh, 1)
            ln_rstd(pool, "A")
            after(pool, END_A)

            def kv_of(h, n, u):
                pool.wait_ge(kx_ready[u], n + 1)
                pool.wait_ge(conv_done[u], raised(conv_done[u]) + n)
                pool.tensor_tensor(view(kv, u, 0, [[PAIRS, MB], [HD, 4], [1, HD]]),
                                   view(kx, u, 0, [[2 * HD, MB], [0, 4], [1, HD]]),
                                   view(kx, u, 0, [[2 * HD, MB], [1, 4], [1, HD]]), ALU.mult)
                pool.tensor_tensor(view(kv, u, 4 * HD, [[PAIRS, MB], [1, 4]]),
                                   view(kx, u, 0, [[2 * HD, MB], [1, 4]]),
                                   view(kx, u, 4, [[2 * HD, MB], [1, 4]]), ALU.mult).then_inc(kv_ready[u], 1)

            def opposite(h, n, u):
                pool.wait_ge(y_copied[u], raised(y_copied[u]) + n + 1)
                pool.wait_ge(conv_out[u], raised(conv_out[u]) + n)
                pool.tensor_tensor(view(pr, u, 6 * HD, [[HD * HD, MB], [1, HD]]),
                                   view(yx, u, 3 * (HD + WRAP), [[YP_, MB], [1, HD]]),
                                   view(qx, u, HD - WRAP, [[2 * HD, MB], [1, HD]]), ALU.mult)
                pool.tensor_tensor(view(pr, u, 7 * HD, [[HD * HD, MB], [4, 2], [1, 4]]),
                                   view(yx, u, 4 * (HD + WRAP), [[YP_, MB], [0, 2], [1, 4]]),
                                   view(qx, u, 4, [[2 * HD, MB], [-4, 2], [1, 4]]), ALU.mult)\
                    .then_inc(pr_pool[u], 1)

            skewed(pool, kv_of, opposite)
            after(pool, END_CONV)
            pool.wait_ge(wB_high, 1)
            pool.tensor_tensor(rwl[:, :], rwf[:, :], f(rwh[:, :]), ALU.subtract)
            pool.tensor_tensor(ewl[:, :, :], ewf[:, :, :], f(ewh[:, :, :]), ALU.subtract).then_inc(wB_ready, 1)
            ln_rstd(pool, "B")
            after(pool, END_B)

            def rstd_c(g):
                pool.wait_ge(ln["C"]["var"], g + 1)
                pool.tensor_tensor(rstd[:, :], vare[:, :], mhalf[:, :], ALU.pow).then_inc(ln["C"]["rstd"], 1)


            def low(h, q):
                pool.wait_ge(cch_ready, 4 * h + q + 1)
                pool.sem_inc(passed, 1)
                pool.tensor_tensor(ccl[:, q % 2, :], ct[:, bass.ds(h * TOKENS + q * GTOK, GTOK)],
                                   f(cch[:, q % 2, :]), ALU.subtract).then_inc(ccl_ready, 1)

            rstd_c(0)
            low(0, 0)
            low(0, 1)
            with pool.Fori(1, GROUPS, 1) as g:
                rstd_c(g)
            low(0, 2)
            low(0, 3)
            with pool.Fori(1, RHEADS, 1) as h:
                for q in range(4):
                    low(h, q)
            after(pool, END_D)

            def rstd_e(g):
                pool.wait_ge(ln["E"]["var"], g + 1)
                pool.tensor_tensor(rstd[:, :], vare[:, :], mhalf[:, :], ALU.pow).then_inc(ln["E"]["rstd"], 1)

            def nothing(g):
                pass

            def low_xe(g):
                pool.wait_ge(xeh_ready, g + 1)
                pool.sem_inc(passed, 1)
                pool.tensor_tensor(xel[:, :, :], turned_group(xt, g), f(xeh[:, :, :]), ALU.subtract)\
                    .then_inc(xel_ready, 1)

            def start():
                rstd_e(0)
                low_xe(0)

            def prepare(g, more):
                if more:
                    rstd_e(g + 1)
                    low_xe(g + 1)

            gated(pool, start, prepare, nothing)
            pool.wait_ge(ln["F"]["var"], 1)
            pool.tensor_tensor(rstd[:, :], vare[:, :], mhalf[:, :], ALU.pow).then_inc(ln["F"]["rstd"], 1)
            after(pool, END_E)

            def cut_gu(g, c, u):
                pool.wait_ge(guh_ready, CHUNKS * g + c + 1)
                pool.tensor_tensor(gul[:, u, :], wst[:, u, 0:GU_W], f(guh[:, u, :]), ALU.subtract).then_inc(gul_ready, 1)

            def slot(g, c, half, u):
                n = CHUNKS * g + c
                pool.wait_ge(dnh_ready, n + 1)
                pool.tensor_tensor(dnl[:, u, :], wst[:, u, GU_W:], f(dnh[:, u, :]), ALU.subtract).then_inc(dnl_ready, 1)
                if not (isinstance(c, int) and c == CHUNKS - 1):
                    cut_gu(g, c + 1, 1 - u)
                for s in range(3):
                    pool.wait_ge(hh_ready, 3 * n + s + 1)
                    pool.tensor_tensor(hl[:, u, s, :], hf[:, s, :], f(hh[:, u, s, :]), ALU.subtract)\
                        .then_inc(hl_ready[s], 1)

            def rstd_f(g):
                pool.wait_ge(ln["F"]["var"], g + 1)
                pool.tensor_tensor(rstd[:, :], vare[:, :], mhalf[:, :], ALU.pow).then_inc(ln["F"]["rstd"], 1)

            def mid(g, more):
                def slots(g, c, half, u):
                    slot(g, c, half, u)
                    if more and isinstance(c, int) and c == 1:
                        rstd_f(g + 1)

                chunks(slots)(pool, g)

            def joint(g, nxt):
                if nxt is not None:
                    cut_gu(nxt, 0, 0)

            groups(pool, mid, joint)

        @block.scalar
        def _(act):
            with act.Fori(0, GROUPS, 1) as g:
                for j in range(GROUP):
                    act.wait_ge(ctx_turned, raised(ctx_turned) + GROUP * g + j + 1)
                    act.sem_inc(passed, 1)
                    act.activation(turned(ct, GROUP * g + j), split(banks[:, j, :]),
                                   ACT.Copy).then_inc(ct_copied, 1)
            after(act, END_A)

            def doubled(dst, src, h, u):
                for rep in range(2):
                    i = act.activation(view(dst, u, rep * HD, [[2 * HD, MB], [1, HD]]), head_cols(src, h), ACT.Copy)
                return i

            def doubled_k(h, n, u):
                act.wait_ge(kv_ready[u], raised(kv_ready[u]) + n)
                act.sem_inc(passed, 1)
                doubled(kx, ct, h, u).then_inc(kx_ready[u], 1)

            def spread(h, n, u):
                act.wait_ge(conv_out[u], raised(conv_out[u]) + n)
                act.sem_inc(passed, 1)
                doubled(qx, qt, h, u)
                act.wait_ge(conv_done[u], raised(conv_done[u]) + n + 1)
                act.sem_inc(passed, 1)
                y = banks[:, 4 * u:4 * u + 4, :].rearrange("p l (b c) -> p (l b) c", b=BATCH)
                rows = y[:, :, 0:4 * HD].rearrange("p m (d i) -> p m d i", d=4)
                act.activation(view(yx, u, WRAP, [[YP_, MB], [HD + WRAP, 4], [1, HD]]), rows, ACT.Copy)
                act.activation(view(yx, u, HD + WRAP, [[YP_, MB], [HD + WRAP, 3], [1, WRAP]]),
                               rows[:, :, 1:4, HD - WRAP:HD], ACT.Copy)
                act.activation(view(yx, u, 4 * (HD + WRAP), [[YP_, MB], [1, 4]]),
                               y[:, :, 4 * HD:PAIRS], ACT.Copy).then_inc(y_copied[u], 1)

            skewed(act, doubled_k, spread)
            act.wait_ge(wB_in, 80)
            act.activation(ewh[:, :, :], ewf[:, :, :], ACT.Copy)
            act.activation(rwh[:, :], rwf[:, :], ACT.Copy).then_inc(wB_high, 1)
            after(act, END_CONV)

            def stage(g):
                for j in range(GROUP):
                    act.wait_ge(o_turned, raised(o_turned) + GROUP * g + j + 1 - GROUP)
                    act.sem_inc(passed, 1)
                    act.activation(ost[:, j, :].rearrange("p (k n) -> p k n", k=KB), turned(qt, GROUP * g + j),
                                   ACT.Copy).then_inc(ost_ready, 1)

            def high(g):
                for j in range(GROUP):
                    act.wait_ge(xb_turned, raised(xb_turned) + GROUP * g + j + 1)
                    act.sem_inc(passed, 1)
                    act.wait_ge(yw_done, raised(yw_done) + GROUP * g + j + 1 - GROUP)
                    act.sem_inc(passed, 1)
                    act.activation(xth[:, j, :], banks[:, 6 + j % 2, :], ACT.Copy).then_inc(xth_ready, 1)

            def norm(g):
                stage(g)
                high(g)

            choice(act, norm, lambda g, nxt: norm(nxt) if nxt is not None else None)
            act.wait_ge(t_vec, 2)
            act.activation(lg[:, :], lg[:, :], ACT.Exp).then_inc(t_exp, 1)
            after(act, END_T)

            def keep_turned(g):
                for j in range(GROUP):
                    act.wait_ge(xc_turned, raised(xc_turned) + GROUP * g + j + 1)
                    act.sem_inc(passed, 1)
                    act.activation(turned(xt, GROUP * g + j), split(banks[:, 4 + j % 2, :]),
                                   ACT.Copy).then_inc(xt_copied, 1)

            act.wait_ge(wh_in, 16)

            def high(dst, src, used, h, q):
                act.wait_ge(used[q % 2], raised(used[q % 2]) + 2 * h + q // 2)
                act.sem_inc(passed, 1)
                return act.activation(dst[:, q % 2, :], src[:, bass.ds(h * TOKENS + q * GTOK, GTOK)], ACT.Copy)

            def high_c(h, q):
                high(cch, ct, mv_done, h, q).then_inc(cch_ready, 1)

            def high_x(h, q):
                high(xxh, xt, sc_done, h, q).then_inc(xxh_ready, 1)

            def evac_m(h, q):
                act.wait_ge(m_done, 4 * h + q + 1)
                act.wait_ge(sc_done[q % 2], raised(sc_done[q % 2]) + 2 * h + q // 2)
                act.activation(mth[:, q % 2, :], banks[:, q % 2, :], ACT.Copy).then_inc(mth_ready, 1)

            def evac_v(h, q):
                act.wait_ge(mv_done[q % 2], raised(mv_done[q % 2]) + 2 * h + q // 2 + 1)
                act.wait_ge(ao_done, raised(ao_done) + 4 * h)
                act.activation(vh[:, 4 * q:4 * q + 4, :], banks[:, 2 + q % 2, :].rearrange("p (i e) -> p i e", i=4),
                               ACT.Copy).then_inc(vh_ready, 1)

            def start():
                act.activation(whh[:, :, :], whf[:, :, :], ACT.Copy).then_inc(whh_ready, 1)
                act.wait_ge(g_done, 1)
                high_g(0)
                high_c(0, 0)
                high_c(0, 1)
                keep_turned(0)
                evac_m(0, 0)
                evac_m(0, 1)
                with act.Fori(1, GROUPS, 1) as g:
                    keep_turned(g)
                act.wait_ge(xt_copied, raised(xt_copied) + TILES)
                high_x(0, 0)
                high_x(0, 1)

            def high_g(h):
                act.wait_ge(mv_done[1], raised(mv_done[1]) + 2 * h)
                act.sem_inc(passed, 1)
                act.activation(grh[:, :], banks[:, 7, bass.ts(h, P)], ACT.Copy).then_inc(grh_ready, 1)

            def first(h):
                high_g(h)
                high_c(h, 0)
                high_c(h, 1)
                high_x(h, 0)
                high_x(h, 1)
                act.wait_ge(a_ready, h)
                act.activation(ah[:, :], aw[:, :], ACT.Copy).then_inc(ah_ready, 1)
                evac_m(h, 0)
                evac_m(h, 1)

            def second(h):
                high_c(h, 2)
                high_c(h, 3)
                evac_v(h, 0)
                evac_v(h, 1)
                high_x(h, 2)
                evac_m(h, 2)
                high_x(h, 3)
                evac_m(h, 3)
                evac_v(h, 2)
                evac_v(h, 3)

            def weigh(h):
                if isinstance(h, int):
                    act.wait_ge(a_ready, h + 1)
                    act.activation(ah[:, :], aw[:, :], ACT.Copy).then_inc(ah_ready, 1)
                for half, bank in ((0, 6), (1, 4)):
                    act.wait_ge(ao_done, raised(ao_done) + 4 * h + 2 * half + 1)
                    act.sem_inc(passed, 1)
                    act.activation(batches(ret_out)[:, 0:4, half, bass.ts(h, P)],
                                   banks[:, bank, :].rearrange("p (b e) -> p b e", b=4), ACT.Copy).then_inc(ro_act, 1)

            heads(act, start, first, second, weigh)
            after(act, END_D)
            def high_x(g):
                act.wait_ge(wt_done, raised(wt_done) + KB * g)
                act.sem_inc(passed, 1)
                act.activation(xeh[:, :, :], turned_group(xt, g), ACT.Copy).then_inc(xeh_ready, 1)

            def start():
                act.wait_ge(wg_in, 16)
                act.activation(wgh[:, :, :], wgf[:, :, :], ACT.Copy).then_inc(wE_high, 1)
                high_x(0)
                act.wait_ge(wo_in, 32)
                act.activation(woh[:, :, :], wof[:, :, :], ACT.Copy).then_inc(wE_high, 1)

            def scaled(g, more):
                act.wait_ge(ul_ready, raised(ul_ready) + GROUP * g)
                for j in range(GROUP):
                    act.wait_ge(y_turned, raised(y_turned) + GROUP * g + j + 1)
                    for k in range(KB):
                        i = act.activation(zt[:, k, j * P:(j + 1) * P], banks[:, j, k * P:(k + 1) * P], ACT.Identity,
                                           bias=gbc[:, KB + k:KB + k + 1], scale=gbc[:, k:k + 1])
                    i.then_inc(zt_ready, 1)
                if more:
                    high_x(g + 1)
                if isinstance(g, int) and g == 0:
                    high_u(0)

            def high_u(g):
                act.wait_ge(zu_ready, raised(zu_ready) + KB * g + KB)
                for j in range(GROUP):
                    a, b = j * P, (j + 1) * P
                    act.wait_ge(wo_done, raised(wo_done) + GROUP * g + j + 1 - GROUP)
                    act.activation(uh[:, :, a:b], zt[:, :, a:b], ACT.Copy).then_inc(uh_ready, 1)

            def out_rows(g):
                if not isinstance(g, int) or g < GROUPS - 1:
                    high_u(g + 1)

            gated(act, start, scaled, out_rows)
            after(act, END_E)
            act.wait_ge(lw_in, 64)
            act.activation(lwh[:, :], lwf[:, :], ACT.Copy).then_inc(lwh_ready, 1)

            def slot(g, c, half, u):
                n = CHUNKS * g + c
                for s in range(3):
                    act.wait_ge(gate_ready, 3 * n + s + 1)
                    act.activation(silu[:, s % 2, :], banks[:, 6, :], ACT.Silu).then_inc(silu_done, 1)
                    act.wait_ge(mul_done, raised(mul_done) + 3 * n + s + 1)
                    act.activation(hh[:, u, s, :], hf[:, s, :], ACT.Copy).then_inc(hh_ready, 1)
                    if s == 1 and isinstance(c, int) and c == 0:
                        for q in range(2, 4):
                            act.wait_ge(mk_turned, 4 * g + q + 1)
                            act.activation(mk[:, q, :], banks[:, q, :], ACT.Copy).then_inc(mk_ready, 1)

            def mid(g, more):
                act.wait_ge(r_vec, raised(r_vec) + R_STEPS * g + 3)
                act.activation(rt[:, 0, :], rt[:, 0, :], ACT.Exp).then_inc(r_exp, 1)
                for q in range(2):
                    act.wait_ge(mk_turned, 4 * g + q + 1)
                    act.activation(mk[:, q, :], banks[:, q, :], ACT.Copy).then_inc(mk_ready, 1)
                for q in range(2):
                    act.wait_ge(rf_ready, 2 * g + q + 1)
                    act.activation(rh[:, q:4:2, :], rf[:, q:4:2, :], ACT.Copy).then_inc(rh_ready, 1)
                chunks(slot)(act, g)

            def joint(g, nxt):
                if nxt is not None:
                    for j in range(GROUP):
                        act.wait_ge(xf_turned, raised(xf_turned) + GROUP * nxt + j + 1)
                        act.activation(xfh[:, :, j * P:(j + 1) * P], split(banks[:, 6 + j % 2, :]), ACT.Copy)\
                            .then_inc(xfh_ready, 1)
                if g is not None:
                    act.wait_ge(z_vec, raised(z_vec) + 2 * g + 2)
                    act.activation(zh[:, :], zf[:, 0, :], ACT.Copy).then_inc(zh_ready, 1)

            groups(act, mid, joint)

        @block.tensor
        def _(pe):
            pe.wait_ge(s_const, 16)
            with pe.Fori(0, GROUPS, 1) as g:
                for j in range(GROUP):
                    pe.wait_ge(c_in[j], raised(c_in[j]) + 16 * (g + 1))
                    pe.wait_ge(ct_copied, raised(ct_copied) + GROUP * g + j + 1 - GROUP)
                    turn(pe, j, cin[:, j, :], ctx_turned)
                for j in range(GROUP):
                    pe.wait_ge(ln["A"]["xn"], raised(ln["A"]["xn"]) + GROUP * g + j + 1)
                    pe.wait_ge(qt_copied, raised(qt_copied) + GROUP * g + j + 1 - GROUP)
                    turn(pe, 4 + j, xn[:, j, :], xa_turned)
            after(pe, END_A)
            with pe.Fori(0, HEADS // 2, 1) as i:
                for u in range(2):
                    pe.wait_ge(strip_ready[u], i + 1)
                    pe.wait_ge(kv_ready[u], raised(kv_ready[u]) + i + 1)
                    pe.wait_ge(y_copied[u], raised(y_copied[u]) + i)
                    for lb in range(KB):
                        dst = banks[:, 4 * u + lb, :].rearrange("p (b c) -> p b c", b=BATCH)[:, :, 0:PAIRS]
                        for m in range(lb + 1):
                            mm = pe.matmul(dst, strip[:, u, (lb - m) * P:(lb - m + 1) * P],
                                           view(kv, u, m * BATCH * PAIRS, [[PAIRS, BATCH], [1, PAIRS]]),
                                           start=m == 0, stop=m == lb)
                    mm.then_inc(conv_done[u], 1)
            after(pe, END_CONV)
            def turn_o(g, j):
                pe.wait_ge(ost_ready, GROUP * g + j + 1)
                if j == 0:
                    pe.wait_ge(xtl_ready, raised(xtl_ready) + GROUP * g)
                if j >= 2:
                    pe.wait_ge(x1_ready, GROUP * g + j - 1)
                turn(pe, 6 + j % 2, ost[:, j, :], o_turned)

            def turn_x(g):
                for j in range(GROUP):
                    pe.wait_ge(ln["B"]["xn"], raised(ln["B"]["xn"]) + GROUP * g + j + 1)
                    if j >= 2:
                        pe.wait_ge(xtl_ready, raised(xtl_ready) + GROUP * g + j - 1)
                    turn(pe, 6 + j % 2, xn[:, j, :], xb_turned)

            def mixed(g, j):
                pe.wait_ge(xtl_ready, raised(xtl_ready) + GROUP * g + j + 1)
                pe.wait_ge(yw_copied, raised(yw_copied) + GROUP * g + j - 1)
                for k in range(KB):
                    a, b = k * P, (k + 1) * P
                    product(pe, banks[:, j, :], xth[:, j, a:b], xtl[:, j, a:b], ewh[:, k, :], ewl[:, k, :],
                            k == 0, k == KB - 1)
                for k in range(KB):
                    a, b = k * P, (k + 1) * P
                    e = slice(k * EXPERTS, (k + 1) * EXPERTS)
                    mm = product(pe, banks[:, 4 + j % 2, 0:EXPERTS], xth[:, j, a:b], xtl[:, j, a:b],
                                 rwh[:, e], rwl[:, e], k == 0, k == KB - 1)
                mm.then_inc(yw_done, 1)

            def norm(g):
                for j in range(GROUP):
                    turn_o(g, j)
                turn_x(g)
                pe.wait_ge(wB_ready, 1)

            def mix(g, nxt):
                for j in range(GROUP):
                    mixed(g, j)
                    if nxt is not None and j < 2:
                        turn_o(nxt, 2 * j)
                        turn_o(nxt, 2 * j + 1)
                if nxt is not None:
                    turn_x(nxt)

            choice(pe, norm, mix)
            pe.wait_ge(t_vec, 5)
            for c in range(2):
                mm = pe.transpose(banks[:, 0, c * P:(c + 1) * P], lg[:, c * P:(c + 1) * P], ident)
            mm.then_inc(t_pe, 1)
            with pe.Fori(0, STEPS, 1) as i:
                pe.wait_ge(bit_cnt, i + 1)
                pe.matmul(banks[:, 1, 0:4], same_e, cnt[:, 4:8], start=True, stop=True).then_inc(bit_sum, 1)
            pe.wait_ge(t_vec, 10)
            pe.matmul(banks[:, 2, 0:1], same_e, cnt[:, 2:3], start=True, stop=True)
            pe.matmul(banks[:, 3, 0:1], lower_e, cnt[:, 3:4], start=True, stop=True)
            pe.matmul(banks[:, 4, 0:1], lower_e, cnt[:, 4:5], start=True, stop=False)
            pe.matmul(banks[:, 4, 0:1], same_e, cnt[:, 3:4], start=False, stop=True).then_inc(t_pe, 1)
            pe.wait_ge(t_vec, T_GATED)
            for c in range(2):
                mm = pe.matmul(banks[:, 5, c * 8:(c + 1) * 8], st_[:, c * P:(c + 1) * P], tile_sel,
                               start=True, stop=True)
            mm.then_inc(t_pe, 1)

            def turn_c(g):
                for j in range(GROUP):
                    pe.wait_ge(ln["C"]["xn"], raised(ln["C"]["xn"]) + GROUP * g + j + 1)
                    pe.wait_ge(xt_copied, raised(xt_copied) + GROUP * g + j - 1)
                    turn(pe, 4 + j % 2, xn[:, j, :], xc_turned)

            def project(h, q):
                u = q % 2
                pe.wait_ge(ccl_ready, 4 * h + q + 1)
                pe.wait_ge(mtl_ready[u], raised(mtl_ready[u]) + 2 * h + q // 2)
                pe.wait_ge(vl_ready[u], raised(vl_ready[u]) + 2 * h + q // 2)
                if q == 0:
                    pe.wait_ge(grl_ready, h + 1)
                product(pe, banks[:, u, :], grh[:, :], grl[:, :], cch[:, u, :], ccl[:, u, :], True, True)\
                    .then_inc(m_done, 1)
                for i in range(4):
                    a, b = i * P, (i + 1) * P
                    mm = product(pe, banks[:, 2 + u, a:b], cch[:, u, a:b], ccl[:, u, a:b],
                                 whh[:, h, :], whl[:, h, :], True, True)
                mm.then_inc(mv_done[u], 1)

            def scores(h, q):
                u = q % 2
                pe.wait_ge(mtl_ready[u], raised(mtl_ready[u]) + 2 * h + q // 2 + 1)
                pe.wait_ge(xxl_ready, 4 * h + q + 1)
                if q == 0:
                    pe.wait_ge(a_read, raised(a_read) + h)
                    pe.wait_ge(ro_act, raised(ro_act) + 2 * h)
                    pe.wait_ge(ro_vec, raised(ro_vec) + 2 * h)
                for b in range(2):
                    o = b * SEQ
                    first, last = q == 0 and b == 0, q == 3 and b == 1
                    product(pe, banks[:, 4, 0:SEQ], mth[:, u, o:o + P], mtl[:, u, o:o + P],
                            xxh[:, u, o:o + SEQ], xxl[:, u, o:o + SEQ], first, last)
                    mm = product(pe, banks[:, 5, 0:SEQ], mth[:, u, o + P:o + SEQ], mtl[:, u, o + P:o + SEQ],
                                 xxh[:, u, o:o + SEQ], xxl[:, u, o:o + SEQ], first, last)
                mm.then_inc(sc_done[u], 1)

            def start():
                pe.wait_ge(wh_in, 16)
                for h in range(RHEADS):
                    mm = pe.transpose(banks[:, 6, h * P:(h + 1) * P], whf[:, h, :], ident)
                mm.then_inc(wh_turned, 1)
                pe.wait_ge(wht_ready, 1)
                for h in range(RHEADS):
                    mm = pe.matmul(banks[:, 7, h * P:(h + 1) * P], wht[:, h, :], wht[:, h, :], start=True, stop=True)
                mm.then_inc(g_done, 1)
                pe.wait_ge(whl_ready, 1)
                turn_c(0)
                first(0)
                with pe.Fori(1, GROUPS, 1) as g:
                    turn_c(g)

            def first(h):
                project(h, 0)
                project(h, 1)

            def second(h):
                scores(h, 0)
                scores(h, 1)
                project(h, 2)
                project(h, 3)
                scores(h, 2)
                scores(h, 3)

            def weigh(h):
                pe.wait_ge(al_ready, raised(al_ready) + h + 1)
                pe.wait_ge(vl_ready[0], raised(vl_ready[0]) + 2 * h + 2)
                pe.wait_ge(vl_ready[1], raised(vl_ready[1]) + 2 * h + 2)
                pe.wait_ge(ro_vec, raised(ro_vec) + 2 * h)
                for o, bank in enumerate((6, 5, 4, 6)):
                    half, i = o // 2, o % 2
                    if o == 3:
                        pe.wait_ge(ro_act, raised(ro_act) + 2 * h + 1)
                    for t in range(2):
                        a = t * SEQ + half * P
                        mm = product(pe, banks[:, bank, :].rearrange("p (b e) -> p b e", b=4), ah[:, a:a + P], al[:, a:a + P],
                                     batches(vh[:, :, :])[:, 4 * i:4 * i + 4, t, :],
                                     batches(vl[:, :, :])[:, 4 * i:4 * i + 4, t, :], t == 0, t == 1)
                    mm.then_inc(ao_done, 1)

            heads(pe, start, first, second, weigh)
            after(pe, END_D)
            def turned_and_gate(g, more):
                for j in range(GROUP):
                    pe.wait_ge(ln["E"]["xn"], raised(ln["E"]["xn"]) + GROUP * g + j + 1)
                    if not isinstance(g, int) or g > 0:
                        pe.wait_ge(zt_ready, GROUP * (g - 1) + j + 1)
                        pe.wait_ge(x3_ready, raised(x3_ready) + GROUP * (g - 2) + j + 1)
                    turn(pe, j, xn[:, j, :], y_turned)
                pe.wait_ge(wE_ready, 1)
                pe.wait_ge(xel_ready, g + 1)
                for jb in range(KB):
                    pe.wait_ge(zu_ready, raised(zu_ready) + KB * g)
                    for k in range(KB):
                        mm = product(pe, banks[:, 4 + jb, :], wgh[:, k, jb * P:(jb + 1) * P], wgl[:, k, jb * P:(jb + 1) * P],
                                     xeh[:, k, :], xel[:, k, :], k == 0, k == KB - 1)
                    mm.then_inc(wt_done, 1)

            def out_rows(g):
                for j in range(GROUP):
                    pe.wait_ge(ul_ready, raised(ul_ready) + GROUP * g + j + 1)
                    if not isinstance(g, int) or g < GROUPS - 1:
                        pe.wait_ge(zt_ready, GROUP * (g + 1) + j + 1)
                    else:
                        pe.wait_ge(x3_ready, raised(x3_ready) + GROUP * (g - 1) + j + 1)
                    for k in range(KB):
                        mm = product(pe, banks[:, j, :], uh[:, k, j * P:(j + 1) * P], ul[:, k, j * P:(j + 1) * P],
                                     woh[:, k, :], wol[:, k, :], k == 0, k == KB - 1)
                    mm.then_inc(wo_done, 1)

            gated(pe, lambda: None, turned_and_gate, out_rows)
            after(pe, END_E)
            R0, A0, U0, B0 = 0, KB * FE, KB * FE + DIM, KB * FE + 2 * DIM

            def turn_masks(g, q):
                pe.wait_ge(r_vec, raised(r_vec) + R_STEPS * g + MASK_STEPS[q])
                for j in range(GROUP):
                    mm = pe.transpose(banks[:, q, j * P:(j + 1) * P], ex[:, q, j * P:(j + 1) * P], ident)
                mm.then_inc(mk_turned, 1)

            def base(g, c, u, between=None):
                n = CHUNKS * g + c
                pe.wait_ge(gul_ready, n + 1)
                for bank, o in ((6, 0), (7, DIM)):
                    if bank == 7 and between:
                        between()
                    if bank == 6:
                        pe.wait_ge(silu_done, raised(silu_done) + 3 * n)
                    else:
                        pe.wait_ge(mul_done, raised(mul_done) + 3 * n)
                    for k in range(KB):
                        a, b = o + k * P, o + (k + 1) * P
                        mm = product(pe, banks[:, bank, :], guh[:, u, a:b], gul[:, u, a:b],
                                     xfh[:, k, :], xfl[:, k, :], k == 0, k == KB - 1)
                    mm.then_inc(gate_ready if bank == 6 else up_ready, 1)

            def lora(g, c, u, s):
                n = CHUNKS * g + c
                pe.wait_ge(silu_done, raised(silu_done) + 3 * n + s + 1)
                product(pe, banks[:, 6, :], guh[:, u, 2 * DIM:2 * DIM + P], gul[:, u, 2 * DIM:2 * DIM + P],
                        rh[:, s, :], rl[:, s, :], False, True, check=True).then_inc(gate_ready, 1)
                pe.wait_ge(mul_done, raised(mul_done) + 3 * n + s + 1)
                product(pe, banks[:, 7, :], guh[:, u, 2 * DIM + P:], gul[:, u, 2 * DIM + P:],
                        rh[:, 2 + s, :], rl[:, 2 + s, :], False, True, check=True).then_inc(up_ready, 1)

            def down(g, c, u, part):
                n = CHUNKS * g + c
                first, last = isinstance(c, int) and c == 0, isinstance(c, int) and c == CHUNKS - 1
                if part < 2:
                    if part == 0:
                        pe.wait_ge(dnl_ready, raised(dnl_ready) + n + 1)
                        pe.wait_ge(hl_ready[0], raised(hl_ready[0]) + n + 1)
                    for j in (2 * part, 2 * part + 1):
                        product(pe, banks[:, j, :], hh[:, u, 0, j * P:(j + 1) * P], hl[:, u, 0, j * P:(j + 1) * P],
                                dnh[:, u, 0:DIM], dnl[:, u, 0:DIM], first, False, check=True)
                    return
                for s in (1, 2):
                    pe.wait_ge(hl_ready[s], raised(hl_ready[s]) + n + 1)
                    mm = product(pe, banks[:, 3 + s, :], dnh[:, u, DIM:], dnl[:, u, DIM:],
                                 hh[:, u, s, :], hl[:, u, s, :], first, last, check=True)
                mm.then_inc(down_done, 1)

            def slot(g, c, half, u):
                if isinstance(c, int) and c == 0:
                    for s in range(2):
                        pe.wait_ge(rl_ready, 2 * g + s + 1)
                        lora(g, c, u, s)
                        if s == 0:
                            for q in range(2, 4):
                                turn_masks(g, q)
                    return
                before = c - 1
                base(g, c, u)
                down(g, before, 1 - u, 0)
                lora(g, c, u, 0)
                down(g, before, 1 - u, 1)
                lora(g, c, u, 1)
                down(g, before, 1 - u, 2)

            def turn_next(g, j):
                pe.wait_ge(ln["F"]["xn"], raised(ln["F"]["xn"]) + GROUP * g + j + 1)
                if j == 0:
                    pe.wait_ge(silu_done, raised(silu_done) + 3 * CHUNKS * g)
                elif j == 1:
                    pe.wait_ge(mul_done, raised(mul_done) + 3 * CHUNKS * g)
                else:
                    pe.wait_ge(xfl_ready, GROUP * g + j - 1)
                turn(pe, 6 + j % 2, xn[:, j, :], xf_turned)

            def mid(g, more):
                chunks(slot)(pe, g)

            def joint(g, nxt):
                if g is not None:
                    down(g, CHUNKS - 1, 0, 0)
                    down(g, CHUNKS - 1, 0, 1)
                if nxt is not None:
                    turn_next(nxt, 0)
                    turn_next(nxt, 1)
                if g is not None:
                    down(g, CHUNKS - 1, 0, 2)
                if nxt is not None:
                    turn_next(nxt, 2)
                    turn_next(nxt, 3)
                    pe.wait_ge(lwl_ready, 1)
                    pe.wait_ge(xfl_ready, GROUP * nxt + GROUP)
                    for k in range(KB):
                        r = slice(R0 + k * FE, R0 + (k + 1) * FE)
                        mm = product(pe, banks[0:FE, 6, :], lwh[:, r], lwl[:, r], xfh[:, k, :], xfl[:, k, :],
                                     k == 0, k == KB - 1)
                    mm.then_inc(lgt_done, 1)
                if g is not None:
                    pe.wait_ge(zl_ready, g + 1)
                    for j in range(GROUP):
                        mm = product(pe, banks[:, j, :], zh[:, j * P:(j + 1) * P], zl[:, j * P:(j + 1) * P],
                                     lwh[:, B0:B0 + DIM], lwl[:, B0:B0 + DIM], False, True, check=True)
                        mm.then_inc(fo_done, 1)
                if nxt is None:
                    return

                def lora_a(bank, o):
                    for k in range(KB):
                        mm = product(pe, banks[:, bank, :], lwh[:, o + k * P:o + (k + 1) * P],
                                     lwl[:, o + k * P:o + (k + 1) * P], xfh[:, k, :], xfl[:, k, :], k == 0, k == KB - 1)
                    mm.then_inc(ra_done, 1)

                pe.wait_ge(lt_ready, nxt + 1)
                pe.sem_inc(passed, 1)
                for j in range(GROUP):
                    mm = pe.transpose(banks[:, 7, j * FE:(j + 1) * FE], lt[:, j * P:(j + 1) * P], ident[0:FE, 0:FE])
                mm.then_inc(lgt_done, 1)
                if g is not None:
                    pe.wait_ge(z_vec, raised(z_vec) + 2 * g + 2)
                lora_a(4, A0)
                lora_a(5, U0)

                def masks():
                    for q in range(2):
                        pe.wait_ge(xo_ready, raised(xo_ready) + GROUP * nxt)
                        turn_masks(nxt, q)
                    pe.wait_ge(r_vec, raised(r_vec) + R_STEPS * nxt + 1)

                base(nxt, 0, 0, masks)

            groups(pe, mid, joint)

        @block.vector
        def _(dve):
            dve.wait_ge(s_mh, 1)
            with dve.Fori(0, GROUPS, 1) as g:
                ln_stats(dve, "A", g, lambda j: xres[:, GROUP * g + j, :],
                         lambda j: hold(dve, x_in[j], 16 * (g + 1)), EPS)
                for j in range(GROUP):
                    dve.wait_ge(xa_turned, raised(xa_turned) + GROUP * g + j + 1 - GROUP)
                    ln_apply(dve, "A", j, xres[:, GROUP * g + j, :])
                for j in range(GROUP):
                    dve.wait_ge(xa_turned, raised(xa_turned) + GROUP * g + j + 1)
                    dve.tensor_copy(turned(qt, GROUP * g + j),
                                    banks[:, 4 + j, :].rearrange("p (k n) -> p k n", k=KB)).then_inc(qt_copied, 1)
            after(dve, END_A)
            dve.wait_ge(d_in, 16)

            def diagonal(h, n, u):
                dve.wait_ge(strip_in[u], 16 * (n + 1))
                dve.scalar_tensor_tensor(strip[:, u, 0:P], ident, dcol[:, bass.ds(h, 1)], strip[:, u, 0:P],
                                         ALU.mult, ALU.add).then_inc(strip_ready[u], 1)

            def weigh(h, n, u, more=True):
                dve.wait_ge(y_copied[u], raised(y_copied[u]) + n + 1)
                dve.wait_ge(conv_out[u], raised(conv_out[u]) + n)
                dve.tensor_tensor(view(pr, u, 0, [[HD * HD, MB], [HD, 4], [1, HD]]),
                                  view(yx, u, WRAP, [[YP_, MB], [HD + WRAP, 4], [1, HD]]),
                                  view(qx, u, 0, [[2 * HD, MB], [1, 4], [1, HD]]), ALU.mult)
                dve.tensor_tensor(view(pr, u, 4 * HD, [[HD * HD, MB], [HD, 2], [1, HD]]),
                                  view(yx, u, HD + 2 * WRAP - 1, [[YP_, MB], [HD + WRAP - 1, 2], [1, HD]]),
                                  view(qx, u, HD - 1, [[2 * HD, MB], [-1, 2], [1, HD]]), ALU.mult)\
                    .then_inc(pr_vec[u], 1)
                if more:
                    diagonal(h + 2, n + 1, u)
                dve.wait_ge(pr_vec[u], n + 1)
                dve.wait_ge(pr_pool[u], n + 1)
                dve.tensor_reduce(head_cols(qt, h), view(pr, u, 0, [[HD * HD, MB], [1, HD], [HD, HD]]),
                                  X_AXIS, ALU.add).then_inc(conv_out[u], 1)

            diagonal(0, 0, 0)
            diagonal(1, 0, 1)
            with dve.Fori(0, HEADS // 2 - 1, 1) as i:
                for u in range(2):
                    weigh(2 * i + u, i, u)
            for u in range(2):
                weigh(HEADS - 2 + u, HEADS // 2 - 1, u, more=False)
            after(dve, END_CONV)
            dve.wait_ge(wB_in, 80)

            def add_conv(g, j):
                dve.wait_ge(o_turned, raised(o_turned) + GROUP * g + j + 1)
                dve.tensor_tensor(xres[:, GROUP * g + j, :], xres[:, GROUP * g + j, :], banks[:, 6 + j % 2, :],
                                  ALU.add).then_inc(x1_ready, 1)

            def norm_x1(g):
                ln_stats(dve, "B", g, lambda j: xres[:, GROUP * g + j, :],
                         lambda j: hold(dve, x1_ready, GROUP * g + j + 1), EPS)
                for j in range(GROUP):
                    dve.wait_ge(xb_turned, raised(xb_turned) + GROUP * g + j + 1 - GROUP)
                    ln_apply(dve, "B", j, xres[:, GROUP * g + j, :])

            def low(g):
                for j in range(GROUP):
                    dve.wait_ge(xth_ready, raised(xth_ready) + GROUP * g + j + 1)
                    dve.tensor_tensor(xtl[:, j, :], banks[:, 6 + j % 2, :], f(xth[:, j, :]), ALU.subtract)\
                        .then_inc(xtl_ready, 1)

            def biases(g, j):
                dve.wait_ge(yw_done, raised(yw_done) + GROUP * g + j + 1)
                dve.tensor_tensor(turned(qt, GROUP * g + j), split(banks[:, j, :]), split(ebb[:, :]), ALU.add)
                dve.tensor_tensor(lg[:, bass.ts(GROUP * g + j, EXPERTS)], banks[:, 4 + j % 2, 0:EXPERTS],
                                  rbb[:, :], ALU.add).then_inc(yw_copied, 1)

            def norm(g):
                for j in range(GROUP):
                    add_conv(g, j)
                norm_x1(g)
                low(g)

            def mix(g, nxt):
                for j in range(2):
                    biases(g, j)
                    if nxt is not None:
                        add_conv(nxt, 2 * j)
                        add_conv(nxt, 2 * j + 1)
                if nxt is not None:
                    norm_x1(nxt)
                biases(g, 2)
                biases(g, 3)
                if nxt is not None:
                    low(nxt)

            choice(dve, norm, mix)
            n_vec = [0]

            def step(ins):
                n_vec[0] += 1
                ins.then_inc(t_vec, 1)
                dve.wait_ge(t_vec, n_vec[0])

            lg3 = lg[:, :].rearrange("p (t e) -> p t e", e=EXPERTS)

            def over_experts(ap):
                return ap.unsqueeze(2).to_broadcast([P, TILES, EXPERTS])

            dve.wait_ge(yw_copied, raised(yw_copied) + TILES)
            step(dve.tensor_reduce(lsc[:, 0:TILES], lg3, X_AXIS, ALU.max))
            step(dve.tensor_tensor(lg3, lg3, over_experts(lsc[:, 0:TILES]), ALU.subtract))
            dve.wait_ge(t_exp, 1)
            step(dve.tensor_reduce(lsc[:, TILES:], lg3, X_AXIS, ALU.add))
            step(dve.reciprocal(lsc[:, 0:TILES], lsc[:, TILES:]))
            step(dve.tensor_tensor(lg3, lg3, over_experts(lsc[:, 0:TILES]), ALU.mult))
            dve.memset(onesr[:, :], 1.0)
            dve.memset(cnt[:, :], 0.0)
            step(dve.memset(pre[:, :], 0))
            dve.wait_ge(t_pe, 1)
            step(dve.tensor_copy(st_[:, :], banks[:, 0, 0:2 * P]))
            with dve.Fori(0, STEPS, 1) as i:
                dve.wait_ge(bit_vec, raised(bit_vec) + 4 * i)
                dve.tensor_tensor(pre[:, 1:4], pre[:, 0:1].to_broadcast([P, 3]), bitc[:, bass.ds(3 * i, 3)], ALU.bitwise_or)\
                    .then_inc(bit_vec, 1)
                dve.wait_ge(bit_vec, raised(bit_vec) + 4 * i + 1)
                for c in range(3):
                    ins = dve.tensor_scalar(junk[:, c, :], st_[:, :], f(pre[:, 1 + c:2 + c]), None, ALU.is_ge, ALU.add,
                                            accum_out=cnt[:, 4 + c:5 + c])
                ins.then_inc(bit_cnt, 1)
                dve.wait_ge(bit_sum, i + 1)
                dve.tensor_scalar(met[:, 0:3], banks[:, 1, 0:3], CAPACITY - 0.5, None, ALU.is_ge, ALU.add,
                                  accum_out=over[:, :]).then_inc(bit_vec, 1)
                dve.wait_ge(bit_vec, raised(bit_vec) + 4 * i + 2)
                dve.tensor_tensor(pre[:, 4:5], over[:, :], bitc[:, bass.ds(3 * i, 1)], ALU.mult).then_inc(bit_vec, 1)
                dve.wait_ge(bit_vec, raised(bit_vec) + 4 * i + 3)
                dve.tensor_tensor(pre[:, 0:1], pre[:, 0:1], pre[:, 4:5], ALU.bitwise_or).then_inc(bit_vec, 1)
            dve.wait_ge(bit_vec, raised(bit_vec) + 4 * STEPS)
            thr = f(pre[:, 0:1])
            step(dve.tensor_scalar(junk[:, 0, :], st_[:, :], thr, None, ALU.is_gt, ALU.add, accum_out=cnt[:, 2:3]))
            step(dve.tensor_scalar(eqs[:, 0:P], st_[:, 0:P], thr, None, ALU.is_equal, ALU.add, accum_out=cnt[:, 3:4]))
            step(dve.tensor_scalar(eqs[:, P:], st_[:, P:], thr, None, ALU.is_equal, ALU.add, accum_out=cnt[:, 4:5]))
            dve.wait_ge(t_pe, 2)
            step(dve.tensor_scalar(cnt[:, 5:6], banks[:, 2, 0:1], -1.0, float(CAPACITY), ALU.mult, ALU.add))
            step(dve.tensor_copy(cnt[:, 6:7], banks[:, 3, 0:1]))
            step(dve.tensor_copy(cnt[:, 7:8], banks[:, 4, 0:1]))
            for c in range(2):
                step(dve.tensor_tensor_scan(scan[:, c * P:(c + 1) * P], onesr[:, :], eqs[:, c * P:(c + 1) * P],
                                            cnt[:, 6 + c:7 + c], ALU.mult, ALU.add))
            step(dve.scalar_tensor_tensor(scan[:, :], scan[:, :], cnt[:, 5:6], eqs[:, :], ALU.is_le, ALU.mult))
            step(dve.tensor_tensor(scan[:, :], scan[:, :], junk[:, 0, :], ALU.add))
            step(dve.tensor_tensor(st_[:, :], st_[:, :], scan[:, :], ALU.mult))
            assert n_vec[0] == T_GATED
            dve.wait_ge(t_pe, 3)
            step(dve.tensor_copy(gate[:, :], banks[:, 5, 0:TILES]))
            assert n_vec[0] == END_T[0][1]

            def norm_x2(g):
                for j in range(GROUP):
                    t = GROUP * g + j
                    dve.scalar_tensor_tensor(split(xres[:, t, :]), turned(qt, t), gate[:, bass.ds(t, 1)], split(xres[:, t, :]),
                                             ALU.mult, ALU.add).then_inc(x2_ready, 1)
                ln_stats(dve, "C", g, lambda j: xres[:, GROUP * g + j, :],
                         lambda j: hold(dve, x2_ready, GROUP * g + j + 1), EPS)
                for j in range(GROUP):
                    dve.wait_ge(xc_turned, raised(xc_turned) + GROUP * g + j + 1 - GROUP)
                    ln_apply(dve, "C", j, xres[:, GROUP * g + j, :])

            dve.wait_ge(wh_in, 16)

            def low_x(h, q):
                dve.wait_ge(xxh_ready, 4 * h + q + 1)
                dve.sem_inc(passed, 1)
                dve.tensor_tensor(xxl[:, q % 2, :], xt[:, bass.ds(h * TOKENS + q * GTOK, GTOK)],
                                  f(xxh[:, q % 2, :]), ALU.subtract).then_inc(xxl_ready, 1)

            def low_m(h, q):
                u = q % 2
                dve.wait_ge(mth_ready, 4 * h + q + 1)
                dve.tensor_tensor(mtl[:, u, :], banks[:, u, :], f(mth[:, u, :]), ALU.subtract).then_inc(mtl_ready[u], 1)

            def low_v(h, q):
                u = q % 2
                dve.wait_ge(vh_ready, 4 * h + q + 1)
                dve.tensor_tensor(vl[:, 4 * q:4 * q + 4, :], banks[:, 2 + u, :].rearrange("p (i e) -> p i e", i=4),
                                  f(vh[:, 4 * q:4 * q + 4, :]), ALU.subtract).then_inc(vl_ready[u], 1)

            def floor(h):
                dve.wait_ge(al_ready, raised(al_ready) + h)
                dve.sem_inc(passed, 1)
                for u in range(2):
                    dve.wait_ge(sc_done[u], raised(sc_done[u]) + 2 * h + 2)
                    dve.sem_inc(passed, 1)
                dve.tensor_tensor(aw[:, :].rearrange("p (t s) -> p t s", t=2), banks[:, 4:6, 0:SEQ],
                                  dmask[:, h, :].rearrange("p (t s) -> p t s", t=2), ALU.mult).then_inc(a_read, 1)
                dve.wait_ge(a_read, raised(a_read) + h + 1)
                dve.scalar_tensor_tensor(aw[:, :], aw[:, :], -1.0, aw[:, :], ALU.mult, ALU.max).then_inc(a_abs, 1)
                dve.wait_ge(a_abs, h + 1)
                dve.tensor_scalar(aw[:, :], aw[:, :], 1.0, None, ALU.max).then_inc(a_ready, 1)

            def low_a(h):
                dve.wait_ge(ah_ready, h + 1)
                dve.tensor_tensor(al[:, :], aw[:, :], f(ah[:, :]), ALU.subtract).then_inc(al_ready, 1)

            def start():
                dve.wait_ge(whh_ready, 1)
                dve.tensor_tensor(whl[:, :, :], whf[:, :, :], f(whh[:, :, :]), ALU.subtract).then_inc(whl_ready, 1)
                dve.wait_ge(wh_turned, 1)
                dve.tensor_copy(wht[:, :, :].rearrange("p h e -> p (h e)"), banks[:, 6, :]).then_inc(wht_ready, 1)
                norm_x2(0)
                low_g(0)
                norm_x2(1)
                low_m(0, 0)
                low_m(0, 1)
                with dve.Fori(2, GROUPS, 1) as g:
                    norm_x2(g)
                low_x(0, 0)
                low_x(0, 1)
                dve.wait_ge(decay_in, 16)

            def low_g(h):
                dve.wait_ge(grh_ready, h + 1)
                dve.sem_inc(passed, 1)
                dve.tensor_tensor(grl[:, :], banks[:, 7, bass.ts(h, P)], f(grh[:, :]), ALU.subtract).then_inc(grl_ready, 1)

            def first(h):
                low_g(h)
                floor(h - 1)
                low_x(h, 0)
                low_x(h, 1)
                low_a(h - 1)
                low_m(h, 0)
                low_m(h, 1)

            def second(h):
                low_v(h, 0)
                low_v(h, 1)
                low_x(h, 2)
                low_m(h, 2)
                low_x(h, 3)
                low_m(h, 3)
                low_v(h, 2)
                low_v(h, 3)

            def weigh(h):
                if isinstance(h, int):
                    floor(h)
                    low_a(h)
                for half, bank in ((0, 5), (1, 6)):
                    dve.wait_ge(ao_done, raised(ao_done) + 4 * h + 2 * half + 2)
                    dve.sem_inc(passed, 1)
                    dve.tensor_copy(batches(ret_out)[:, 4:8, half, bass.ts(h, P)],
                                    banks[:, bank, :].rearrange("p (b e) -> p b e", b=4)).then_inc(ro_vec, 1)

            heads(dve, start, first, second, weigh)
            after(dve, END_D)
            def norm(g, part):
                if part == 0:
                    ln_stats(dve, "F", g, lambda j: xres[:, GROUP * g + j, :], lambda j: None, EPS, wait=False)
                    return
                dve.wait_ge(ln["F"]["rstd"], g + 1)
                for j in range(GROUP):
                    dve.wait_ge(xf_turned, raised(xf_turned) + GROUP * g + j + 1 - GROUP)
                    ln_apply(dve, "F", j, xres[:, GROUP * g + j, :])

            def norm_e(g):
                ln_stats(dve, "E", g, lambda j: tile_rows(qt, GROUP * g + j), lambda j: None, GN_EPS)
                for j in range(GROUP):
                    dve.wait_ge(y_turned, raised(y_turned) + GROUP * g + j + 1 - GROUP)
                    ln_apply(dve, "E", j, tile_rows(qt, GROUP * g + j))

            def start():
                norm_e(0)
                dve.wait_ge(wE_high, 1)
                dve.tensor_tensor(wgl[:, :, :], wgf[:, :, :], f(wgh[:, :, :]), ALU.subtract).then_inc(wE_ready, 1)
                dve.wait_ge(wE_high, 2)
                dve.tensor_tensor(wol[:, :, :], wof[:, :, :], f(woh[:, :, :]), ALU.subtract).then_inc(wE_ready, 1)

            def low_u(g, j):
                a, b = j * P, (j + 1) * P
                dve.wait_ge(uh_ready, GROUP * g + j + 1)
                dve.tensor_tensor(ul[:, :, a:b], zt[:, :, a:b], f(uh[:, :, a:b]), ALU.subtract).then_inc(ul_ready, 1)

            def gated_features(g, more):
                if more:
                    norm_e(g + 1)
                for jb in range(KB):
                    dve.wait_ge(wt_done, raised(wt_done) + KB * g + jb + 1)
                    dve.wait_ge(zt_ready, GROUP * g + GROUP)
                    dve.scalar_tensor_tensor(zt[:, jb, :], banks[:, 4 + jb, :], 0.0, zt[:, jb, :], ALU.max, ALU.mult)\
                        .then_inc(zu_ready, 1)
                if isinstance(g, int) and g == 0:
                    for j in range(GROUP):
                        low_u(0, j)

            def out_rows(g):
                if isinstance(g, int) and g == GROUPS - 1:
                    dve.wait_ge(y_turned, raised(y_turned) + TILES)
                    norm(0, 0)
                    norm(0, 1)
                for j in range(GROUP):
                    dve.wait_ge(wo_done, raised(wo_done) + GROUP * g + j + 1)
                    dve.tensor_tensor(xres[:, GROUP * g + j, :], xres[:, GROUP * g + j, :], banks[:, j, :], ALU.add)\
                        .then_inc(x3_ready, 1)
                    if not isinstance(g, int) or g < GROUPS - 1:
                        low_u(g + 1, j)

            gated(dve, start, gated_features, out_rows)
            after(dve, END_E)
            dve.wait_ge(lwh_ready, 1)
            dve.tensor_tensor(lwl[:, :], lwf[:, :], f(lwh[:, :]), ALU.subtract).then_inc(lwl_ready, 1)

            def cut_gu(g, c, half, u, uses):
                dve.wait_ge(wst_in[u], 16 * loads(g, half, u))
                dve.wait_ge(up_ready, raised(up_ready) + uses)
                dve.tensor_copy(guh[:, u, :], wst[:, u, 0:GU_W]).then_inc(guh_ready, 1)

            def slot(g, c, half, u):
                n = CHUNKS * g + c
                first = isinstance(c, int) and c == 0
                dve.wait_ge(down_done, raised(down_done) + (n if first else n - 1))
                dve.tensor_copy(dnh[:, u, :], wst[:, u, GU_W:]).then_inc(dnh_ready, 1)
                for s in range(3):
                    dve.wait_ge(up_ready, raised(up_ready) + 3 * n + s + 1)
                    dve.wait_ge(silu_done, raised(silu_done) + 3 * n + s + 1)
                    dve.wait_ge(hl_ready[s], raised(hl_ready[s]) + n)
                    dve.tensor_tensor(hf[:, s, :], banks[:, 7, :], silu[:, s % 2, :], ALU.mult).then_inc(mul_done, 1)
                    if s == 0 and not (isinstance(c, int) and c == CHUNKS - 1):
                        cut_gu(g, c + 1, half + (1 if u == 1 else 0), 1 - u, 3 * n)

            def router(g):
                k_vec = [0]

                def link(ins):
                    k_vec[0] += 1
                    ins.then_inc(r_vec, 1)
                    dve.wait_ge(r_vec, raised(r_vec) + R_STEPS * g + k_vec[0])

                def by_e(i):
                    return rt[:, i, :].rearrange("p (t e) -> p t e", e=FE)

                def per_token(i):
                    return rsm[:, i, :].unsqueeze(2).to_broadcast([P, GROUP, FE])

                def spread_ranks(q):
                    link(dve.tensor_copy(ex[:, q, :].rearrange("p (e r) -> p e r", r=RANK),
                                         rt[:, 6 + q, :].unsqueeze(2).to_broadcast([P, GROUP * FE, RANK])))
                    assert k_vec[0] == MASK_STEPS[q]

                dve.wait_ge(lgt_done, 2 * g + 2)
                link(dve.tensor_copy(rt[:, 0, :], banks[:, 7, 0:GROUP * FE]))
                link(dve.tensor_reduce(rsm[:, 0, :], by_e(0), X_AXIS, ALU.max))
                link(dve.tensor_tensor(by_e(0), by_e(0), per_token(0), ALU.subtract))
                dve.wait_ge(r_exp, g + 1)
                link(dve.tensor_reduce(rsm[:, 1, :], by_e(0), X_AXIS, ALU.add))
                link(dve.reciprocal(rsm[:, 2, :], rsm[:, 1, :]))
                link(dve.tensor_tensor(by_e(0), by_e(0), per_token(2), ALU.mult))
                for probs, hot in ((0, 3), (4, 5)):
                    link(dve.tensor_reduce(rsm[:, 3, :], by_e(probs), X_AXIS, ALU.max))
                    link(dve.tensor_tensor(by_e(1), by_e(probs), per_token(3), ALU.is_equal))
                    link(dve.tensor_tensor(rt[:, 2, :], rt[:, 1, :], rank8, ALU.mult))
                    link(dve.tensor_reduce(rsm[:, 4, :], by_e(2), X_AXIS, ALU.max))
                    link(dve.tensor_tensor(by_e(hot), by_e(2), per_token(4), ALU.is_equal))
                    if probs == 0:
                        link(dve.scalar_tensor_tensor(rt[:, 4, :], rt[:, 3, :], -2.0, rt[:, 0, :], ALU.mult, ALU.add))
                for q, hot, other, op in ((0, 3, None, None), (1, 5, 6, ALU.subtract), (2, 3, 0, ALU.mult), (3, 5, 0, ALU.mult)):
                    if other is None:
                        link(dve.tensor_scalar(rt[:, 6 + q, :], rt[:, hot, :], SCALING, None, ALU.mult))
                    else:
                        link(dve.scalar_tensor_tensor(rt[:, 6 + q, :], rt[:, hot, :], SCALING, rt[:, other, :], ALU.mult, op))
                    if q < 2:
                        spread_ranks(q)
                for q in range(2):
                    dve.wait_ge(mk_ready, 4 * g + q + 1)
                    dve.wait_ge(ra_done, 2 * g + 2)
                    dve.tensor_tensor(rf[:, q, :], banks[:, 4, :], mk[:, q, :], ALU.mult)
                    dve.tensor_tensor(rf[:, 2 + q, :], banks[:, 5, :], mk[:, q, :], ALU.mult).then_inc(rf_ready, 1)
                for q in range(2):
                    dve.wait_ge(rh_ready, 2 * g + q + 1)
                    dve.tensor_tensor(rl[:, q:4:2, :], rf[:, q:4:2, :], f(rh[:, q:4:2, :]), ALU.subtract)\
                        .then_inc(rl_ready, 1)
                    if q == 0:
                        spread_ranks(2)
                        spread_ranks(3)
                assert k_vec[0] == R_STEPS

            def mid(g, more):
                router(g)

                def slots(g, c, half, u):
                    slot(g, c, half, u)
                    if more and isinstance(c, int) and c in (1, 2):
                        norm(g + 1, c - 1)

                chunks(slots)(dve, g)

            def joint(g, nxt):
                def low(j):
                    dve.wait_ge(xfh_ready, GROUP * nxt + j + 1)
                    dve.tensor_tensor(xfl[:, :, j * P:(j + 1) * P], split(banks[:, 6 + j % 2, :]),
                                      f(xfh[:, :, j * P:(j + 1) * P]), ALU.subtract).then_inc(xfl_ready, 1)

                if nxt is not None:
                    low(0)
                    low(1)
                if g is not None:
                    dve.wait_ge(down_done, raised(down_done) + CHUNKS * g + CHUNKS)
                    dve.wait_ge(mk_ready, 4 * g + 4)
                    for s in range(2):
                        i = dve.tensor_tensor(zf[:, s, :], banks[:, 4 + s, :], mk[:, 2 + s, :], ALU.mult)
                    i.then_inc(z_vec, 1)
                    dve.wait_ge(z_vec, raised(z_vec) + 2 * g + 1)
                    dve.tensor_tensor(zf[:, 0, :], zf[:, 0, :], zf[:, 1, :], ALU.add).then_inc(z_vec, 1)
                if nxt is not None:
                    low(2)
                    low(3)
                if g is not None:
                    dve.wait_ge(zh_ready, g + 1)
                    dve.tensor_tensor(zl[:, :], zf[:, 0, :], f(zh[:, :]), ALU.subtract).then_inc(zl_ready, 1)
                if nxt is not None:
                    dve.wait_ge(lgt_done, 2 * nxt + 1)
                    dve.tensor_copy(lt[:, :], banks[0:FE, 6, :]).then_inc(lt_ready, 1)
                if g is not None:
                    for j in range(GROUP):
                        dve.wait_ge(fo_done, GROUP * g + j + 1)
                        dve.tensor_tensor(xres[:, GROUP * g + j, :], xres[:, GROUP * g + j, :], banks[:, j, :], ALU.add)\
                            .then_inc(xo_ready, 1)
                if nxt is not None:
                    cut_gu(nxt, 0, 0, 0, 3 * CHUNKS * nxt)

            groups(dve, mid, joint)


T_GATED = 18
R_STEPS = 25
MASK_STEPS = (19, 21, 24, 25)

_OUT = (BATCH, SEQ, DIM)


def kernel(**inputs):
    import numpy as _np
    import concourse.bacc as _bacc
    from concourse import mybir as _mybir
    from concourse.bass_utils import run_bass_kernel_spmd as _run

    def blocks(w):
        return w.reshape(-1, P, w.shape[1]).transpose(1, 0, 2)

    a = {n: _np.asarray(v) for n, v in inputs.items()}
    padded = _np.concatenate([_np.zeros((HEADS, P - 1), _np.float32), a["L0_xattn_ssm_kernel"]], axis=1)
    strips = _np.stack([padded[:, P - 1 - p:P - 1 - p + DIM] for p in range(P)], axis=1)
    r = _np.arange(P)
    same = (r[:, None] % EXPERTS == r[None, :] % EXPERTS)
    earlier = same & (r[:, None] // EXPERTS < r[None, :] // EXPERTS)
    selector = r[:, None] // EXPERTS == _np.arange(8)[None, :]
    ranks = _np.tile(FE - _np.arange(FE), GROUP)[None, :].repeat(P, axis=0)
    consts = _np.concatenate([_np.eye(P), same, earlier, selector, ranks], axis=1).astype(_np.float32)
    low = 1 << _np.arange(BITS - 2, -1, -2)
    bits = _np.tile(_np.stack([low, 2 * low, 3 * low], axis=1).reshape(1, -1).astype(_np.int32), (P, 1))
    gam = 1.0 - 2.0 ** (-5.0 - _np.arange(RHEADS))
    i = _np.arange(SEQ, dtype=_np.float64)
    expo = i[None, :] - i[:, None]
    dm = _np.where(expo[None] <= 0, gam[:, None, None] ** _np.minimum(expo, 0)[None], 0.0)
    dm = dm / _np.sqrt(dm.sum(axis=-1))[:, None, :] / _np.sqrt(float(P))
    decay = dm.transpose(0, 2, 1).reshape(RHEADS, 2, P, SEQ).transpose(2, 0, 1, 3).reshape(P, RHEADS, 2 * SEQ)
    decay = decay.astype(_np.float32)
    ffg, ffu = (a[n].T.reshape(KB, P, CHUNKS, P).transpose(2, 1, 0, 3).reshape(CHUNKS, P, DIM)
                for n in ("L1_ffn_Wg", "L1_ffn_Wu"))
    bg, bu = (a[n].transpose(0, 2, 1).reshape(P, CHUNKS, P).transpose(1, 0, 2) for n in ("L1_ffn_Bg", "L1_ffn_Bu"))
    wd = a["L1_ffn_Wd"].T.reshape(CHUNKS, P, DIM)
    ad = a["L1_ffn_Ad"].reshape(FE * RANK, CHUNKS, P).transpose(1, 2, 0)
    chunk_w = _np.concatenate([ffg, ffu, bg, bu, wd, ad], axis=2)
    values = [
        ("x", a["x"]), ("ctx", a["ctx_2048"]), ("strips", strips),
        ("d_bc", _np.broadcast_to(a["L0_xattn_D"], (P, HEADS))), ("consts", consts), ("bits", bits),
        ("rw", blocks(a["L0_ffn_router_w"]).reshape(P, -1)),
        ("rb", _np.broadcast_to(a["L0_ffn_router_b"], (P, EXPERTS))),
        ("ew", blocks(a["L0_ffn_expert_w"])), ("eb", _np.broadcast_to(a["L0_ffn_expert_b"], (P, DIM))),
        ("wh", a["L1_xattn_Wh"].transpose(1, 0, 2)), ("decay", decay),
        ("wg", blocks(a["L1_xattn_wg_w"])), ("wo", blocks(a["L1_xattn_wo_w"])),
        ("gb", _np.concatenate([a["L1_xattn_gn_gamma"].reshape(KB, P).T, a["L1_xattn_gn_beta"].reshape(KB, P).T], axis=1)),
        ("wr", blocks(a["L1_ffn_Wr"].T).reshape(P, -1)),
        ("ag", blocks(a["L1_ffn_Ag"].reshape(FE * RANK, DIM).T).reshape(P, -1)),
        ("au", blocks(a["L1_ffn_Au"].reshape(FE * RANK, DIM).T).reshape(P, -1)),
        ("bd", a["L1_ffn_Bd"].transpose(0, 2, 1).reshape(FE * RANK, DIM)),
        ("chunk_w", chunk_w),
    ]
    nc = _bacc.Bacc("TRN2", target_bir_lowering=False, num_devices=1)
    arrays, args = {}, []
    for name, v in values:
        v = _np.ascontiguousarray(v)
        arrays[f"in_{name}"] = v
        args.append(nc.dram_tensor(f"in_{name}", v.shape, _mybir.dt.from_np(v.dtype), kind="ExternalInput").ap())
    args.append(nc.dram_tensor("out_0", _OUT, _mybir.dt.float32, kind="ExternalOutput").ap())
    build(nc, *args)
    res = _run(nc, [arrays], core_ids=[0])
    return res.results[0]["out_0"]
```
